# Optimizing a Trainium2 kernel written in Bass

```python
import numpy as np
import jax
import jax.numpy as jnp

def _softmax(x, axis=-1):
    return jax.nn.softmax(x, axis=axis)

def _gelu(x):
    return jax.nn.gelu(x, approximate=True)

def _silu(x):
    return jax.nn.silu(x)

def _sigmoid(x):
    return jax.nn.sigmoid(x)

def _layernorm(x, axis=-1, eps=1e-05):
    m = jnp.mean(x, axis=axis, keepdims=True)
    v = jnp.var(x, axis=axis, keepdims=True)
    return (x - m) / jnp.sqrt(v + eps)

def _scatter_add(tgt, idx, src, axis=0):
    return tgt.at[idx].add(src)

def _segment_sum(src, seg, n):
    return jax.ops.segment_sum(src, seg, n)
kernel_name = 'mk_recurrent_d4_jaxref_r8_4d6f2a'

def setup_inputs(seed: int=0):
    np.random.seed(seed)
    _w = jnp.asarray

    def _L0_attn_setup():
        import jax, jax.numpy as jnp
        import numpy as np
        B, S, D = (8, 512, 128)
        H, DK, DV, L = (8, 64, 64, 32)
        key = jax.random.key(seed)
        ks = jax.random.split(key, 6)
        x = jax.random.normal(ks[0], (B, S, D), dtype=jnp.float32)
        sd = 1.0 / np.sqrt(D)
        Wq = jax.random.normal(ks[1], (D, H * DK), dtype=jnp.float32) * sd
        Wk = jax.random.normal(ks[2], (D, H * DK), dtype=jnp.float32) * sd
        Wv = jax.random.normal(ks[3], (D, H * DV), dtype=jnp.float32) * sd
        betas = jax.random.normal(ks[4], (1, H, 1, DV), dtype=jnp.float32)
        Wo = jax.random.normal(ks[5], (H * DV, D), dtype=jnp.float32) * (1.0 / np.sqrt(H * DV))
        return {'x': x, 'Wq': Wq, 'Wk': Wk, 'Wv': Wv, 'betas': betas, 'Wo': Wo}
    _L0_attn_in = _L0_attn_setup()

    def _L0_ffn_setup():
        import jax, jax.numpy as jnp
        import numpy as np
        EPS = 1e-06
        LN_EPS = 1e-05

        def _absmean_core(W):
            gamma = jnp.mean(jnp.abs(W)) + EPS
            Ws = W / gamma
            Wq = jnp.sign(Ws) * jnp.minimum(jnp.round(jnp.abs(Ws)), 1.0)
            return (Wq, gamma)

        @jax.custom_vjp
        def absmean(W):
            return _absmean_core(W)[0]

        def _absmean_fwd(W):
            Wq, gamma = _absmean_core(W)
            return (Wq, gamma)

        def _absmean_bwd(gamma, g):
            return (g / gamma,)
        absmean.defvjp(_absmean_fwd, _absmean_bwd)

        def layernorm(x, w, b, eps=LN_EPS):
            mu = jnp.mean(x, axis=-1, keepdims=True)
            var = jnp.mean((x - mu) ** 2, axis=-1, keepdims=True)
            return (x - mu) * jax.lax.rsqrt(var + eps) * w + b
        key = jax.random.key(seed)
        k1, k2, k3 = jax.random.split(key, 3)
        d, h = (128, 512)
        B, T = (8, 256)
        return {'x': jax.random.normal(k1, (B, T, d), jnp.float32), 'W_fc': jax.random.normal(k2, (h, d), jnp.float32), 'ln_w': jnp.ones((h,), jnp.float32), 'ln_b': jnp.zeros((h,), jnp.float32), 'W_proj': jax.random.normal(k3, (d, h), jnp.float32)}
    _L0_ffn_in = _L0_ffn_setup()

    def _L1_attn_setup():
        import jax, jax.numpy as jnp
        import numpy as np
        B, T, C, H = (2, 256, 128, 16)
        HS = C // H

        def _rope_cos_sin(t, hs):
            pos = jnp.arange(t, dtype=jnp.float32)[:, None]
            i = jnp.arange(1, hs // 2 + 1, dtype=jnp.float32)[None]
            theta = 1.0 / 10000.0 ** (2.0 * (i - 1.0) / hs)
            ang = pos * theta
            return (jnp.cos(ang), jnp.sin(ang))

        def _apply_rope(u, cos, sin):
            u2 = u.reshape(*u.shape[:-1], HS // 2, 2)
            x0, x1 = (u2[..., 0], u2[..., 1])
            c = cos[None, None]
            s = sin[None, None]
            r0 = x0 * c - x1 * s
            r1 = x0 * s + x1 * c
            return jnp.stack([r0, r1], axis=-1).reshape(u.shape)
        key = jax.random.key(seed)
        ks = jax.random.split(key, 5)
        return {'x': jax.random.normal(ks[0], (B, T, C), dtype=jnp.float32), 'W_qkv': jax.random.normal(ks[1], (C, 3 * C), dtype=jnp.float32) * 0.02, 'b_qkv': jax.random.normal(ks[2], (3 * C,), dtype=jnp.float32) * 0.02, 'W_proj': jax.random.normal(ks[3], (C, C), dtype=jnp.float32) * 0.02, 'b_proj': jax.random.normal(ks[4], (C,), dtype=jnp.float32) * 0.02}
    _L1_attn_in = _L1_attn_setup()

    def _L1_ffn_setup():
        import jax, jax.numpy as jnp
        import numpy as np
        TOP_K = 2
        key = jax.random.key(seed)
        k1, k2, k3, k4, k5 = jax.random.split(key, 5)
        B, S, D, F, E = (2, 128, 128, 256, 8)
        return {'x': jax.random.normal(k1, (B, S, D), dtype=jnp.float32), 'router_kernel_DE': jax.random.normal(k2, (D, E), dtype=jnp.float32) * 0.02, 'kernel_gating_EDF': jax.random.normal(k3, (E, D, F), dtype=jnp.float32) * 0.02, 'kernel_up_EDF': jax.random.normal(k4, (E, D, F), dtype=jnp.float32) * 0.02, 'kernel_down_EFD': jax.random.normal(k5, (E, F, D), dtype=jnp.float32) * 0.02}
    _L1_ffn_in = _L1_ffn_setup()

    def _L2_attn_setup():
        import jax, jax.numpy as jnp
        import numpy as np
        D_MODEL = 128
        N_HEADS = 64
        D_HEAD = D_MODEL // N_HEADS
        B = 2
        S = 256

        def _xavier(key, fan):
            lim = np.sqrt(6.0 / (2 * fan)).astype(np.float32)
            return jax.random.uniform(key, (fan, fan), dtype=jnp.float32, minval=-lim, maxval=lim)
        key = jax.random.key(seed)
        ks = jax.random.split(key, 9)
        blim = 1.0 / np.sqrt(D_MODEL)

        def bias(k):
            return jax.random.uniform(k, (D_MODEL,), dtype=jnp.float32, minval=-blim, maxval=blim)
        return {'x': jax.random.normal(ks[0], (B, S, D_MODEL), dtype=jnp.float32), 'Wq': _xavier(ks[1], D_MODEL), 'bq': bias(ks[2]), 'Wk': _xavier(ks[3], D_MODEL), 'bk': bias(ks[4]), 'Wv': _xavier(ks[5], D_MODEL), 'bv': bias(ks[6]), 'Wo': _xavier(ks[7], D_MODEL), 'bo': jnp.zeros((D_MODEL,), dtype=jnp.float32), 'beta': jnp.zeros((1,), dtype=jnp.float32)}
    _L2_attn_in = _L2_attn_setup()

    def _L2_ffn_setup():
        import jax, jax.numpy as jnp
        import numpy as np
        key = jax.random.key(seed)
        ks = jax.random.split(key, 4)
        B, T, M, E, F = (4, 256, 128, 8, 512)
        hidden_states = jax.random.normal(ks[0], (B, T, M), dtype=jnp.float32)
        wg = jax.random.normal(ks[1], (M, E), dtype=jnp.float32) * (1.0 / np.sqrt(M))
        w1 = jax.random.normal(ks[2], (E, M, F), dtype=jnp.float32) * (1.0 / np.sqrt(M))
        b1 = jnp.zeros((E, F), dtype=jnp.float32)
        w2 = jax.random.normal(ks[3], (E, F, M), dtype=jnp.float32) * (1.0 / np.sqrt(F))
        b2 = jnp.zeros((E, M), dtype=jnp.float32)
        return {'hidden_states': hidden_states, 'wg': wg, 'w1': w1, 'b1': b1, 'w2': w2, 'b2': b2}
    _L2_ffn_in = _L2_ffn_setup()

    def _L3_attn_setup():
        import jax, jax.numpy as jnp
        import numpy as np
        B, L, D_MODEL = (2, 512, 128)
        D_INNER, D_STATE, D_CONV, DT_RANK = (256, 16, 4, 64)

        def _reference_tuple_inner(hidden_states, in_proj_w, conv_w, conv_b, x_proj_w, dt_proj_w, dt_proj_b, A_log, D, out_proj_w):
            b = hidden_states.shape[0]
            d_inner, d_conv = conv_w.shape
            d_state = A_log.shape[1]
            dt_rank = dt_proj_w.shape[1]
            proj = jnp.einsum('bld,ed->ble', hidden_states, in_proj_w).transpose(0, 2, 1)
            u, z = jnp.split(proj, 2, axis=1)
            conv_state = u[..., -d_conv:]
            x = jax.lax.conv_general_dilated(u, conv_w[:, None, :], (1,), [(d_conv - 1, 0)], dimension_numbers=('NCH', 'OIH', 'NCH'), feature_group_count=d_inner)
            x = jax.nn.silu(x + conv_b[None, :, None])
            x_dbl = jnp.einsum('bdl,ed->ble', x, x_proj_w)
            time_step = x_dbl[..., :dt_rank]
            Bmat = x_dbl[..., dt_rank:dt_rank + d_state]
            Cmat = x_dbl[..., dt_rank + d_state:]
            dt = jax.nn.softplus(jnp.einsum('blr,dr->bld', time_step, dt_proj_w) + dt_proj_b)
            delta = jax.nn.softplus(dt + dt_proj_b)
            A = -jnp.exp(A_log)
            xs = x.transpose(2, 0, 1)
            deltas = delta.transpose(1, 0, 2)
            Bs = Bmat.transpose(1, 0, 2)
            Cs = Cmat.transpose(1, 0, 2)
            init = jnp.zeros((b, d_inner, d_state), x.dtype)

            def step(state, inp):
                d_t, u_t, b_t, c_t = inp
                state = jnp.exp(d_t[..., None] * A) * state + (d_t * u_t)[..., None] * b_t[:, None, :]
                y_t = jnp.einsum('bdn,bn->bd', state, c_t)
                return (state, y_t)
            last_state, ys = jax.lax.scan(step, init, (deltas, xs, Bs, Cs))
            y = ys.transpose(1, 0, 2)
            y = y + x.transpose(0, 2, 1) * D
            y = y * jax.nn.silu(z.transpose(0, 2, 1))
            out = jnp.einsum('bld,ed->ble', y, out_proj_w)
            return (out, conv_state, last_state)
        key = jax.random.key(seed)
        ks = jax.random.split(key, 8)
        rn = lambda k, s, sc=0.02: jax.random.normal(k, s, dtype=jnp.float32) * sc
        A = jnp.broadcast_to(jnp.arange(1, D_STATE + 1, dtype=jnp.float32), (D_INNER, D_STATE))
        return {'hidden_states': jax.random.normal(ks[0], (B, L, D_MODEL), dtype=jnp.float32), 'in_proj_w': rn(ks[1], (2 * D_INNER, D_MODEL)), 'conv_w': rn(ks[2], (D_INNER, D_CONV), 0.2), 'conv_b': jnp.zeros((D_INNER,), jnp.float32), 'x_proj_w': rn(ks[3], (DT_RANK + 2 * D_STATE, D_INNER)), 'dt_proj_w': rn(ks[4], (D_INNER, DT_RANK), 0.1), 'dt_proj_b': rn(ks[5], (D_INNER,), 0.1), 'A_log': jnp.log(A), 'D': jnp.ones((D_INNER,), jnp.float32), 'out_proj_w': rn(ks[6], (D_MODEL, D_INNER))}
    _L3_attn_in = _L3_attn_setup()

    def _L3_ffn_setup():
        import jax, jax.numpy as jnp
        import numpy as np
        from math import sqrt
        B, S, D, H, E, K, FF = (2, 128, 128, 16, 8, 2, 512)
        HD = D // H
        EPS = 1e-05

        def _rope_cache(seq_len, hd):
            inv_freq = 1.0 / 10000.0 ** (jnp.arange(0, hd, 2, dtype=jnp.float32) / hd)
            t = jnp.arange(seq_len, dtype=jnp.float32)
            freqs = t[:, None] * inv_freq[None, :]
            emb = jnp.concatenate([freqs, freqs], axis=-1)
            return (jnp.cos(emb), jnp.sin(emb))

        def _rotate_half(x):
            x1, x2 = jnp.split(x, 2, axis=-1)
            return jnp.concatenate([-x2, x1], axis=-1)

        def _layernorm(x, g, b):
            m = jnp.mean(x, axis=-1, keepdims=True)
            v = jnp.var(x, axis=-1, keepdims=True)
            return (x - m) * jax.lax.rsqrt(v + EPS) * g + b

        def _forward(x, Wq, bq, Wk, bk, Wv, bv, Wo, bo, Wg, bg, W1, b1, W2, b2, g1, be1, g2, be2):
            bsz, seq, d = x.shape
            q = (x @ Wq + bq).reshape(bsz, seq, H, HD).transpose(0, 2, 1, 3)
            k = (x @ Wk + bk).reshape(bsz, seq, H, HD).transpose(0, 2, 1, 3)
            v = (x @ Wv + bv).reshape(bsz, seq, H, HD).transpose(0, 2, 1, 3)
            cos, sin = _rope_cache(seq, HD)
            cos = cos[None, None]
            sin = sin[None, None]
            q = q * cos + _rotate_half(q) * sin
            k = k * cos + _rotate_half(k) * sin
            scores = jnp.einsum('bhqd,bhkd->bhqk', q, k) / sqrt(HD)
            attn = jax.nn.softmax(scores, axis=-1)
            ao = jnp.einsum('bhqk,bhkd->bhqd', attn, v)
            ao = ao.transpose(0, 2, 1, 3).reshape(bsz, seq, d)
            attn_out = ao @ Wo + bo
            x1 = _layernorm(x + attn_out, g1, be1)
            gate_logits = x1 @ Wg + bg
            gate_probs = jax.nn.softmax(gate_logits, axis=-1)
            topk_p, topk_i = jax.lax.top_k(gate_probs, K)
            topk_p = topk_p / jnp.sum(topk_p, axis=-1, keepdims=True)
            comb = jnp.sum(jax.nn.one_hot(topk_i, E, dtype=x.dtype) * topk_p[..., None], axis=-2)
            h = jax.nn.gelu(jnp.einsum('bsd,edf->bsef', x1, W1) + b1, approximate=False)
            y = jnp.einsum('bsef,efd->bsed', h, W2) + b2
            moe_out = jnp.einsum('bse,bsed->bsd', comb, y)
            return _layernorm(x1 + moe_out, g2, be2)
        key = jax.random.key(seed)
        ks = jax.random.split(key, 20)
        std = 0.02
        p = lambda k, sh: jax.random.normal(k, sh, dtype=jnp.float32) * std
        return {'x': jax.random.normal(ks[0], (B, S, D), dtype=jnp.float32), 'Wq': p(ks[1], (D, D)), 'bq': jnp.zeros((D,), jnp.float32), 'Wk': p(ks[2], (D, D)), 'bk': jnp.zeros((D,), jnp.float32), 'Wv': p(ks[3], (D, D)), 'bv': jnp.zeros((D,), jnp.float32), 'Wo': p(ks[4], (D, D)), 'bo': jnp.zeros((D,), jnp.float32), 'Wg': p(ks[5], (D, E)), 'bg': jnp.zeros((E,), jnp.float32), 'W1': p(ks[6], (E, D, FF)), 'b1': jnp.zeros((E, FF), jnp.float32), 'W2': p(ks[7], (E, FF, D)), 'b2': jnp.zeros((E, D), jnp.float32), 'g1': jnp.ones((D,), jnp.float32), 'be1': jnp.zeros((D,), jnp.float32), 'g2': jnp.ones((D,), jnp.float32), 'be2': jnp.zeros((D,), jnp.float32)}
    _L3_ffn_in = _L3_ffn_setup()
    _d = {'L0_attn_x': _L0_attn_in['x'], 'L0_attn_Wq': _L0_attn_in['Wq'], 'L0_attn_Wk': _L0_attn_in['Wk'], 'L0_attn_Wv': _L0_attn_in['Wv'], 'L0_attn_betas': _L0_attn_in['betas'], 'L0_attn_Wo': _L0_attn_in['Wo'], 'L0_ffn_W_fc': _L0_ffn_in['W_fc'], 'L0_ffn_ln_w': _L0_ffn_in['ln_w'], 'L0_ffn_ln_b': _L0_ffn_in['ln_b'], 'L0_ffn_W_proj': _L0_ffn_in['W_proj'], 'L1_attn_W_qkv': _L1_attn_in['W_qkv'], 'L1_attn_b_qkv': _L1_attn_in['b_qkv'], 'L1_attn_W_proj': _L1_attn_in['W_proj'], 'L1_attn_b_proj': _L1_attn_in['b_proj'], 'L1_ffn_router_kernel_DE': _L1_ffn_in['router_kernel_DE'], 'L1_ffn_kernel_gating_EDF': _L1_ffn_in['kernel_gating_EDF'], 'L1_ffn_kernel_up_EDF': _L1_ffn_in['kernel_up_EDF'], 'L1_ffn_kernel_down_EFD': _L1_ffn_in['kernel_down_EFD'], 'L2_attn_Wq': _L2_attn_in['Wq'], 'L2_attn_bq': _L2_attn_in['bq'], 'L2_attn_Wk': _L2_attn_in['Wk'], 'L2_attn_bk': _L2_attn_in['bk'], 'L2_attn_Wv': _L2_attn_in['Wv'], 'L2_attn_bv': _L2_attn_in['bv'], 'L2_attn_Wo': _L2_attn_in['Wo'], 'L2_attn_bo': _L2_attn_in['bo'], 'L2_attn_beta': _L2_attn_in['beta'], 'L2_ffn_wg': _L2_ffn_in['wg'], 'L2_ffn_w1': _L2_ffn_in['w1'], 'L2_ffn_b1': _L2_ffn_in['b1'], 'L2_ffn_w2': _L2_ffn_in['w2'], 'L2_ffn_b2': _L2_ffn_in['b2'], 'L3_attn_in_proj_w': _L3_attn_in['in_proj_w'], 'L3_attn_conv_w': _L3_attn_in['conv_w'], 'L3_attn_conv_b': _L3_attn_in['conv_b'], 'L3_attn_x_proj_w': _L3_attn_in['x_proj_w'], 'L3_attn_dt_proj_w': _L3_attn_in['dt_proj_w'], 'L3_attn_dt_proj_b': _L3_attn_in['dt_proj_b'], 'L3_attn_A_log': _L3_attn_in['A_log'], 'L3_attn_D': _L3_attn_in['D'], 'L3_attn_out_proj_w': _L3_attn_in['out_proj_w'], 'L3_ffn_Wq': _L3_ffn_in['Wq'], 'L3_ffn_bq': _L3_ffn_in['bq'], 'L3_ffn_Wk': _L3_ffn_in['Wk'], 'L3_ffn_bk': _L3_ffn_in['bk'], 'L3_ffn_Wv': _L3_ffn_in['Wv'], 'L3_ffn_bv': _L3_ffn_in['bv'], 'L3_ffn_Wo': _L3_ffn_in['Wo'], 'L3_ffn_bo': _L3_ffn_in['bo'], 'L3_ffn_Wg': _L3_ffn_in['Wg'], 'L3_ffn_bg': _L3_ffn_in['bg'], 'L3_ffn_W1': _L3_ffn_in['W1'], 'L3_ffn_b1': _L3_ffn_in['b1'], 'L3_ffn_W2': _L3_ffn_in['W2'], 'L3_ffn_b2': _L3_ffn_in['b2'], 'L3_ffn_g1': _L3_ffn_in['g1'], 'L3_ffn_be1': _L3_ffn_in['be1'], 'L3_ffn_g2': _L3_ffn_in['g2'], 'L3_ffn_be2': _L3_ffn_in['be2']}
    _x0 = _d['L0_attn_x']
    _d['L0_attn_x'] = jax.random.normal(jax.random.fold_in(jax.random.key(seed), 1), (16, 256, 128), dtype=_x0.dtype)
    del _x0
    return _d

def reference(L0_attn_x, L0_attn_Wq, L0_attn_Wk, L0_attn_Wv, L0_attn_betas, L0_attn_Wo, L0_ffn_W_fc, L0_ffn_ln_w, L0_ffn_ln_b, L0_ffn_W_proj, L1_attn_W_qkv, L1_attn_b_qkv, L1_attn_W_proj, L1_attn_b_proj, L1_ffn_router_kernel_DE, L1_ffn_kernel_gating_EDF, L1_ffn_kernel_up_EDF, L1_ffn_kernel_down_EFD, L2_attn_Wq, L2_attn_bq, L2_attn_Wk, L2_attn_bk, L2_attn_Wv, L2_attn_bv, L2_attn_Wo, L2_attn_bo, L2_attn_beta, L2_ffn_wg, L2_ffn_w1, L2_ffn_b1, L2_ffn_w2, L2_ffn_b2, L3_attn_in_proj_w, L3_attn_conv_w, L3_attn_conv_b, L3_attn_x_proj_w, L3_attn_dt_proj_w, L3_attn_dt_proj_b, L3_attn_A_log, L3_attn_D, L3_attn_out_proj_w, L3_ffn_Wq, L3_ffn_bq, L3_ffn_Wk, L3_ffn_bk, L3_ffn_Wv, L3_ffn_bv, L3_ffn_Wo, L3_ffn_bo, L3_ffn_Wg, L3_ffn_bg, L3_ffn_W1, L3_ffn_b1, L3_ffn_W2, L3_ffn_b2, L3_ffn_g1, L3_ffn_be1, L3_ffn_g2, L3_ffn_be2):

    def _L0_attn_ref(x, Wq, Wk, Wv, betas, Wo):
        import jax, jax.numpy as jnp
        import numpy as np
        B, S, D = (8, 512, 128)
        H, DK, DV, L = (8, 64, 64, 32)
        b, s, d = x.shape
        n_seq = s // L
        xs = x.reshape(b, n_seq, L, d)

        def proj(W, dh):
            p = xs @ W
            return p.reshape(b, n_seq, L, H, dh).transpose(1, 0, 3, 2, 4)
        q = proj(Wq, DK)
        k = proj(Wk, DK)
        v = proj(Wv, DV)
        scale = 1.0 / np.sqrt(DK)
        gate = jax.nn.sigmoid(betas)
        mem0 = jnp.zeros((b, H, DK, DV), dtype=x.dtype)
        z0 = jnp.ones((b, H, DK, 1), dtype=x.dtype) / DK

        def step(carry, inp):
            mem, z = carry
            q_s, k_s, v_s = inp
            sq = jax.nn.elu(q_s) + 1.0
            att_mem = sq @ mem / (sq @ z)
            sk = jax.nn.elu(k_s) + 1.0
            mem = mem + jnp.einsum('bhlk,bhlv->bhkv', sk, v_s)
            z = z + sk.sum(axis=-2, keepdims=True).transpose(0, 1, 3, 2)
            att_dot = jax.nn.softmax(jnp.einsum('bhik,bhjk->bhij', q_s, k_s) * scale, axis=-1)
            att = att_dot @ v_s
            att = gate * att_mem + (1.0 - gate) * att
            return ((mem, z), att)
        _, outs = jax.lax.scan(step, (mem0, z0), (q, k, v))
        out = outs.transpose(1, 0, 3, 2, 4).reshape(b, s, H * DV)
        return out @ Wo

    def _L0_ffn_ref(x, W_fc, ln_w, ln_b, W_proj):
        import jax, jax.numpy as jnp
        import numpy as np
        EPS = 1e-06
        LN_EPS = 1e-05

        def _absmean_core(W):
            gamma = jnp.mean(jnp.abs(W)) + EPS
            Ws = W / gamma
            Wq = jnp.sign(Ws) * jnp.minimum(jnp.round(jnp.abs(Ws)), 1.0)
            return (Wq, gamma)

        @jax.custom_vjp
        def absmean(W):
            return _absmean_core(W)[0]

        def _absmean_fwd(W):
            Wq, gamma = _absmean_core(W)
            return (Wq, gamma)

        def _absmean_bwd(gamma, g):
            return (g / gamma,)
        absmean.defvjp(_absmean_fwd, _absmean_bwd)

        def layernorm(x, w, b, eps=LN_EPS):
            mu = jnp.mean(x, axis=-1, keepdims=True)
            var = jnp.mean((x - mu) ** 2, axis=-1, keepdims=True)
            return (x - mu) * jax.lax.rsqrt(var + eps) * w + b
        h = jnp.einsum('btd,hd->bth', x, absmean(W_fc))
        h = jax.nn.gelu(h, approximate=False)
        h = layernorm(h, ln_w, ln_b)
        return jnp.einsum('bth,dh->btd', h, absmean(W_proj))

    def _L1_attn_ref(x, W_qkv, b_qkv, W_proj, b_proj):
        import jax, jax.numpy as jnp
        import numpy as np
        B, T, C, H = (2, 256, 128, 16)
        HS = C // H

        def _rope_cos_sin(t, hs):
            pos = jnp.arange(t, dtype=jnp.float32)[:, None]
            i = jnp.arange(1, hs // 2 + 1, dtype=jnp.float32)[None]
            theta = 1.0 / 10000.0 ** (2.0 * (i - 1.0) / hs)
            ang = pos * theta
            return (jnp.cos(ang), jnp.sin(ang))

        def _apply_rope(u, cos, sin):
            u2 = u.reshape(*u.shape[:-1], HS // 2, 2)
            x0, x1 = (u2[..., 0], u2[..., 1])
            c = cos[None, None]
            s = sin[None, None]
            r0 = x0 * c - x1 * s
            r1 = x0 * s + x1 * c
            return jnp.stack([r0, r1], axis=-1).reshape(u.shape)
        b, t, c = x.shape
        qkv = x @ W_qkv + b_qkv
        qkv = qkv.reshape(b, t, H, 3 * HS).transpose(0, 2, 1, 3)
        q, k, v = jnp.split(qkv, 3, axis=-1)
        cos, sin = _rope_cos_sin(t, HS)
        q = _apply_rope(q, cos, sin)
        k = _apply_rope(k, cos, sin)
        att = jnp.einsum('bhqd,bhkd->bhqk', q, k) / jnp.sqrt(jnp.float32(HS))
        causal = jnp.tril(jnp.ones((t, t), dtype=bool))[None, None]
        att = jnp.where(causal, att, jnp.float32(-1000000000.0))
        att = jax.nn.softmax(att, axis=-1)
        y = jnp.einsum('bhqk,bhkd->bhqd', att, v)
        y = y.transpose(0, 2, 1, 3).reshape(b, t, c)
        return y @ W_proj + b_proj

    def _L1_ffn_ref(x, router_kernel_DE, kernel_gating_EDF, kernel_up_EDF, kernel_down_EFD):
        import jax, jax.numpy as jnp
        import numpy as np
        TOP_K = 2
        E = router_kernel_DE.shape[-1]
        x = x.astype(jnp.float32)
        logits_BSE = jnp.einsum('BSD,DE->BSE', x, router_kernel_DE)
        probs_BSE = jax.nn.softmax(logits_BSE.astype(jnp.float32), axis=-1)
        weights_BSK, indices_BSK = jax.lax.top_k(probs_BSE, TOP_K)
        norm_weights_BSK = jax.nn.softmax(weights_BSK, axis=-1)
        one_hot_BSKE = jax.nn.one_hot(indices_BSK, num_classes=E, dtype=x.dtype)
        full_weights_BSE = jnp.sum(one_hot_BSKE * norm_weights_BSK[..., None], axis=2)
        gating_BSEF = jnp.einsum('BSD,EDF->BSEF', x, kernel_gating_EDF)
        act_BSEF = jax.nn.silu(gating_BSEF)
        up_BSEF = jnp.einsum('BSD,EDF->BSEF', x, kernel_up_EDF)
        fuse_BSEF = act_BSEF * up_BSEF
        down_BSED = jnp.einsum('BSEF,EFD->BSED', fuse_BSEF, kernel_down_EFD)
        out_BSD = jnp.einsum('BSED,BSE->BSD', down_BSED, full_weights_BSE)
        return out_BSD.astype(jnp.float32)

    def _L2_attn_ref(x, Wq, bq, Wk, bk, Wv, bv, Wo, bo, beta):
        import jax, jax.numpy as jnp
        import numpy as np
        D_MODEL = 128
        N_HEADS = 64
        D_HEAD = D_MODEL // N_HEADS
        B = 2
        S = 256

        def _xavier(key, fan):
            lim = np.sqrt(6.0 / (2 * fan)).astype(np.float32)
            return jax.random.uniform(key, (fan, fan), dtype=jnp.float32, minval=-lim, maxval=lim)
        b, s, dm = x.shape
        h, d = (N_HEADS, D_HEAD)

        def heads(y):
            return y.reshape(b, s, h, d).transpose(0, 2, 1, 3).reshape(b * h, s, d)
        q = heads(x @ Wq.T + bq)
        k = heads(x @ Wk.T + bk)
        v = heads(x @ Wv.T + bv)
        be = jnp.exp(beta)
        q = jax.nn.softmax(be * q, axis=-1)
        k = jax.nn.softmax(be * k, axis=-1)
        kv = jnp.cumsum(jnp.einsum('zsD,zsd->zsDd', k, v), axis=1)
        kn = jnp.cumsum(k, axis=1)
        num = jnp.einsum('zsD,zsDd->zsd', q, kv)
        den = jnp.sum(q * kn, axis=-1, keepdims=True)
        out = num / den
        out = out.reshape(b, h, s, d).transpose(0, 2, 1, 3).reshape(b, s, dm)
        return out @ Wo.T + bo

    def _L2_ffn_ref(hidden_states, wg, w1, b1, w2, b2):
        import jax, jax.numpy as jnp
        import numpy as np
        B, T, M = hidden_states.shape
        E = wg.shape[1]
        S = B * T
        MIN_CAPACITY = 4
        C = max((S + E - 1) // E, MIN_CAPACITY)
        x = hidden_states.reshape(S, M)
        logits = x @ wg
        gates = jax.nn.softmax(logits, axis=-1)
        idx = jnp.argmax(gates, axis=-1)
        mask1 = jax.nn.one_hot(idx, E, dtype=gates.dtype)
        l_aux = jnp.sum(gates.mean(0) * mask1.mean(0)) * E
        locations1 = jnp.cumsum(mask1, axis=0) - 1.0
        mask1 = mask1 * (locations1 < C)
        gates1_s = jnp.sum(gates * mask1, axis=1)
        loc_s = jnp.sum(locations1 * mask1, axis=1).astype(jnp.int32)
        loc_sc = jax.nn.one_hot(loc_s, C, dtype=gates.dtype)
        combine_weights = jnp.einsum('se,sc->sec', gates1_s[:, None] * mask1, loc_sc)
        dispatch_mask = (combine_weights > 0).astype(x.dtype)
        dispatched = jnp.einsum('sec,sm->ecm', dispatch_mask, x)
        h = jax.nn.gelu(jnp.einsum('ecm,emf->ecf', dispatched, w1) + b1[:, None, :])
        expert_out = jnp.einsum('ecf,efm->ecm', h, w2) + b2[:, None, :]
        out = jnp.einsum('sec,ecm->sm', combine_weights, expert_out)
        return out.reshape(B, T, M)

    def _L3_attn_ref(hidden_states, in_proj_w, conv_w, conv_b, x_proj_w, dt_proj_w, dt_proj_b, A_log, D, out_proj_w):
        import jax, jax.numpy as jnp
        import numpy as np
        B, L, D_MODEL = (2, 512, 128)
        D_INNER, D_STATE, D_CONV, DT_RANK = (256, 16, 4, 64)

        def _reference_tuple_inner(hidden_states, in_proj_w, conv_w, conv_b, x_proj_w, dt_proj_w, dt_proj_b, A_log, D, out_proj_w):
            b = hidden_states.shape[0]
            d_inner, d_conv = conv_w.shape
            d_state = A_log.shape[1]
            dt_rank = dt_proj_w.shape[1]
            proj = jnp.einsum('bld,ed->ble', hidden_states, in_proj_w).transpose(0, 2, 1)
            u, z = jnp.split(proj, 2, axis=1)
            conv_state = u[..., -d_conv:]
            x = jax.lax.conv_general_dilated(u, conv_w[:, None, :], (1,), [(d_conv - 1, 0)], dimension_numbers=('NCH', 'OIH', 'NCH'), feature_group_count=d_inner)
            x = jax.nn.silu(x + conv_b[None, :, None])
            x_dbl = jnp.einsum('bdl,ed->ble', x, x_proj_w)
            time_step = x_dbl[..., :dt_rank]
            Bmat = x_dbl[..., dt_rank:dt_rank + d_state]
            Cmat = x_dbl[..., dt_rank + d_state:]
            dt = jax.nn.softplus(jnp.einsum('blr,dr->bld', time_step, dt_proj_w) + dt_proj_b)
            delta = jax.nn.softplus(dt + dt_proj_b)
            A = -jnp.exp(A_log)
            xs = x.transpose(2, 0, 1)
            deltas = delta.transpose(1, 0, 2)
            Bs = Bmat.transpose(1, 0, 2)
            Cs = Cmat.transpose(1, 0, 2)
            init = jnp.zeros((b, d_inner, d_state), x.dtype)

            def step(state, inp):
                d_t, u_t, b_t, c_t = inp
                state = jnp.exp(d_t[..., None] * A) * state + (d_t * u_t)[..., None] * b_t[:, None, :]
                y_t = jnp.einsum('bdn,bn->bd', state, c_t)
                return (state, y_t)
            last_state, ys = jax.lax.scan(step, init, (deltas, xs, Bs, Cs))
            y = ys.transpose(1, 0, 2)
            y = y + x.transpose(0, 2, 1) * D
            y = y * jax.nn.silu(z.transpose(0, 2, 1))
            out = jnp.einsum('bld,ed->ble', y, out_proj_w)
            return (out, conv_state, last_state)
        return _reference_tuple_inner(hidden_states, in_proj_w, conv_w, conv_b, x_proj_w, dt_proj_w, dt_proj_b, A_log, D, out_proj_w)[0]

    def _L3_ffn_ref(x, Wq, bq, Wk, bk, Wv, bv, Wo, bo, Wg, bg, W1, b1, W2, b2, g1, be1, g2, be2):
        import jax, jax.numpy as jnp
        import numpy as np
        from math import sqrt
        B, S, D, H, E, K, FF = (2, 128, 128, 16, 8, 2, 512)
        HD = D // H
        EPS = 1e-05

        def _rope_cache(seq_len, hd):
            inv_freq = 1.0 / 10000.0 ** (jnp.arange(0, hd, 2, dtype=jnp.float32) / hd)
            t = jnp.arange(seq_len, dtype=jnp.float32)
            freqs = t[:, None] * inv_freq[None, :]
            emb = jnp.concatenate([freqs, freqs], axis=-1)
            return (jnp.cos(emb), jnp.sin(emb))

        def _rotate_half(x):
            x1, x2 = jnp.split(x, 2, axis=-1)
            return jnp.concatenate([-x2, x1], axis=-1)

        def _layernorm(x, g, b):
            m = jnp.mean(x, axis=-1, keepdims=True)
            v = jnp.var(x, axis=-1, keepdims=True)
            return (x - m) * jax.lax.rsqrt(v + EPS) * g + b

        def _forward(x, Wq, bq, Wk, bk, Wv, bv, Wo, bo, Wg, bg, W1, b1, W2, b2, g1, be1, g2, be2):
            bsz, seq, d = x.shape
            q = (x @ Wq + bq).reshape(bsz, seq, H, HD).transpose(0, 2, 1, 3)
            k = (x @ Wk + bk).reshape(bsz, seq, H, HD).transpose(0, 2, 1, 3)
            v = (x @ Wv + bv).reshape(bsz, seq, H, HD).transpose(0, 2, 1, 3)
            cos, sin = _rope_cache(seq, HD)
            cos = cos[None, None]
            sin = sin[None, None]
            q = q * cos + _rotate_half(q) * sin
            k = k * cos + _rotate_half(k) * sin
            scores = jnp.einsum('bhqd,bhkd->bhqk', q, k) / sqrt(HD)
            attn = jax.nn.softmax(scores, axis=-1)
            ao = jnp.einsum('bhqk,bhkd->bhqd', attn, v)
            ao = ao.transpose(0, 2, 1, 3).reshape(bsz, seq, d)
            attn_out = ao @ Wo + bo
            x1 = _layernorm(x + attn_out, g1, be1)
            gate_logits = x1 @ Wg + bg
            gate_probs = jax.nn.softmax(gate_logits, axis=-1)
            topk_p, topk_i = jax.lax.top_k(gate_probs, K)
            topk_p = topk_p / jnp.sum(topk_p, axis=-1, keepdims=True)
            comb = jnp.sum(jax.nn.one_hot(topk_i, E, dtype=x.dtype) * topk_p[..., None], axis=-2)
            h = jax.nn.gelu(jnp.einsum('bsd,edf->bsef', x1, W1) + b1, approximate=False)
            y = jnp.einsum('bsef,efd->bsed', h, W2) + b2
            moe_out = jnp.einsum('bse,bsed->bsd', comb, y)
            return _layernorm(x1 + moe_out, g2, be2)
        return _forward(x, Wq, bq, Wk, bk, Wv, bv, Wo, bo, Wg, bg, W1, b1, W2, b2, g1, be1, g2, be2)
    x = L0_attn_x
    xn = _layernorm(x, axis=-1)
    s = _L0_attn_ref(xn, L0_attn_Wq, L0_attn_Wk, L0_attn_Wv, L0_attn_betas, L0_attn_Wo)
    g = _silu(_L0_ffn_ref(xn, L0_ffn_W_fc, L0_ffn_ln_w, L0_ffn_ln_b, L0_ffn_W_proj))
    x = x + s * g
    xn = _layernorm(x, axis=-1)
    s = _L1_attn_ref(xn, L1_attn_W_qkv, L1_attn_b_qkv, L1_attn_W_proj, L1_attn_b_proj)
    g = _silu(_L1_ffn_ref(xn, L1_ffn_router_kernel_DE, L1_ffn_kernel_gating_EDF, L1_ffn_kernel_up_EDF, L1_ffn_kernel_down_EFD))
    x = x + s * g
    xn = _layernorm(x, axis=-1)
    s = _L2_attn_ref(xn, L2_attn_Wq, L2_attn_bq, L2_attn_Wk, L2_attn_bk, L2_attn_Wv, L2_attn_bv, L2_attn_Wo, L2_attn_bo, L2_attn_beta)
    g = _silu(_L2_ffn_ref(xn, L2_ffn_wg, L2_ffn_w1, L2_ffn_b1, L2_ffn_w2, L2_ffn_b2))
    x = x + s * g
    xn = _layernorm(x, axis=-1)
    s = _L3_attn_ref(xn, L3_attn_in_proj_w, L3_attn_conv_w, L3_attn_conv_b, L3_attn_x_proj_w, L3_attn_dt_proj_w, L3_attn_dt_proj_b, L3_attn_A_log, L3_attn_D, L3_attn_out_proj_w)
    g = _silu(_L3_ffn_ref(xn, L3_ffn_Wq, L3_ffn_bq, L3_ffn_Wk, L3_ffn_bk, L3_ffn_Wv, L3_ffn_bv, L3_ffn_Wo, L3_ffn_bo, L3_ffn_Wg, L3_ffn_bg, L3_ffn_W1, L3_ffn_b1, L3_ffn_W2, L3_ffn_b2, L3_ffn_g1, L3_ffn_be1, L3_ffn_g2, L3_ffn_be2))
    x = x + s * g
    return x

_drawn_inputs = setup_inputs


def setup_inputs(seed=0):
    import zlib

    import numpy as np

    out = dict(_drawn_inputs(seed))
    spreads = {'L0_ffn_ln_w': (1.0, 0.2),
     'L0_ffn_ln_b': (0.0, 0.1),
     'L2_attn_bo': (0.0, 0.1),
     'L2_ffn_b1': (0.0, 0.1),
     'L2_ffn_b2': (0.0, 0.1),
     'L3_attn_conv_b': (0.0, 0.1),
     'L3_attn_D': (1.0, 0.2),
     'L3_ffn_bq': (0.0, 0.1),
     'L3_ffn_bk': (0.0, 0.1),
     'L3_ffn_bv': (0.0, 0.1),
     'L3_ffn_bo': (0.0, 0.1),
     'L3_ffn_bg': (0.0, 0.1),
     'L3_ffn_b1': (0.0, 0.1),
     'L3_ffn_b2': (0.0, 0.1),
     'L3_ffn_g1': (1.0, 0.2),
     'L3_ffn_be1': (0.0, 0.1),
     'L3_ffn_g2': (1.0, 0.2),
     'L3_ffn_be2': (0.0, 0.1)}
    factors = {}
    for name, (base, spread) in spreads.items():
        noise = np.random.default_rng([zlib.crc32(name.encode()), seed]).standard_normal(out[name].shape)
        drawn = base * np.exp(spread * noise) if base else spread * noise
        out[name] = jnp.asarray(drawn.astype(out[name].dtype))
    for name, factor in factors.items():
        out[name] = (out[name] * factor).astype(out[name].dtype)
    return out
```

```python
from contextlib import ExitStack

import concourse.bass as bass
from concourse import mybir

ALU = mybir.AluOpType
ACT = mybir.ActivationFunctionType
AX = mybir.AxisListType.X
F32 = mybir.dt.float32

P = 128
NSEQ, T, D = 16, 256, 128
TILES = T // P
LN_EPS = 1e-5
LAYERS = 4

H0, DK0, SEG = 8, 64, 32
F0 = 512
NCH0 = H0 * DK0 // P
HALF0 = H0 // 2

H1, HD1 = 16, 8
E1, F1 = 8, 256
ROWS = 32
GR = ROWS // HD1


def bcast(ap, n):
    return ap.unsqueeze(2).to_broadcast([ap.shape[0], ap.shape[1], n])


class Core:
    pass


def layer_norm_buffers(nc, ctx, c):
    c.stats = ctx.enter_context(nc.sbuf_tensor("ln_stats", [P, TILES, 6], F32))
    c.meanvar = ctx.enter_context(nc.sbuf_tensor("ln_meanvar", [P, TILES, 2], F32))
    c.var_eps = ctx.enter_context(nc.sbuf_tensor("ln_var_eps", [P, TILES], F32))
    c.rstd = ctx.enter_context(nc.sbuf_tensor("ln_rstd", [P, TILES], F32))
    c.minus_half = ctx.enter_context(nc.sbuf_tensor("minus_half", [P, 8], F32))
    c.xn = ctx.enter_context(nc.sbuf_tensor("xn", [P, TILES, D], F32))
    c.xnT = ctx.enter_context(nc.sbuf_tensor("xnT", [P, T], F32))


def layer_semaphore(nc, name):
    return nc.alloc_semaphore(name=name)


def run_layer(nc, c, layer):
    before = nc.snapshot_sems()
    layer(nc, c)
    nc.clear_and_free_semaphores(nc.allocated_since(before))
    nc.all_engine_barrier()


class NormSems:

    def __init__(self, sem, name):
        self.var_ready = sem(name + "_var_ready")
        self.rstd_ready = sem(name + "_rstd_ready")
        self.xn_ready = sem(name + "_xn_ready")
        self.xnT_in_psum = sem(name + "_xnT_in_psum")


def norm_stats(nc, c, s, m):
    for a in range(TILES):
        nc.vector.bn_stats(c.stats[:, a, :], c.x[:, 2 * m + a, :])
    nc.vector.drain()
    for a in range(TILES):
        nc.vector.bn_aggr(c.meanvar[:, a, :], c.stats[:, a, :])
    nc.vector.drain()
    nc.vector.tensor_scalar(c.var_eps[:, :], c.meanvar[:, :, 1], LN_EPS, None, ALU.add).then_inc(s.var_ready, 1)


def norm_power(nc, c, s, m):
    nc.gpsimd.wait_ge(s.var_ready, m + 1)
    nc.gpsimd.tensor_tensor(c.rstd[:, :], c.var_eps[:, :], c.minus_half[:, 0:TILES], ALU.pow).then_inc(s.rstd_ready, 1)


def norm_apply(nc, c, s, m, first):
    nc.vector.wait_ge(s.rstd_ready, m + 1)
    if not first:
        nc.vector.wait_ge(s.xnT_in_psum, m)
    for a in range(TILES):
        done = nc.vector.tensor_scalar(c.xn[:, a, :], c.x[:, 2 * m + a, :], c.meanvar[:, a, 0:1],
                                       c.rstd[:, a:a + 1], ALU.subtract, ALU.mult)
    done.then_inc(s.xn_ready, 1)


def norm_transpose(nc, c, s, m, bank):
    nc.tensor.wait_ge(s.xn_ready, m + 1)
    for a in range(TILES):
        done = nc.tensor.transpose(bank[:, a * P:(a + 1) * P], c.xn[:, a, :], c.ident[:, :])
    done.then_inc(s.xnT_in_psum, 1)


def norm_copy(nc, c, s, m, bank, bank_read):
    nc.scalar.wait_ge(s.xnT_in_psum, m + 1)
    nc.scalar.activation(c.xnT[:, :], bank[:, 0:T], ACT.Copy).then_inc(bank_read, 1)


H2 = 64
E2, F2 = 8, 512
CAP2 = NSEQ * T // E2


H3, HD3 = 16, 8
E3, F3 = 8, 512
DI, NS, DCONV, RANK = 256, 16, 4, 64
CI = DI // P
SG = 4


class RouteBuffers:

    def __init__(self, sb, sem):
        self.logits = sb("r_logits", [P, TILES, 8])
        self.most = sb("r_most", [P, TILES])
        self.total = sb("r_total", [P, TILES])
        self.recip = sb("r_recip", [P, TILES])
        self.probs = sb("r_probs", [P, TILES, 8])
        self.best = sb("r_best", [P, TILES, 8])
        self.index = sb("r_index", [P, TILES, 8], mybir.dt.uint32)
        self.place = sb("r_place", [P, TILES, 8])
        self.shifted = sem("r_shifted")
        self.exped = sem("r_exped")


def route_shift(nc, r, bank_cols, bank_read, bias=None):
    v = nc.vector
    if bias is None:
        v.tensor_copy(r.logits[:, :, :], bank_cols).then_inc(bank_read, 1)
    else:
        v.tensor_tensor(r.logits[:, :, :], bank_cols, bias, ALU.add).then_inc(bank_read, 1)
    v.drain()
    v.tensor_reduce(r.most[:, :], r.logits[:, :, :], AX, ALU.max)
    v.drain()
    v.tensor_tensor(r.logits[:, :, :], r.logits[:, :, :], bcast(r.most[:, :], 8), ALU.subtract)\
        .then_inc(r.shifted, 1)


def route_exp(nc, r, n):
    nc.scalar.wait_ge(r.shifted, n + 1)
    nc.scalar.activation(r.logits[:, :, :], r.logits[:, :, :], ACT.Exp).then_inc(r.exped, 1)


def route_best(nc, r, n):
    v = nc.vector
    v.wait_ge(r.exped, n + 1)
    v.tensor_reduce(r.total[:, :], r.logits[:, :, :], AX, ALU.add)
    v.drain()
    v.reciprocal(r.recip[:, :], r.total[:, :])
    v.drain()
    v.tensor_tensor(r.probs[:, :, :], r.logits[:, :, :], bcast(r.recip[:, :], 8), ALU.mult)
    v.drain()
    for a in range(TILES):
        v.max(r.best[:, a, :], r.probs[:, a, :])
    v.drain()
    for a in range(TILES):
        v.max_index(r.index[:, a, :], r.best[:, a, :], r.probs[:, a, :])
    v.drain()
    v.tensor_copy(r.place[:, :, :], r.index[:, :, :])


def close_layer(nc, c, n, s_rows, z_rows, half_tanh, u, done_sem=None):
    v = nc.vector
    v.scalar_tensor_tensor(out=u, in0=half_tanh, scalar=1.0, in1=z_rows, op0=ALU.add, op1=ALU.mult)
    v.drain()
    v.scalar_tensor_tensor(out=u, in0=u, scalar=0.5, in1=s_rows, op0=ALU.mult, op1=ALU.mult)
    v.drain()
    for a in range(TILES):
        v.tensor_tensor(c.x[:, 2 * n + a, :], c.x[:, 2 * n + a, :], u[:, a, :], ALU.add)


def setup(nc, ctx, ctx01, A, c):
    def sb_all(name, shape):
        return ctx.enter_context(nc.sbuf_tensor(name, shape, F32))

    def sb(name, shape):
        return ctx01.enter_context(nc.sbuf_tensor(name, shape, F32))

    layer_norm_buffers(nc, ctx, c)
    c.x = sb_all("x", [P, TILES * (NSEQ + 1), D])
    c.ident = sb_all("ident", [P, P])
    c.iota8 = sb_all("iota8", [P, 8])
    c.row_mask = sb_all("row_mask", [P, GR])
    c.cos1, c.sin1 = (sb_all(name, [P, TILES, 2 * H1 * HD1 // 2]) for name in ("cos1", "sin1"))
    c.ones = sb_all("ones_pt", [P, T])
    c.w2 = {}
    for name in ("Wq", "Wk", "Wv", "Wo"):
        c.w2[name] = sb_all("l2_" + name, [P, D])
    for name in ("bq", "bk", "bv", "bo"):
        c.w2[name] = sb_all("l2_" + name, [P, D])
    c.beta = sb_all("beta", [P, 1])
    c.same_head = sb_all("same_head", [P, 3, P])
    c.until = sb_all("until", [P, P])
    c.wg2 = sb_all("wg2", [P, E2])
    c.w12, c.b12 = sb_all("w12", [P, E2, F2]), sb_all("b12", [P, E2, F2 // P])
    c.w22, c.b22 = sb_all("w22", [P, E2, F2 // P, D]), sb_all("b22", [E2, D])
    c.w2_loaded = ctx.enter_context(nc.semaphore("w2_loaded"))
    c.W2_ALL = 16 * 16
    c.wq0, c.wk0, c.wv0 = sb("wq0", [P, H0 * DK0]), sb("wk0", [P, H0 * DK0]), sb("wv0", [P, H0 * DK0])
    c.wo0 = sb("wo0", [P, NCH0, D])
    c.gate = sb("gate", [P, H0 * DK0])
    c.gate1m = sb("gate1m", [P, H0 * DK0])
    c.lnw0 = sb("lnw0", [P, F0 // P])
    c.lnb0 = sb("lnb0", [P, F0 // P])
    c.wfcT = sb("wfcT", [P, F0])
    c.wprojT = sb("wprojT", [P, F0 // P, D])
    c.zrow = sb("zrow", [P, 2, DK0 + 1])
    c.mem_mask = sb("mem_mask", [P, 3 * P])

    c.causal = sb("causal", [P, 3 * P])
    c.wqkv1, c.bqkv1 = sb("wqkv1", [P, 3 * D]), sb("bqkv1", [P, 3 * D])
    c.wproj1, c.bproj1 = sb("wproj1", [P, D]), sb("bproj1", [P, D])
    c.router1 = sb("router1", [P, E1])
    c.gating1, c.up1 = sb("gating1", [P, E1, F1]), sb("up1", [P, E1, F1])
    c.down1 = sb("down1", [P, E1, F1 // P, D])

    c.w1_loaded = ctx.enter_context(nc.semaphore("w1_loaded"))
    c.W1_ALL = 13 * 16
    c.x_loaded = ctx.enter_context(nc.semaphore("x_loaded"))
    c.w0_loaded = ctx.enter_context(nc.semaphore("w0_loaded"))
    consts_made = ctx.enter_context(nc.semaphore("consts_made"))
    gate_ready = ctx.enter_context(nc.semaphore("gate_ready"))
    abs_sums = ctx.enter_context(nc.semaphore("abs_sums"))
    totals = ctx.enter_context(nc.semaphore("totals"))
    ternary = ctx.enter_context(nc.semaphore("ternary"))
    turned = ctx.enter_context(nc.semaphore("turned"))
    out_copied = ctx.enter_context(nc.semaphore("ternary_copied"))

    with ExitStack() as tmp:
        wfc = tmp.enter_context(nc.sbuf_tensor("wfc", [P, F0 // P, D], F32))
        wproj = tmp.enter_context(nc.sbuf_tensor("wproj", [P, F0], F32))
        ones = tmp.enter_context(nc.sbuf_tensor("ones", [P, P], F32))
        sums = tmp.enter_context(nc.sbuf_tensor("abs_sum", [P, 2], F32))
        limit = tmp.enter_context(nc.sbuf_tensor("limit", [P, 4], F32))
        neg = tmp.enter_context(nc.sbuf_tensor("neg", [P, 2, F0], F32))
        bank = [tmp.enter_context(nc.psum_tensor(f"setup_bank{i}", [P, 512], F32)) for i in range(3)]
        block = tmp.enter_context(nc.Block())

        @block.sync
        def _(sp):
            sp.dma_start(wfc[:, :, :], A["L0_ffn_W_fc"].rearrange("(c p) d -> p c d", p=P)).then_inc(c.w0_loaded, 16)
            sp.dma_start(wproj[:, :], A["L0_ffn_W_proj"]).then_inc(c.w0_loaded, 16)
            x_rows = A["L0_attn_x"].rearrange("b (a p) d -> p (b a) d", p=P)
            sp.dma_start(c.x[:, 0:TILES * NSEQ, :], x_rows).then_inc(c.x_loaded, 16)
            sp.dma_start(c.wq0[:, :], A["L0_attn_Wq"]).then_inc(c.w0_loaded, 16)
            sp.dma_start(c.wk0[:, :], A["L0_attn_Wk"]).then_inc(c.w0_loaded, 16)
            sp.dma_start(c.wv0[:, :], A["L0_attn_Wv"]).then_inc(c.w0_loaded, 16)
            sp.dma_start(c.wo0[:, :, :], A["L0_attn_Wo"].rearrange("(c p) d -> p c d", p=P)).then_inc(c.w0_loaded, 16)

            for dst, src in (
                    (c.iota8[:, :], A["const_iota8"]), (c.causal[:, :], A["const_causal"]),
                    (c.row_mask[:, :], A["const_row_mask"]),
                    (c.cos1[:, :, :], A["const_cos1"].rearrange("(a p) k -> p a k", p=P)),
                    (c.sin1[:, :, :], A["const_sin1"].rearrange("(a p) k -> p a k", p=P)),
                    (c.wqkv1[:, :], A["L1_attn_W_qkv"]), (c.bqkv1[:, :], A["L1_attn_b_qkv"].partition_broadcast(P)),
                    (c.wproj1[:, :], A["L1_attn_W_proj"]), (c.bproj1[:, :], A["L1_attn_b_proj"].partition_broadcast(P)),
                    (c.router1[:, :], A["L1_ffn_router_kernel_DE"]),
                    (c.gating1[:, :, :], A["L1_ffn_kernel_gating_EDF"].rearrange("e d f -> d e f")),
                    (c.up1[:, :, :], A["L1_ffn_kernel_up_EDF"].rearrange("e d f -> d e f")),
                    (c.down1[:, :, :, :], A["L1_ffn_kernel_down_EFD"].rearrange("e (k p) d -> p e k d", p=P))):
                sp.dma_start(dst, src).then_inc(c.w1_loaded, 16)
            for name in ("Wq", "Wk", "Wv", "Wo"):
                sp.dma_start(c.w2[name][:, :], A["L2_attn_" + name]).then_inc(c.w2_loaded, 16)
            for name in ("bq", "bk", "bv", "bo"):
                sp.dma_start(c.w2[name][:, :], A["L2_attn_" + name].partition_broadcast(P)).then_inc(c.w2_loaded, 16)
            for dst, src in (
                    (c.beta[:, :], A["L2_attn_beta"].partition_broadcast(P)),
                    (c.same_head[:, :, :], A["const_same_head"]), (c.until[:, :], A["const_until"]),
                    (c.wg2[:, :], A["L2_ffn_wg"]),
                    (c.w12[:, :, :], A["L2_ffn_w1"].rearrange("e d f -> d e f")),
                    (c.b12[:, :, :], A["L2_ffn_b1"].rearrange("e (k p) -> p e k", p=P)),
                    (c.w22[:, :, :, :], A["L2_ffn_w2"].rearrange("e (k p) d -> p e k d", p=P)),
                    (c.b22[:, :], A["L2_ffn_b2"])):
                with nc.allow_non_contiguous_dma("the columns of b1 are small"):
                    sp.dma_start(dst, src).then_inc(c.w2_loaded, 16)

        @block.scalar
        def _(act):
            betas = A["L0_attn_betas"].rearrange("a h b v -> (a b) (h v)")
            act.dma_start(c.gate[:, :], betas[0].partition_broadcast(P)).then_inc(gate_ready, 16)
            with nc.allow_non_contiguous_dma("two small columns"):
                act.dma_start(c.lnw0[:, :], A["L0_ffn_ln_w"].rearrange("(c p) -> p c", p=P)).then_inc(c.w0_loaded, 16)
                act.dma_start(c.lnb0[:, :], A["L0_ffn_ln_b"].rearrange("(c p) -> p c", p=P)).then_inc(c.w0_loaded, 16)
            act.wait_ge(gate_ready, 16)
            nc.scalar.activation(c.gate[:, :], c.gate[:, :], ACT.Sigmoid).then_inc(gate_ready, 1)

        @block.gpsimd
        def _(pool):
            nc.gpsimd.memset(c.minus_half[:, :], -0.5)
            nc.gpsimd.memset(c.x[:, TILES * NSEQ:, :], 0.0)
            nc.gpsimd.memset(c.ident[:, :], 0.0)
            nc.gpsimd.memset(c.zrow[:, :, :], 0.0)
            nc.gpsimd.memset(c.mem_mask[:, :], 1.0)
            nc.gpsimd.drain()
            nc.gpsimd.affine_select(out=c.ident[:, :], in_=c.ident[:, :], compare_op=ALU.not_equal, fill=1.0,
                                    base=0, pattern=[[-1, P]], channel_multiplier=1)
            for lo, hi in ((0, 2 * P), (2 * P, 3 * P)):
                seg = c.mem_mask[:, lo:hi].rearrange("p (a r) -> p a r", r=SEG)
                nc.gpsimd.affine_select(out=seg, in_=seg, compare_op=ALU.is_gt, fill=0.0, base=0,
                                        pattern=[[SEG, (hi - lo) // SEG], [0, SEG]], channel_multiplier=-1)
            nc.gpsimd.memset(c.zrow[0:DK0, 0, DK0:DK0 + 1], 1.0 / DK0)
            nc.gpsimd.drain()
            nc.gpsimd.memset(c.zrow[DK0:P, 1, DK0:DK0 + 1], 1.0 / DK0).then_inc(consts_made, 1)

        @block.vector
        def _(dve):
            nc.vector.memset(ones[:, :], 1.0)
            dve.wait_ge(c.w0_loaded, 16 * 8)
            nc.vector.tensor_reduce(sums[:, 0:1], wfc[:, :, :], mybir.AxisListType.XY, ALU.add,
                                    apply_absolute_value=True)
            nc.vector.tensor_reduce(sums[:, 1:2], wproj[:, :], AX, ALU.add,
                                    apply_absolute_value=True).then_inc(abs_sums, 1)
            dve.wait_ge(totals, 1)
            nc.vector.tensor_scalar(limit[:, 2:4], bank[2][:, 0:2], 1.0 / (F0 * D), 1e-6, ALU.mult, ALU.add)
            nc.vector.drain()
            nc.vector.tensor_scalar(limit[:, 0:2], limit[:, 2:4], 0.5, None, ALU.mult)
            nc.vector.tensor_scalar(limit[:, 2:4], limit[:, 2:4], -0.5, None, ALU.mult)
            nc.vector.drain()
            for i, w in enumerate((wfc[:, :, :].rearrange("p c d -> p (c d)"), wproj[:, :])):
                nc.vector.tensor_scalar(neg[:, i, :], w, limit[:, 2 + i:3 + i], None, ALU.is_lt)
            nc.vector.drain()
            for i, w in enumerate((wfc[:, :, :].rearrange("p c d -> p (c d)"), wproj[:, :])):
                done = nc.vector.scalar_tensor_tensor(out=w, in0=w, scalar=limit[:, i:i + 1], in1=neg[:, i, :],
                                                      op0=ALU.is_gt, op1=ALU.subtract)
            done.then_inc(ternary, 1)
            dve.wait_ge(gate_ready, 17)
            nc.vector.tensor_scalar(c.gate1m[:, :], c.gate[:, :], -1.0, 1.0, ALU.mult, ALU.add)
            dve.wait_ge(turned, 1)
            nc.vector.tensor_copy(c.wfcT[:, :], bank[0][:, :])
            nc.vector.tensor_copy(c.wprojT[:, :, :].rearrange("p c d -> p (c d)"), bank[1][:, :]).then_inc(out_copied, 1)

        @block.tensor
        def _(pe):
            pe.wait_ge(consts_made, 1)
            pe.wait_ge(abs_sums, 1)
            nc.tensor.matmul(bank[2][:, 0:2], ones[:, :], sums[:, :], start=True, stop=True).then_inc(totals, 1)
            pe.wait_ge(ternary, 1)
            for j in range(F0 // P):
                nc.tensor.transpose(bank[0][:, j * P:(j + 1) * P], wfc[:, j, :], c.ident[:, :])
                done = nc.tensor.transpose(bank[1][:, j * P:(j + 1) * P], wproj[:, j * P:(j + 1) * P], c.ident[:, :])
            done.then_inc(turned, 1)


def layer0(nc, c):
    with ExitStack() as ctx:
        def sb(name, shape):
            return ctx.enter_context(nc.sbuf_tensor("a0_" + name, shape, F32))

        def sem(name):
            return layer_semaphore(nc, "l0_" + name)

        bank = [ctx.enter_context(nc.psum_tensor(f"l0_bank{i}", [P, 512], F32)) for i in range(8)]
        qk = sb("qk", [P, NCH0, 2, T])
        pos = sb("pos", [P, NCH0, 2, T])
        low = sb("low", [P, 2, 2 * T])
        vdot = sb("vdot", [P, TILES, H0 * DK0])
        vmem = sb("vmem", [P, TILES, H0, DK0 + 1])
        AG = TILES * H0 // 2
        top = sb("top", [P, 2, AG])
        shifted = sb("shifted", [P, 2, AG, SEG])
        recip = sb("recip", [P, TILES, H0])
        total = sb("total", [P, AG, 2])
        probsT = sb("probsT", [P, 2, AG, P])
        memT = sb("memT", [P, 2, 3 * P])
        rden = sb("rden", [P, TILES, HALF0])
        part = sb("part", [P, TILES, HALF0, DK0])
        part2 = sb("part2", [P, TILES, HALF0, DK0])
        att = sb("att", [P, TILES, H0 * DK0])
        attT = sb("attT", [P, TILES, NCH0, P])
        h = sb("h", [P, TILES, F0])
        hstats = sb("hstats", [P, TILES, 6])
        hmv = sb("hmv", [P, TILES, 2])
        hve = sb("hve", [P, TILES])
        hrstd = sb("hrstd", [P, TILES])
        hT = sb("hT", [P, TILES, F0 // P, P])
        th = sb("th", [P, TILES, D])
        u = sb("u", [P, TILES, D])

        s = NormSems(sem, "n")
        free = [sem(f"bank{i}_read") for i in range(8)]
        PER0, PER1, PER45 = 5, 4, 7
        qk_in_psum = sem("qk_in_psum")
        v_in_psum = sem("v_in_psum")
        h_in_psum = sem("h_in_psum")
        low_ready = sem("low_ready")
        low_exp = sem("low_exp")
        pos_ready = sem("pos_ready")
        scores_in_psum = sem("scores_in_psum")
        shifted_ready = sem("shifted_ready")
        exp_ready = sem("exp_ready")
        probs_ready = sem("probs_ready")
        mem_scores = sem("mem_scores")
        mem_used = sem("mem_used")
        dot_done = sem("dot_done")
        att_ready = sem("att_ready")
        attT_in_psum = sem("attT_in_psum")
        hvar_ready = sem("hvar_ready")
        hrstd_ready = sem("hrstd_ready")
        hn_ready = sem("hn_ready")
        hT_in_psum = sem("hT_in_psum")
        sz_in_psum = sem("sz_in_psum")
        th_ready = sem("th_ready")

        block = ctx.enter_context(nc.Block())

        @block.tensor
        def _(pe):
            pe.sem_inc(free[1], 1)
            for i in (2, 3, 4, 5, 6, 7):
                pe.sem_inc(free[i], 1)
            norm_transpose(nc, c, s, 0, bank[0])
            with pe.Fori(0, NSEQ) as n:
                pe.wait_ge(free[0], PER0 * n + 1)
                for j in range(NCH0):
                    per = PER0 if j % 2 == 0 else PER1
                    pe.wait_ge(free[j % 2], per * n + j // 2 + 1)
                    cols = slice(j * P, (j + 1) * P)
                    nc.tensor.matmul(bank[j % 2][:, 0:T], c.wq0[:, cols], c.xnT[:, :], start=True, stop=True)
                    nc.tensor.matmul(bank[j % 2][:, T:2 * T], c.wk0[:, cols], c.xnT[:, :],
                                     start=True, stop=True).then_inc(qk_in_psum, 1)
                for a in range(TILES):
                    pe.wait_ge(free[a], (PER0, PER1)[a] * n + 3)
                    nc.tensor.matmul(bank[a][:, :], c.xnT[:, a * P:(a + 1) * P], c.wv0[:, :],
                                     start=True, stop=True).then_inc(v_in_psum, 1)
                for a in range(TILES):
                    if a == 1:
                        pe.wait_ge(free[0], PER0 * n + 3)
                        pe.wait_ge(free[2], 2 * n + 1)
                        pe.wait_ge(free[3], 2 * n + 1)
                        pe.wait_ge(shifted_ready, 2 * n + 1)
                    pe.wait_ge(free[a], (PER0, PER1)[a] * n + 4)
                    nc.tensor.matmul(bank[a][:, :], c.xnT[:, a * P:(a + 1) * P], c.wfcT[:, :],
                                     start=True, stop=True).then_inc(h_in_psum, 1)
                for odd in range(2):
                    rows = slice(DK0 * odd, DK0 * odd + DK0)
                    for ag in range(AG):
                        a, pair = divmod(ag, H0 // 2)
                        for g in range(P // SEG):
                            t0 = a * P + g * SEG
                            done = nc.tensor.matmul(
                                bank[2 + odd][g * SEG:(g + 1) * SEG, ag * SEG:(ag + 1) * SEG],
                                qk[rows, pair, 0, t0:t0 + SEG], qk[rows, pair, 1, t0:t0 + SEG],
                                start=True, stop=True)
                    done.then_inc(scores_in_psum, 1)

                def memory_scores(hd):
                    b = 4 + hd % 2
                    pe.wait_ge(free[b], PER45 * n + hd // 2 + 1)
                    rows = slice(DK0 * (hd % 2), DK0 * (hd % 2) + DK0)
                    nc.tensor.matmul(bank[b][:, 0:T], pos[rows, hd // 2, 1, 0:P], pos[rows, hd // 2, 0, :],
                                     start=True, stop=True)
                    nc.tensor.matmul(bank[b][:, T:3 * P], pos[rows, hd // 2, 1, P:T], pos[rows, hd // 2, 0, P:T],
                                     start=True, stop=True).then_inc(mem_scores, 1)

                def memory_out(hd):
                    if hd % HALF0 == 0:
                        pe.wait_ge(free[6], 2 * n + hd // HALF0 + 1)
                        pe.wait_ge(free[7], 2 * n + hd // HALF0 + 1)
                    pe.wait_ge(free[4 + hd % 2], PER45 * n + hd // 2 + 2)
                    w = DK0 + 1
                    for a in range(TILES):
                        out = bank[6 + a][:, (hd % HALF0) * w:(hd % HALF0 + 1) * w]
                        for kt in range(a + 1):
                            lo = (a if kt == 0 else 2) * P
                            nc.tensor.matmul(out, memT[:, hd % 2, lo:lo + P], vmem[:, kt, hd, :],
                                             start=(kt == 0), stop=False)
                        done = nc.tensor.matmul(out, pos[:, hd // 2, 0, a * P:(a + 1) * P],
                                                c.zrow[:, hd % 2, :],
                                                start=False, stop=True)
                    done.then_inc(mem_used, 1)

                def softmax_out(half):
                    pe.wait_ge(probs_ready, n + 1)
                    if half == 1:
                        pe.wait_ge(free[2], 2 * n + 2)
                        pe.wait_ge(free[3], 2 * n + 2)
                    for a in range(TILES):
                        for i in range(HALF0):
                            hd = half * HALF0 + i
                            done = nc.tensor.matmul(bank[2 + a][:, 256 + i * DK0:256 + (i + 1) * DK0],
                                                    probsT[:, hd % 2, a * (H0 // 2) + hd // 2, :], vdot[:, a, hd * DK0:(hd + 1) * DK0],
                                                    start=True, stop=True)
                    done.then_inc(dot_done, 1)

                pe.wait_ge(pos_ready, NCH0 * n + NCH0)
                pe.wait_ge(free[0], PER0 * n + 4)
                pe.wait_ge(free[1], PER1 * n + 4)
                memory_scores(0)
                for hd in range(H0):
                    if hd + 1 < H0:
                        memory_scores(hd + 1)
                    memory_out(hd)
                    if hd % HALF0 == HALF0 - 1:
                        softmax_out(hd // HALF0)
                pe.wait_ge(hn_ready, n + 1)
                for a in range(TILES):
                    pe.wait_ge(free[4 + a], PER45 * n + 5)
                    for j in range(F0 // P):
                        done = nc.tensor.transpose(bank[4 + a][:, j * P:(j + 1) * P], h[:, a, j * P:(j + 1) * P],
                                                   c.ident[:, :])
                    done.then_inc(hT_in_psum, 1)
                pe.wait_ge(free[0], PER0 * n + 5)
                norm_transpose(nc, c, s, n + 1, bank[0])
                pe.wait_ge(att_ready, 2 * n + 2)
                for a in range(TILES):
                    pe.wait_ge(free[4 + a], PER45 * n + 6)
                    for j in range(NCH0):
                        done = nc.tensor.transpose(bank[4 + a][:, j * P:(j + 1) * P],
                                                   att[:, a, j * P:(j + 1) * P], c.ident[:, :])
                    done.then_inc(attT_in_psum, 1)
                for a in range(TILES):
                    pe.wait_ge(free[4 + a], PER45 * n + 7)
                    for j in range(F0 // P):
                        nc.tensor.matmul(bank[4 + a][:, 0:D], hT[:, a, j, :], c.wprojT[:, j, :],
                                         start=(j == 0), stop=(j == F0 // P - 1))
                    for j in range(NCH0):
                        done = nc.tensor.matmul(bank[4 + a][:, D:2 * D], attT[:, a, j, :], c.wo0[:, j, :],
                                                start=(j == 0), stop=(j == NCH0 - 1))
                    done.then_inc(sz_in_psum, 1)

        @block.scalar
        def _(act):
            norm_copy(nc, c, s, 0, bank[0], free[0])
            with act.Fori(0, NSEQ) as n:
                def copy_qk(j):
                    if j == 0:
                        act.wait_ge(scores_in_psum, 2 * n + 1)
                    act.wait_ge(qk_in_psum, NCH0 * n + j + 1)
                    nc.scalar.activation(qk[:, j, :, :].rearrange("p a t -> p (a t)"), bank[j % 2][:, :],
                                         ACT.Copy).then_inc(free[j % 2], 1)

                def exp_low(j):
                    act.wait_ge(low_ready, NCH0 * n + j + 1)
                    nc.scalar.activation(low[:, j % 2, :], low[:, j % 2, :], ACT.Exp).then_inc(low_exp, 1)

                copy_qk(0)
                for j in range(1, NCH0):
                    copy_qk(j)
                    exp_low(j - 1)
                exp_low(NCH0 - 1)
                for a in range(TILES):
                    act.wait_ge(shifted_ready, TILES * n + a + 2)
                    rows = shifted[:, a, :, :].rearrange("p h k -> p (h k)")
                    nc.scalar.activation(rows, rows, ACT.Exp, scale=DK0 ** -0.5).then_inc(exp_ready, 1)
                act.wait_ge(hT_in_psum, TILES * n + 1)
                for a in range(TILES):
                    act.wait_ge(h_in_psum, TILES * n + a + 1)
                    nc.scalar.activation(h[:, a, :], bank[a][:, :], ACT.Gelu).then_inc(free[a], 1)
                act.wait_ge(sz_in_psum, TILES * n + 1)
                for a in range(TILES):
                    act.wait_ge(hT_in_psum, TILES * n + a + 2)
                    for j in range(F0 // P):
                        done = nc.scalar.activation(hT[:, a, j, :], bank[4 + a][:, j * P:(j + 1) * P], ACT.Identity,
                                                    bias=c.lnb0[:, j:j + 1], scale=c.lnw0[:, j:j + 1])
                    done.then_inc(free[4 + a], 1)
                act.wait_ge(h_in_psum, TILES * n + 2)
                norm_copy(nc, c, s, n + 1, bank[0], free[0])
                for a in range(TILES):
                    act.wait_ge(attT_in_psum, TILES * n + a + 2)
                    nc.scalar.activation(attT[:, a, :, :].rearrange("p c t -> p (c t)"), bank[4 + a][:, :],
                                         ACT.Copy).then_inc(free[4 + a], 1)
                for a in range(TILES):
                    act.wait_ge(sz_in_psum, TILES * n + a + 2)
                    nc.scalar.activation(th[:, a, :], bank[4 + a][:, 0:D], ACT.Tanh, scale=0.5).then_inc(th_ready, 1)

        @block.gpsimd
        def _(pool):
            norm_power(nc, c, s, 0)
            with pool.Fori(0, NSEQ) as n:
                norm_power(nc, c, s, n + 1)
                pool.wait_ge(hvar_ready, n + 1)
                nc.gpsimd.tensor_tensor(hrstd[:, :], hve[:, :], c.minus_half[:, 0:TILES], ALU.pow)\
                    .then_inc(hrstd_ready, 1)

        @block.vector
        def _(dve):
            nc.vector.memset(probsT[:, :, :, :].rearrange("p o g k -> p (o g k)"), 0.0)
            nc.vector.memset(vmem[:, :, :, DK0:DK0 + 1], 1.0)
            for g in (shifted_ready, scores_in_psum, hT_in_psum, sz_in_psum, mem_used, dot_done, attT_in_psum):
                dve.sem_inc(g, 1)
            dve.wait_ge(c.x_loaded, 16)
            norm_stats(nc, c, s, 0)
            norm_apply(nc, c, s, 0, True)
            with dve.Fori(0, NSEQ) as n:
                def take_low(j):
                    dve.wait_ge(free[j % 2], (PER0, PER1)[j % 2] * n + j // 2 + 2)
                    nc.vector.tensor_scalar(low[:, j % 2, :], qk[:, j, :, :].rearrange("p a t -> p (a t)"), 0.0, None,
                                            ALU.min).then_inc(low_ready, 1)

                def elu_plus_1(j):
                    if j == 0:
                        dve.wait_ge(mem_used, H0 * n + 1)
                    dve.wait_ge(low_exp, NCH0 * n + j + 1)
                    nc.vector.scalar_tensor_tensor(
                        out=pos[:, j, :, :].rearrange("p a t -> p (a t)"),
                        in0=qk[:, j, :, :].rearrange("p a t -> p (a t)"), scalar=0.0,
                        in1=low[:, j % 2, :], op0=ALU.max, op1=ALU.add).then_inc(pos_ready, 1)

                take_low(0)
                for j in range(1, NCH0):
                    take_low(j)
                    elu_plus_1(j - 1)
                    nc.vector.drain()
                elu_plus_1(NCH0 - 1)
                dve.wait_ge(dot_done, 2 * n + 1)
                for a in range(TILES):
                    dve.wait_ge(v_in_psum, TILES * n + a + 1)
                    nc.vector.tensor_tensor(vdot[:, a, :], bank[a][:, :], c.gate1m[:, :], ALU.mult)
                    nc.vector.tensor_tensor(vmem[:, a, :, 0:DK0], bank[a][:, :].rearrange("p (h v) -> p h v", h=H0),
                                            c.gate[:, :].rearrange("p (h v) -> p h v", h=H0), ALU.mult)\
                        .then_inc(free[a], 1)
                norm_stats(nc, c, s, n + 1)
                for a in range(TILES):
                    dve.wait_ge(scores_in_psum, TILES * n + a + 2)
                    nc.vector.tensor_reduce(top[:, a, :], bank[2 + a][:, 0:256].rearrange("p (h k) -> p h k", h=AG),
                                            AX, ALU.max)
                nc.vector.drain()
                for a in range(TILES):
                    nc.vector.tensor_tensor(shifted[:, a, :, :], bank[2 + a][:, 0:256].rearrange("p (h k) -> p h k", h=AG),
                                            bcast(top[:, a, :], SEG), ALU.subtract).then_inc(shifted_ready, 1)
                norm_apply(nc, c, s, n + 1, False)
                for a in range(TILES):
                    dve.wait_ge(exp_ready, TILES * n + a + 1)
                    nc.vector.tensor_reduce(total[:, :, a], shifted[:, a, :, :], AX, ALU.add)
                    for g in range(P // SEG):
                        rows = slice(g * SEG, (g + 1) * SEG)
                        nc.vector.transpose(probsT[rows, a, :, rows], shifted[rows, a, :, :])
                nc.vector.drain()
                nc.vector.reciprocal(recip[:, :, :].rearrange("p a h -> p (a h)"),
                                     total[:, :, :].rearrange("p g o -> p (g o)")).then_inc(probs_ready, 1)

                def mask_memory(hd):
                    b = 4 + hd % 2
                    if hd >= 2:
                        dve.wait_ge(mem_used, H0 * n + hd)
                    dve.wait_ge(mem_scores, H0 * n + hd + 1)
                    nc.vector.tensor_tensor(memT[:, hd % 2, :], bank[b][:, 0:3 * P], c.mem_mask[:, :], ALU.mult)\
                        .then_inc(free[b], 1)

                def combine(half):
                    dve.wait_ge(mem_used, H0 * n + (half + 1) * HALF0 + 1)
                    w = DK0 + 1
                    mem = [bank[6 + a][:, 0:HALF0 * w].rearrange("p (h v) -> p h v", v=w) for a in range(TILES)]
                    for a in range(TILES):
                        nc.vector.reciprocal(rden[:, a, :], mem[a][:, :, DK0])
                    nc.vector.drain()
                    for a in range(TILES):
                        nc.vector.tensor_tensor(part[:, a, :, :], mem[a][:, :, 0:DK0], bcast(rden[:, a, :], DK0),
                                                ALU.mult).then_inc(free[6 + a], 1)
                    dve.wait_ge(dot_done, 2 * n + half + 2)
                    for a in range(TILES):
                        nc.vector.tensor_tensor(part2[:, a, :, :],
                                                bank[2 + a][:, 256:512].rearrange("p (h v) -> p h v", v=DK0),
                                                bcast(recip[:, a, half * HALF0:(half + 1) * HALF0], DK0), ALU.mult)\
                            .then_inc(free[2 + a], 1)
                    nc.vector.drain()
                    if half == 0:
                        dve.wait_ge(attT_in_psum, TILES * n + 1)
                    lo = half * HALF0 * DK0
                    for a in range(TILES):
                        done = nc.vector.tensor_tensor(
                            att[:, a, lo:lo + HALF0 * DK0].rearrange("p (h v) -> p h v", v=DK0),
                            part[:, a, :, :], part2[:, a, :, :], ALU.add)
                    done.then_inc(att_ready, 1)

                for hd in range(HALF0 + 1):
                    mask_memory(hd)
                dve.wait_ge(free[0], PER0 * n + 5)
                dve.wait_ge(free[1], PER1 * n + 5)
                for a in range(TILES):
                    nc.vector.bn_stats(hstats[:, a, :], h[:, a, :])
                nc.vector.drain()
                for a in range(TILES):
                    nc.vector.bn_aggr(hmv[:, a, :], hstats[:, a, :])
                nc.vector.drain()
                nc.vector.tensor_scalar(hve[:, :], hmv[:, :, 1], LN_EPS, None, ALU.add).then_inc(hvar_ready, 1)
                combine(0)
                for hd in range(HALF0 + 1, H0):
                    mask_memory(hd)
                dve.wait_ge(hrstd_ready, n + 1)
                for a in range(TILES):
                    done = nc.vector.tensor_scalar(h[:, a, :], h[:, a, :], hmv[:, a, 0:1], hrstd[:, a:a + 1],
                                                   ALU.subtract, ALU.mult)
                done.then_inc(hn_ready, 1)
                combine(1)
                for a in range(TILES):
                    dve.wait_ge(th_ready, TILES * n + a + 1)
                    nc.vector.scalar_tensor_tensor(out=u[:, a, :], in0=th[:, a, :], scalar=1.0, in1=bank[4 + a][:, 0:D],
                                                   op0=ALU.add, op1=ALU.mult)
                nc.vector.drain()
                for a in range(TILES):
                    nc.vector.scalar_tensor_tensor(out=u[:, a, :], in0=u[:, a, :], scalar=0.5,
                                                   in1=bank[4 + a][:, D:2 * D], op0=ALU.mult, op1=ALU.mult)\
                        .then_inc(free[4 + a], 1)
                nc.vector.drain()
                for a in range(TILES):
                    nc.vector.tensor_tensor(c.x[:, 2 * n + a, :], c.x[:, 2 * n + a, :], u[:, a, :], ALU.add)


def layer1(nc, c):
    with ExitStack() as ctx:
        def sb(name, shape, dtype=F32):
            return ctx.enter_context(nc.sbuf_tensor("b1_" + name, shape, dtype))

        def sem(name):
            return layer_semaphore(nc, "l1_" + name)

        bank = [ctx.enter_context(nc.psum_tensor(f"l1_bank{i}", [P, 512], F32)) for i in range(8)]
        KF = F1 // P
        CH = E1 * KF
        assert CH == H1 and KF == 2
        RP = 4
        qkv = sb("qkv", [P, TILES, 3 * D])
        rot = sb("rot", [P, TILES, 2, H1, HD1 // 2, 2])
        t1 = sb("t1", [P, 2, H1, HD1 // 2])
        t2 = sb("t2", [P, 2, H1, HD1 // 2])
        t3 = sb("t3", [P, 2, H1, HD1 // 2])
        t4 = sb("t4", [P, 2, H1, HD1 // 2])
        qT = sb("qT", [P, GR, T])
        kT = sb("kT", [P, T])
        neg = sb("neg", [P, RP, 3 * P])
        nmax = sb("nmax", [P, RP, TILES])
        total = sb("total", [P, TILES, H1])
        recip = sb("recip", [P, TILES, H1])
        pT = sb("pT", [P, 2, 3 * P])
        y = sb("y", [P, TILES, D])
        yT = sb("yT", [P, T])
        s_out = sb("s_out", [P, TILES, D])
        r = RouteBuffers(sb, sem)
        diff = sb("diff", [P, TILES])
        ediff = sb("ediff", [P, TILES])
        ediff1 = sb("ediff1", [P, TILES])
        first = sb("first", [P, TILES])
        second = sb("second", [P, TILES])
        comb = sb("comb", [P, TILES, E1])
        comb2 = sb("comb2", [P, TILES, E1])
        th = sb("th", [P, 2, T])
        gated = sb("gated", [P, 2, T])
        fused = sb("fused", [P, 4, T])
        acc = sb("acc", [P, TILES, D])
        th_z = sb("th_z", [P, TILES, D])
        u = sb("u", [P, TILES, D])
        SCALE = float(HD1) ** -0.5

        s = NormSems(sem, "n")
        read = [sem(f"bank{i}_read") for i in range(8)]
        PER0 = 8
        PERS = H1 // 2
        PER7 = E1
        qkv_in_psum = sem("qkv_in_psum")
        logits_in_psum = sem("logits_in_psum")
        diff_ready = sem("diff_ready")
        ediff_ready = sem("ediff_ready")
        rot_ready = sem("rot_ready")
        qkT_in_psum = sem("qkT_in_psum")
        scores_in_psum = sem("scores_in_psum")
        exp_ready = sem("exp_ready")
        pT_in_psum = sem("pT_in_psum")
        head_done = sem("head_done")
        y_ready = sem("y_ready")
        yT_in_psum = sem("yT_in_psum")
        s_in_psum = sem("s_in_psum")
        hidden_in_psum = sem("hidden_in_psum")
        th_ready = sem("th_ready")
        down_in_psum = sem("down_in_psum")
        acc_ready = sem("acc_ready")
        th_z_ready = sem("th_z_ready")

        block = ctx.enter_context(nc.Block())

        @block.tensor
        def _(pe):
            for i in range(1, 8):
                pe.sem_inc(read[i], 1)
            pe.wait_ge(c.w1_loaded, c.W1_ALL)
            norm_transpose(nc, c, s, 0, bank[0])
            with pe.Fori(0, NSEQ) as n:
                pe.wait_ge(read[0], PER0 * n + 1)
                for a in range(TILES):
                    pe.wait_ge(read[0], PER0 * n + a + 1)
                    nc.tensor.matmul(bank[0][:, 0:3 * D], c.xnT[:, a * P:(a + 1) * P], c.wqkv1[:, :],
                                     start=True, stop=True).then_inc(qkv_in_psum, 1)
                pe.wait_ge(read[0], PER0 * n + 3)
                for a in range(TILES):
                    done = nc.tensor.matmul(bank[0][:, a * E1:(a + 1) * E1], c.xnT[:, a * P:(a + 1) * P],
                                            c.router1[:, :], start=True, stop=True)
                done.then_inc(logits_in_psum, 1)

                def hidden(k):
                    b, e, f = 5 + k % 2, k // KF, k % KF
                    pe.wait_ge(read[b], PERS * n + k // 2 + 1)
                    nc.tensor.matmul(bank[b][:, 0:T], c.gating1[:, e, f * P:(f + 1) * P], c.xnT[:, :],
                                     start=True, stop=True)
                    nc.tensor.matmul(bank[b][:, T:2 * T], c.up1[:, e, f * P:(f + 1) * P], c.xnT[:, :],
                                     start=True, stop=True).then_inc(hidden_in_psum, 1)

                def scores(h):
                    b, rows = 1 + h % 2, slice(ROWS * (h // GR), ROWS * (h // GR) + ROWS)
                    pe.wait_ge(read[b], PERS * n + h // 2 + 1)
                    nc.tensor.matmul(bank[b][:, 0:P], qT[rows, h % GR, 0:P], kT[rows, 0:P], start=True, stop=True)
                    nc.tensor.matmul(bank[b][:, P:3 * P], qT[rows, h % GR, P:T], kT[rows, :],
                                     start=True, stop=True).then_inc(scores_in_psum, 1)

                def turn_probs(h):
                    b = 3 + h % 2
                    pe.wait_ge(read[b], PERS * n + h // 2 + 1)
                    pe.wait_ge(exp_ready, H1 * n + h + 1)
                    for j in range(3):
                        done = nc.tensor.transpose(bank[b][:, j * P:(j + 1) * P],
                                                   neg[:, h % RP, j * P:(j + 1) * P], c.ident[:, :])
                    done.then_inc(pT_in_psum, 1)

                def head_out(h):
                    pe.wait_ge(read[3 + h % 2], PERS * n + h // 2 + 2)
                    v = [qkv[:, a, 3 * HD1 * h + 2 * HD1:3 * HD1 * h + 3 * HD1] for a in range(TILES)]
                    out = [bank[0][:, a * D + h * HD1:a * D + (h + 1) * HD1] for a in range(TILES)]
                    p = pT[:, h % 2, :]
                    nc.tensor.matmul(out[0], p[:, 0:P], v[0], start=True, stop=True)
                    nc.tensor.matmul(out[1], p[:, P:2 * P], v[0], start=True, stop=False)
                    nc.tensor.matmul(out[1], p[:, 2 * P:3 * P], v[1], start=False, stop=True).then_inc(head_done, 1)

                def down(e):
                    pe.wait_ge(read[6], PERS * n + e + 2)
                    pe.wait_ge(read[7], PER7 * n + e + 1)
                    for a in range(TILES):
                        for f in range(KF):
                            done = nc.tensor.matmul(bank[7][:, a * D:(a + 1) * D],
                                                    fused[:, (KF * e + f) % 4, a * P:(a + 1) * P],
                                                    c.down1[:, e, f, :], start=(f == 0), stop=(f == KF - 1))
                    done.then_inc(down_in_psum, 1)

                hidden(0)
                hidden(1)
                pe.wait_ge(rot_ready, n + 1)
                pe.wait_ge(read[0], PER0 * n + 4)
                for a in range(TILES):
                    for i in range(2):
                        done = nc.tensor.transpose(bank[0][:, i * T + a * P:i * T + (a + 1) * P],
                                                   rot[:, a, i, :, :, :].rearrange("p h k o -> p (h k o)"),
                                                   c.ident[:, :])
                done.then_inc(qkT_in_psum, 1)
                pe.wait_ge(read[0], PER0 * n + 5)
                for k in range(H1 + 2):
                    if k < H1:
                        scores(k)
                    if k + 2 < CH:
                        hidden(k + 2)
                    if 1 <= k <= H1:
                        turn_probs(k - 1)
                    if k >= 2:
                        head_out(k - 2)
                    if k % 2 and k < H1:
                        down(k // 2)
                pe.wait_ge(y_ready, n + 1)
                for a in range(TILES):
                    done = nc.tensor.transpose(bank[0][:, a * P:(a + 1) * P], y[:, a, :], c.ident[:, :])
                done.then_inc(yT_in_psum, 1)
                pe.wait_ge(read[0], PER0 * n + 7)
                for a in range(TILES):
                    done = nc.tensor.matmul(bank[0][:, a * D:(a + 1) * D], yT[:, a * P:(a + 1) * P], c.wproj1[:, :],
                                            start=True, stop=True)
                done.then_inc(s_in_psum, 1)
                pe.wait_ge(read[0], PER0 * n + 8)
                norm_transpose(nc, c, s, n + 1, bank[0])

        @block.scalar
        def _(act):
            norm_copy(nc, c, s, 0, bank[0], read[0])
            with act.Fori(0, NSEQ) as n:
                def tanh_gate(k):
                    act.wait_ge(hidden_in_psum, CH * n + k + 1)
                    nc.scalar.activation(th[:, k % 2, :], bank[5 + k % 2][:, 0:T], ACT.Tanh, scale=0.5)\
                        .then_inc(th_ready, 1)

                def exp_scores(h):
                    act.wait_ge(read[1 + h % 2], PERS * n + h // 2 + 2)
                    for a, cols in enumerate((slice(0, P), slice(P, 3 * P))):
                        done = nc.scalar.activation(neg[:, h % RP, cols], neg[:, h % RP, cols], ACT.Exp,
                                                    bias=nmax[:, h % RP, a:a + 1], scale=-1.0,
                                                    accum_out=total[:, a, h:h + 1])
                    done.then_inc(exp_ready, 1)

                def copy_pT(h):
                    if h >= 2:
                        act.wait_ge(head_done, H1 * n + h - 1)
                    act.wait_ge(pT_in_psum, H1 * n + h + 1)
                    nc.scalar.activation(pT[:, h % 2, :], bank[3 + h % 2][:, 0:3 * P], ACT.Copy)\
                        .then_inc(read[3 + h % 2], 1)

                route_exp(nc, r, n)
                act.wait_ge(diff_ready, n + 1)
                nc.scalar.activation(ediff[:, :], diff[:, :], ACT.Exp).then_inc(ediff_ready, 1)
                tanh_gate(0)
                tanh_gate(1)
                act.wait_ge(qkT_in_psum, n + 1)
                nc.scalar.activation(kT[:, :], bank[0][:, T:2 * T], ACT.Copy)
                for i in range(GR):
                    done = nc.scalar.activation(qT[:, i, :], bank[0][:, 0:T], ACT.Copy, scale=c.row_mask[:, i:i + 1])
                done.then_inc(read[0], 1)
                for k in range(H1 + 1):
                    if k + 2 < CH:
                        tanh_gate(k + 2)
                    if k < H1:
                        exp_scores(k)
                    if k >= 1:
                        copy_pT(k - 1)
                act.wait_ge(acc_ready, n + 1)
                nc.scalar.activation(th_z[:, :, :], acc[:, :, :], ACT.Tanh, scale=0.5).then_inc(th_z_ready, 1)
                act.wait_ge(yT_in_psum, n + 1)
                nc.scalar.activation(yT[:, :], bank[0][:, 0:T], ACT.Copy).then_inc(read[0], 1)
                norm_copy(nc, c, s, n + 1, bank[0], read[0])

        @block.gpsimd
        def _(pool):
            norm_power(nc, c, s, 0)
            with pool.Fori(0, NSEQ) as n:
                norm_power(nc, c, s, n + 1)

        @block.vector
        def _(dve):
            dve.wait_ge(c.w1_loaded, c.W1_ALL)
            norm_stats(nc, c, s, 0)
            norm_apply(nc, c, s, 0, True)
            with dve.Fori(0, NSEQ) as n:
                for a in range(TILES):
                    dve.wait_ge(qkv_in_psum, TILES * n + a + 1)
                    nc.vector.tensor_tensor(qkv[:, a, :], bank[0][:, 0:3 * D], c.bqkv1[:, :], ALU.add)\
                        .then_inc(read[0], 1)
                dve.wait_ge(logits_in_psum, n + 1)
                route_shift(nc, r, bank[0][:, 0:TILES * E1].rearrange("p (a e) -> p a e", e=E1), read[0])
                for a in range(TILES):
                    part = qkv[:, a, :].rearrange("p (h i k o) -> p i h k o", h=H1, i=3, o=2)
                    cos = c.cos1[:, a, :].rearrange("p (i h k) -> p i h k", i=2, h=H1)
                    sin = c.sin1[:, a, :].rearrange("p (i h k) -> p i h k", i=2, h=H1)
                    for i in range(2):
                        even, odd = part[:, i, :, :, 0], part[:, i, :, :, 1]
                        nc.vector.tensor_tensor(t1[:, i], even, cos[:, i], ALU.mult)
                        nc.vector.tensor_tensor(t2[:, i], odd, sin[:, i], ALU.mult)
                        nc.vector.tensor_tensor(t3[:, i], even, sin[:, i], ALU.mult)
                        nc.vector.tensor_tensor(t4[:, i], odd, cos[:, i], ALU.mult)
                    nc.vector.drain()
                    nc.vector.tensor_tensor(rot[:, a, :, :, :, 0], t1[:, :, :, :], t2[:, :, :, :], ALU.subtract)
                    done = nc.vector.tensor_tensor(rot[:, a, :, :, :, 1], t3[:, :, :, :], t4[:, :, :, :], ALU.add)
                    if a == 0:
                        nc.vector.drain()
                done.then_inc(rot_ready, 1)
                route_best(nc, r, n)
                nc.vector.tensor_tensor(diff[:, :], r.best[:, :, 1], r.best[:, :, 0], ALU.subtract)\
                    .then_inc(diff_ready, 1)

                def scores_come(h):
                    if h >= RP:
                        dve.wait_ge(pT_in_psum, H1 * n + h - RP + 1)
                    dve.wait_ge(scores_in_psum, H1 * n + h + 1)

                def fuse(k, h=None):
                    b = 5 + k % 2
                    dve.wait_ge(th_ready, CH * n + k + 1)
                    nc.vector.scalar_tensor_tensor(out=gated[:, k % 2, :], in0=th[:, k % 2, :], scalar=1.0,
                                                   in1=bank[b][:, 0:T], op0=ALU.add, op1=ALU.mult)
                    nc.vector.drain()
                    if h is not None:
                        scores_come(h)
                    nc.vector.tensor_tensor(fused[:, k % 4, :], gated[:, k % 2, :], bank[b][:, T:2 * T], ALU.mult)\
                        .then_inc(read[b], 1)

                def negate_scores(h):
                    b = 1 + h % 2
                    for a, (lo, hi) in enumerate(((0, P), (P, 3 * P))):
                        done = nc.vector.tensor_tensor_reduce(
                            neg[:, h % RP, lo:hi], bank[b][:, lo:hi], c.causal[:, lo:hi], -SCALE, 3e38,
                            ALU.add, ALU.min, nmax[:, h % RP, a:a + 1])
                    done.then_inc(read[b], 1)

                dve.wait_ge(ediff_ready, n + 1)
                nc.vector.tensor_scalar(ediff1[:, :], ediff[:, :], 1.0, None, ALU.add)
                nc.vector.drain()
                nc.vector.reciprocal(first[:, :], ediff1[:, :])
                nc.vector.drain()
                nc.vector.tensor_scalar(first[:, :], first[:, :], 0.5, None, ALU.mult)
                nc.vector.drain()
                nc.vector.tensor_tensor(second[:, :], first[:, :], ediff[:, :], ALU.mult)
                nc.vector.drain()
                for a in range(TILES):
                    nc.vector.tensor_scalar(comb[:, a, :], c.iota8[:, :], r.place[:, a, 0:1], first[:, a:a + 1],
                                            ALU.is_equal, ALU.mult)
                    nc.vector.tensor_scalar(comb2[:, a, :], c.iota8[:, :], r.place[:, a, 1:2], second[:, a:a + 1],
                                            ALU.is_equal, ALU.mult)
                nc.vector.drain()
                nc.vector.tensor_tensor(comb[:, :, :], comb[:, :, :], comb2[:, :, :], ALU.add)
                fuse(0)
                fuse(1)
                norm_stats(nc, c, s, n + 1)
                for k in range(H1):
                    if k + 2 < CH:
                        fuse(k + 2, k)
                    else:
                        scores_come(k)
                        nc.vector.memset(nmax[:, k % RP, :], 0.0)
                        nc.vector.drain()
                    negate_scores(k)
                    if k == 4:
                        norm_apply(nc, c, s, n + 1, False)
                    if k % 2:
                        e = k // 2
                        dve.wait_ge(down_in_psum, E1 * n + e + 1)
                        for a in range(TILES):
                            rows = bank[7][:, a * D:(a + 1) * D]
                            if e == 0:
                                done = nc.vector.tensor_scalar(acc[:, a, :], rows, comb[:, a, 0:1], None, ALU.mult)
                            else:
                                done = nc.vector.scalar_tensor_tensor(out=acc[:, a, :], in0=rows,
                                                                      scalar=comb[:, a, e:e + 1], in1=acc[:, a, :],
                                                                      op0=ALU.mult, op1=ALU.add)
                        done.then_inc(read[7], 1)
                nc.vector.drain().then_inc(acc_ready, 1)
                nc.vector.wait_ge(exp_ready, H1 * n + H1)
                nc.vector.reciprocal(recip[:, :, :], total[:, :, :])
                nc.vector.drain()
                dve.wait_ge(head_done, H1 * n + H1)
                nc.vector.tensor_tensor(y[:, :, :].rearrange("p a (h v) -> p (a h) v", v=HD1),
                                        bank[0][:, 0:TILES * D].rearrange("p (g v) -> p g v", v=HD1),
                                        bcast(recip[:, :, :].rearrange("p a h -> p (a h)"), HD1), ALU.mult)\
                    .then_inc(read[0], 1)
                nc.vector.drain().then_inc(y_ready, 1)
                dve.wait_ge(s_in_psum, n + 1)
                nc.vector.tensor_tensor(s_out[:, :, :], bank[0][:, 0:TILES * D].rearrange("p (a d) -> p a d", d=D),
                                        c.bproj1[:, :].unsqueeze(1).to_broadcast([P, TILES, D]), ALU.add)\
                    .then_inc(read[0], 1)
                nc.vector.drain()
                dve.wait_ge(th_z_ready, n + 1)
                close_layer(nc, c, n, s_out[:, :, :], acc[:, :, :], th_z[:, :, :], u[:, :, :])


def layer2(nc, c):
    with ExitStack() as ctx:
        def sb(name, shape, dtype=F32):
            return ctx.enter_context(nc.sbuf_tensor("c2_" + name, shape, dtype))

        def sem(name):
            return layer_semaphore(nc, "l2_" + name)

        bank = [ctx.enter_context(nc.psum_tensor(f"l2_bank{i}", [P, 512], F32)) for i in range(7)]
        KF = F2 // P
        wT = sb("wT", [P, 4, P])
        proj = sb("proj", [P, 4, P])
        brow = sb("brow", [P, 4, P])
        bcol = sb("bcol", [P, 4])
        nbeta = sb("nbeta", [P, 1])
        qk = sb("qk", [P, 2, T])
        kvk = sb("kvk", [P, 3, T])
        cum = sb("cum", [P, 3, T])
        qcum = sb("qcum", [P, 3, T])
        rden = sb("rden", [P, T])
        attT = sb("attT", [P, T])
        s_out = sb("s_out", [P, TILES, D])
        r = RouteBuffers(sb, sem)
        mask = sb("mask", [P, TILES, E2])
        kept = sb("kept", [P, TILES, E2])
        seen = sb("seen", [P, E2])
        comb = sb("comb", [P, TILES, E2])
        combT = sb("combT", [E2, T])
        hid = sb("hid", [P, 2, KF, T])
        acc = sb("acc", [P, TILES, D])
        th_z = sb("th_z", [P, TILES, D])
        u = sb("u", [P, TILES, D])

        s = NormSems(sem, "n")
        read = [sem(f"bank{i}_read") for i in range(7)]
        PER0 = 5
        PERU = E2
        PER3 = E2 + 1
        weights_turned = sem("weights_turned")
        weights_copied = sem("weights_copied")
        biases_turned = sem("biases_turned")
        attention_ready = sem("attention_weights_ready")
        beta_exp = sem("beta_exp")
        logits_in_psum = sem("logits_in_psum")
        mask_ready = sem("mask_ready")
        count_in_psum = sem("count_in_psum")
        comb_ready = sem("comb_ready")
        combT_in_psum = sem("combT_in_psum")
        qk_in_psum = sem("qk_in_psum")
        v_in_psum = sem("v_in_psum")
        qcum_ready = sem("qcum_ready")
        att_in_psum = sem("att_in_psum")
        attT_ready = sem("attT_ready")
        s_in_psum = sem("s_in_psum")
        hidden_in_psum = sem("hidden_in_psum")
        down_in_psum = sem("down_in_psum")
        acc_ready = sem("acc_ready")
        th_z_ready = sem("th_z_ready")

        block = ctx.enter_context(nc.Block())

        @block.sync
        def _(sp):
            with nc.allow_non_contiguous_dma("columns of small parameters"):
                for dst, src in c.w3_loads:
                    sp.dma_start(dst, src).then_inc(c.w3_loaded, 16)

        @block.tensor
        def _(pe):
            for i in range(1, 7):
                pe.sem_inc(read[i], 1)
            pe.wait_ge(c.w2_loaded, c.W2_ALL)
            for i, name in enumerate(("Wq", "Wk", "Wv", "Wo")):
                done = nc.tensor.transpose(bank[1][:, i * P:(i + 1) * P], c.w2[name][:, :], c.ident[:, :])
            done.then_inc(weights_turned, 1)
            pe.wait_ge(weights_copied, 1)
            for i in range(4):
                done = nc.tensor.transpose(bank[2][:, i * P:(i + 1) * P], brow[:, i, :], c.ident[:, :])
            done.then_inc(biases_turned, 1)
            norm_transpose(nc, c, s, 0, bank[0])
            pe.wait_ge(attention_ready, 1)
            with pe.Fori(0, NSEQ) as n:
                pe.wait_ge(read[0], PER0 * n + 1)
                for a in range(TILES):
                    done = nc.tensor.matmul(bank[0][:, a * E2:(a + 1) * E2], c.xnT[:, a * P:(a + 1) * P],
                                            c.wg2[:, :], start=True, stop=True)
                done.then_inc(logits_in_psum, 1)
                for b, lo, ready in ((4, 0, qk_in_psum), (5, 2, v_in_psum)):
                    pe.wait_ge(read[b], n + 1)
                    for i in range(2):
                        done = nc.tensor.matmul(bank[b][:, i * T:(i + 1) * T], proj[:, lo + i, :], c.xnT[:, :],
                                                start=True, stop=True)
                    done.then_inc(ready, 1)

                def up(e):
                    for b in range(2):
                        pe.wait_ge(read[1 + b], PERU * n + e + 1)
                        for i in range(2):
                            k = 2 * b + i
                            done = nc.tensor.matmul(bank[1 + b][:, i * T:(i + 1) * T],
                                                    c.w12[:, e, k * P:(k + 1) * P], c.xnT[:, :],
                                                    start=True, stop=True)
                        done.then_inc(hidden_in_psum, 1)

                def down(e):
                    pe.wait_ge(read[1], PERU * n + e + 2)
                    pe.wait_ge(read[2], PERU * n + e + 2)
                    pe.wait_ge(read[3], PER3 * n + e + 1)
                    for a in range(TILES):
                        for k in range(KF):
                            done = nc.tensor.matmul(bank[3][:, a * D:(a + 1) * D],
                                                    hid[:, e % 2, k, a * P:(a + 1) * P], c.w22[:, e, k, :],
                                                    start=(k == 0), stop=(k == KF - 1))
                    done.then_inc(down_in_psum, 1)

                up(0)
                up(1)
                pe.wait_ge(mask_ready, n + 1)
                pe.wait_ge(read[0], PER0 * n + 2)
                nc.tensor.matmul(bank[0][:, 0:E2], c.until[:, :], mask[:, 0, :], start=True, stop=True)
                nc.tensor.matmul(bank[0][:, E2:2 * E2], c.ones[:, 0:P], mask[:, 0, :], start=True, stop=False)
                nc.tensor.matmul(bank[0][:, E2:2 * E2], c.until[:, :], mask[:, 1, :], start=False, stop=True)
                nc.tensor.matmul(bank[0][:, 2 * E2:3 * E2], c.ones[:, 0:P], mask[:, 0, :], start=True, stop=False)
                nc.tensor.matmul(bank[0][:, 2 * E2:3 * E2], c.ones[:, 0:P], mask[:, 1, :], start=False, stop=True)\
                    .then_inc(count_in_psum, 1)
                for e in range(E2):
                    down(e)
                    if e + 2 < E2:
                        up(e + 2)
                    if e == 2:
                        pe.wait_ge(qcum_ready, n + 1)
                        pe.wait_ge(read[6], n + 1)
                        nc.tensor.matmul(bank[6][:, 0:T], c.same_head[:, 0, :], qcum[:, 0, :], start=True, stop=False)
                        nc.tensor.matmul(bank[6][:, 0:T], c.same_head[:, 1, :], qcum[:, 1, :], start=False, stop=True)
                        nc.tensor.matmul(bank[6][:, T:2 * T], c.same_head[:, 2, :], qcum[:, 2, :],
                                         start=True, stop=True).then_inc(att_in_psum, 1)
                    if e == 3:
                        pe.wait_ge(comb_ready, n + 1)
                        pe.wait_ge(read[0], PER0 * n + 3)
                        for a in range(TILES):
                            done = nc.tensor.transpose(bank[0][0:E2, a * P:(a + 1) * P], comb[:, a, :], c.ident[:, :])
                        done.then_inc(combT_in_psum, 1)
                    if e == 5:
                        pe.wait_ge(attT_ready, n + 1)
                        pe.wait_ge(read[0], PER0 * n + 4)
                        for a in range(TILES):
                            done = nc.tensor.matmul(bank[0][:, a * D:(a + 1) * D], attT[:, a * P:(a + 1) * P],
                                                    wT[:, 3, :], start=True, stop=True)
                        done.then_inc(s_in_psum, 1)
                    if e == 6:
                        pe.wait_ge(read[0], PER0 * n + 5)
                        norm_transpose(nc, c, s, n + 1, bank[0])
                pe.wait_ge(read[3], PER3 * n + E2 + 1)
                for a in range(TILES):
                    done = nc.tensor.matmul(bank[3][:, a * D:(a + 1) * D], combT[:, a * P:(a + 1) * P], c.b22[:, :],
                                            start=True, stop=True)
                done.then_inc(down_in_psum, 1)

        @block.scalar
        def _(act):
            act.wait_ge(c.w2_loaded, c.W2_ALL)
            nc.scalar.activation(c.beta[:, :], c.beta[:, :], ACT.Exp).then_inc(beta_exp, 1)
            norm_copy(nc, c, s, 0, bank[0], read[0])
            act.wait_ge(attention_ready, 1)
            with act.Fori(0, NSEQ) as n:
                route_exp(nc, r, n)
                act.wait_ge(qk_in_psum, n + 1)
                for i in range(2):
                    done = nc.scalar.activation(qk[:, i, :], bank[4][:, i * T:(i + 1) * T], ACT.Exp,
                                                bias=bcol[:, i:i + 1], scale=nbeta[:, 0:1])
                done.then_inc(read[4], 1)

                def gelu(e):
                    if e >= 2:
                        act.wait_ge(down_in_psum, PER3 * n + e - 1)
                    for b in range(2):
                        act.wait_ge(hidden_in_psum, 2 * E2 * n + 2 * e + b + 1)
                        for i in range(2):
                            k = 2 * b + i
                            done = nc.scalar.activation(hid[:, e % 2, k, :], bank[1 + b][:, i * T:(i + 1) * T],
                                                        ACT.Gelu_apprx_tanh, bias=c.b12[:, e, k:k + 1])
                        done.then_inc(read[1 + b], 1)

                for e in range(E2):
                    gelu(e)
                    if e == 5:
                        act.wait_ge(combT_in_psum, n + 1)
                        nc.scalar.activation(combT[:, :], bank[0][0:E2, 0:T], ACT.Copy).then_inc(read[0], 1)
                norm_copy(nc, c, s, n + 1, bank[0], read[0])
                act.wait_ge(acc_ready, n + 1)
                nc.scalar.activation(th_z[:, :, :], acc[:, :, :], ACT.Tanh, scale=0.5).then_inc(th_z_ready, 1)

        @block.gpsimd
        def _(pool):
            norm_power(nc, c, s, 0)
            with pool.Fori(0, NSEQ) as n:
                norm_power(nc, c, s, n + 1)

        @block.vector
        def _(dve):
            v = nc.vector
            v.memset(seen[:, :], 0.0)
            v.memset(c.ones[:, :], 1.0)
            dve.wait_ge(weights_turned, 1)
            v.tensor_copy(wT[:, :, :], bank[1][:, :].rearrange("p (i d) -> p i d", i=4))
            v.drain()
            for dst, src in ((proj, [wT[:, i, :] for i in range(3)]),
                             (brow, [c.w2[name][:, :] for name in ("bq", "bk", "bv")])):
                for i in range(2):
                    pair = src[i].rearrange("p (h o) -> p h o", o=2)
                    out = dst[:, i, :].rearrange("p (h o) -> p h o", o=2)
                    v.tensor_tensor(out[:, :, 0], pair[:, :, 0], pair[:, :, 1], ALU.subtract)
                    v.tensor_tensor(out[:, :, 1], pair[:, :, 1], pair[:, :, 0], ALU.subtract)
                pair = src[2].rearrange("p (h o) -> p h o", o=2)
                for i in range(2):
                    v.tensor_copy(dst[:, 2 + i, :].rearrange("p (h o) -> p h o", o=2), bcast(pair[:, :, i], 2))
            v.drain().then_inc(weights_copied, 1)
            dve.wait_ge(beta_exp, 1)
            v.tensor_scalar(nbeta[:, :], c.beta[:, :], -1.0, None, ALU.mult)
            v.drain()
            dve.wait_ge(biases_turned, 1)
            for i in range(4):
                col = bank[2][:, i * P:i * P + 1]
                if i < 2:
                    v.tensor_scalar(bcol[:, i:i + 1], col, nbeta[:, 0:1], None, ALU.mult)
                else:
                    v.tensor_copy(bcol[:, i:i + 1], col)
            v.drain().then_inc(attention_ready, 2)
            norm_stats(nc, c, s, 0)
            norm_apply(nc, c, s, 0, True)
            with dve.Fori(0, NSEQ) as n:
                dve.wait_ge(logits_in_psum, n + 1)
                route_shift(nc, r, bank[0][:, 0:TILES * E2].rearrange("p (a e) -> p a e", e=E2), read[0])
                route_best(nc, r, n)
                v.drain()
                for a in range(TILES):
                    v.tensor_scalar(mask[:, a, :], c.iota8[:, :], r.place[:, a, 0:1], None, ALU.is_equal)
                v.drain().then_inc(mask_ready, 1)
                dve.wait_ge(read[4], n + 2)
                v.tensor_scalar(qk[:, :, :], qk[:, :, :], 1.0, None, ALU.add)
                v.drain()
                v.reciprocal(qk[:, :, :], qk[:, :, :])
                v.drain()
                dve.wait_ge(v_in_psum, n + 1)
                for i in range(2):
                    done = v.scalar_tensor_tensor(out=kvk[:, i, :], in0=bank[5][:, i * T:(i + 1) * T],
                                                  scalar=bcol[:, 2 + i:3 + i], in1=qk[:, 1, :],
                                                  op0=ALU.add, op1=ALU.mult)
                done.then_inc(read[5], 1)
                v.drain()
                for i in range(3):
                    v.tensor_tensor_scan(cum[:, i, :], c.ones[:, :], kvk[:, i, :] if i < 2 else qk[:, 1, :], 0.0,
                                         ALU.mult, ALU.add)
                v.drain()
                dve.wait_ge(count_in_psum, n + 1)
                count = bank[0][:, 0:TILES * E2].rearrange("p (a e) -> p a e", e=E2)
                v.tensor_tensor(kept[:, :, :], count, seen[:, :].unsqueeze(1).to_broadcast([P, TILES, E2]), ALU.add)
                v.drain()
                v.tensor_tensor(seen[:, :], seen[:, :], bank[0][:, 2 * E2:3 * E2], ALU.add).then_inc(read[0], 1)
                v.tensor_scalar(kept[:, :, :], kept[:, :, :], float(CAP2), None, ALU.is_le)
                v.drain()
                v.tensor_tensor(kept[:, :, :], kept[:, :, :], mask[:, :, :], ALU.mult)
                v.drain()
                v.tensor_tensor(comb[:, :, :], kept[:, :, :], r.probs[:, :, :], ALU.mult)
                v.drain().then_inc(comb_ready, 1)
                for i in range(3):
                    v.tensor_tensor(qcum[:, i, :], cum[:, i, :], qk[:, 0, :], ALU.mult)
                v.drain().then_inc(qcum_ready, 1)
                norm_stats(nc, c, s, n + 1)

                def add_expert(e):
                    dve.wait_ge(down_in_psum, PER3 * n + e + 1)
                    for a in range(TILES):
                        rows = bank[3][:, a * D:(a + 1) * D]
                        if e == 0:
                            done = v.tensor_scalar(acc[:, a, :], rows, comb[:, a, 0:1], None, ALU.mult)
                        else:
                            done = v.scalar_tensor_tensor(out=acc[:, a, :], in0=rows, scalar=comb[:, a, e:e + 1],
                                                          in1=acc[:, a, :], op0=ALU.mult, op1=ALU.add)
                    done.then_inc(read[3], 1)

                for e in range(E2):
                    add_expert(e)
                    if e == 2:
                        norm_apply(nc, c, s, n + 1, False)
                    if e == 3:
                        dve.wait_ge(att_in_psum, n + 1)
                        v.reciprocal(rden[:, :], bank[6][:, T:2 * T])
                        v.drain()
                        v.tensor_tensor(attT[:, :], bank[6][:, 0:T], rden[:, :], ALU.mult).then_inc(read[6], 1)
                        v.drain().then_inc(attT_ready, 1)
                    if e == 5:
                        dve.wait_ge(s_in_psum, n + 1)
                        v.tensor_tensor(s_out[:, :, :], bank[0][:, 0:TILES * D].rearrange("p (a d) -> p a d", d=D),
                                        c.w2["bo"][:, :].unsqueeze(1).to_broadcast([P, TILES, D]), ALU.add)\
                            .then_inc(read[0], 1)
                dve.wait_ge(down_in_psum, PER3 * n + PER3)
                v.tensor_tensor(acc[:, :, :], bank[3][:, 0:TILES * D].rearrange("p (a d) -> p a d", d=D),
                                acc[:, :, :], ALU.add).then_inc(read[3], 1)
                v.drain().then_inc(acc_ready, 1)
                dve.wait_ge(th_z_ready, n + 1)
                close_layer(nc, c, n, s_out[:, :, :], acc[:, :, :], th_z[:, :, :], u[:, :, :])


def layer3_weights(nc, ctx, A, c):
    def sb(name, shape):
        return ctx.enter_context(nc.sbuf_tensor("w3_" + name, shape, F32))

    w = c.w3 = Core()
    w.in_proj = sb("in_proj", [P, 2 * CI, D])
    w.x_proj = sb("x_proj", [RANK + 2 * NS, DI])
    w.dt_proj = sb("dt_proj", [P, CI, RANK])
    w.out_proj = sb("out_proj", [P, DI])
    w.conv, w.conv_b = sb("conv", [P, CI, DCONV]), sb("conv_b", [P, CI])
    w.dt_b, w.A_log, w.skip = sb("dt_b", [P, CI]), sb("A_log", [P, CI, NS]), sb("skip", [P, CI])
    w.qkv, w.bqkv = sb("qkv", [P, 3, D]), sb("bqkv", [P, 3, D])
    w.o, w.bo = sb("o", [P, D]), sb("bo", [P, D])
    w.g, w.bg = sb("g", [P, E3]), sb("bg", [P, E3])
    w.w1, w.b1 = sb("w1", [P, E3, F3]), sb("b1", [P, E3, F3 // P])
    w.w2, w.b2 = sb("w2", [P, E3, F3 // P, D]), sb("b2", [E3, D])
    w.g1, w.be1, w.g2, w.be2 = (sb(name, [P, D]) for name in ("g1", "be1", "g2", "be2"))
    c.w3_loaded = ctx.enter_context(nc.semaphore("w3_loaded"))
    a, f = "L3_attn_", "L3_ffn_"
    c.w3_loads = [
        (w.in_proj[:, :, :], A[a + "in_proj_w"].rearrange("(c p) d -> p c d", p=P)),
        (w.x_proj[:, :], A[a + "x_proj_w"]),
        (w.dt_proj[:, :, :], A[a + "dt_proj_w"].rearrange("(c p) r -> p c r", p=P)),
        (w.out_proj[:, :], A[a + "out_proj_w"]),
        (w.conv[:, :, :], A[a + "conv_w"].rearrange("(c p) k -> p c k", p=P)),
        (w.conv_b[:, :], A[a + "conv_b"].rearrange("(c p) -> p c", p=P)),
        (w.dt_b[:, :], A[a + "dt_proj_b"].rearrange("(c p) -> p c", p=P)),
        (w.A_log[:, :, :], A[a + "A_log"].rearrange("(c p) s -> p c s", p=P)),
        (w.skip[:, :], A[a + "D"].rearrange("(c p) -> p c", p=P)),
        (w.o[:, :], A[f + "Wo"]), (w.g[:, :], A[f + "Wg"]),
        (w.w1[:, :, :], A[f + "W1"].rearrange("e d f -> d e f")),
        (w.b1[:, :, :], A[f + "b1"].rearrange("e (k p) -> p e k", p=P)),
        (w.w2[:, :, :, :], A[f + "W2"].rearrange("e (k p) d -> p e k d", p=P)),
        (w.b2[:, :], A[f + "b2"])]
    for i, name in enumerate("qkv"):
        c.w3_loads += [(w.qkv[:, i, :], A[f + "W" + name]),
                       (w.bqkv[:, i, :], A[f + "b" + name].partition_broadcast(P))]
    for dst, name in ((w.bo, "bo"), (w.bg, "bg"), (w.g1, "g1"), (w.be1, "be1"), (w.g2, "g2"), (w.be2, "be2")):
        c.w3_loads.append((dst[:, :], A[f + name].partition_broadcast(P)))
    c.W3_ALL = 16 * len(c.w3_loads)


def layer3(nc, c):
    w = c.w3
    with ExitStack() as ctx:
        def sb(name, shape, dtype=F32):
            return ctx.enter_context(nc.sbuf_tensor("d3_" + name, shape, dtype))

        def sem(name):
            return layer_semaphore(nc, "l3_" + name)

        bank = [ctx.enter_context(nc.psum_tensor(f"l3_bank{i}", [P, 512], F32)) for i in range(8)]
        KF = F3 // P
        PAIRS = NS // 2
        XD = RANK + 2 * NS
        RP = 4
        in_projT = sb("in_projT", [P, 2 * CI, P])
        x_projT = sb("x_projT", [P, CI, XD])
        dt_projT = sb("dt_projT", [RANK, CI, P])
        out_projT = sb("out_projT", [P, CI, D])
        negA = sb("negA", [P, CI, NS])
        nconv_b = sb("nconv_b", [P, CI])
        upad = sb("upad", [P, CI, DCONV - 1 + T])
        z = sb("z", [P, CI, T])
        zg = sb("zg", [P, CI, T])
        xs = sb("xs", [P, CI, T])
        tmp = sb("tmp", [P, CI, T])
        xdbl = sb("xdbl", [XD, T])
        dv = sb("dv", [P, CI, T])
        dneg = sb("dneg", [P, CI, T])
        delta = sb("delta", [P, CI, T])
        du = sb("du", [P, CI, T])
        dA = [c.w12[:, :, :].rearrange("p e f -> p (e f)").rearrange("p (s t) -> p s t", t=T),
              c.w22[:, :, :, :].rearrange("p e k d -> p (e k d)").rearrange("p (s t) -> p s t", t=T)]
        st = [sb(f"state{i}", [P, NS, T]) for i in range(CI)]
        qkv = sb("qkv", [P, TILES, 3 * D])
        rot = sb("rot", [P, TILES, 2, H3, 2, HD3 // 2])
        t1, t2, t3, t4 = (sb(f"t{i}", [P, 2, H3, HD3 // 2]) for i in range(1, 5))
        qT = sb("qT", [P, GR, T])
        kT = sb("kT", [P, T])
        scale_mask = sb("scale_mask", [P, GR])
        probs = sb("probs", [P, RP, TILES, T])
        nmax = sb("nmax", [P, RP, TILES])
        total = sb("total", [P, TILES, H3])
        recip = sb("recip", [P, TILES, H3])
        pT = sb("pT", [P, 2, 4 * P])
        y = sb("y", [P, TILES, D])
        yT = sb("yT", [P, T])
        x1 = sb("x1", [P, TILES, D])
        x1T = sb("x1T", [P, T])
        rows = sb("rows", [P, TILES, D])
        stats = sb("stats", [P, TILES, 6])
        meanvar = sb("meanvar", [P, TILES, 2])
        var_eps = sb("var_eps", [P, TILES])
        rstd = sb("rstd", [P, TILES])
        r = RouteBuffers(sb, sem)
        psum2 = sb("psum2", [P, TILES])
        first = sb("first", [P, TILES])
        second = sb("second", [P, TILES])
        comb = sb("comb", [P, TILES, E3])
        comb2 = sb("comb2", [P, TILES, E3])
        combT = sb("combT", [E3, T])
        hid = sb("hid", [P, 2, KF, T])
        acc = sb("acc", [P, TILES, D])
        ym = sb("ym", [P, CI, T])
        s_out = sb("s_out", [P, TILES, D])
        th_z = sb("th_z", [P, TILES, D])
        u = sb("u", [P, TILES, D])

        s = NormSems(sem, "n")
        read = [sem(f"bank{i}_read") for i in range(8)]
        PER0 = 12
        PER12 = 16
        PER34 = 10
        PER56 = 8
        PER7 = 10
        weights_turned = sem("weights_turned")
        weights_ready = sem("weights_ready")
        a_exp = sem("a_exp")
        qkv_in_psum = sem("qkv_in_psum")
        u_in_psum = sem("u_in_psum")
        z_in_psum = sem("z_in_psum")
        z_exp = sem("z_exp")
        rot_ready = sem("rot_ready")
        qkT_in_psum = sem("qkT_in_psum")
        scores_in_psum = sem("scores_in_psum")
        max_ready = sem("max_ready")
        pT_in_psum = sem("pT_in_psum")
        head_done = sem("head_done")
        conv_ready = sem("conv_ready")
        conv_exp = sem("conv_exp")
        xs_ready = sem("xs_ready")
        xdbl_in_psum = sem("xdbl_in_psum")
        dt_in_psum = sem("dt_in_psum")
        dneg_ready = sem("dneg_ready")
        dlog_ready = sem("dlog_ready")
        delta_ready = sem("delta_ready")
        dA_ready = sem("dA_ready")
        bc_in_psum = sem("bc_in_psum")
        cstate_ready = sem("cstate_ready")
        sum_in_psum = sem("sum_in_psum")
        y_ready = sem("y_ready")
        yT_in_psum = sem("yT_in_psum")
        o_in_psum = sem("o_in_psum")
        var_ready = sem("var_ready")
        rstd_ready = sem("rstd_ready")
        x1_ready = sem("x1_ready")
        x1T_in_psum = sem("x1T_in_psum")
        logits_in_psum = sem("logits_in_psum")
        comb_ready = sem("comb_ready")
        combT_in_psum = sem("combT_in_psum")
        hidden_in_psum = sem("hidden_in_psum")
        down_in_psum = sem("down_in_psum")
        ym_ready = sem("ym_ready")
        s_in_psum = sem("s_in_psum")
        gate_ready = sem("gate_ready")
        th_z_ready = sem("th_z_ready")

        block = ctx.enter_context(nc.Block())

        @block.tensor
        def _(pe):
            for i in range(1, 8):
                pe.sem_inc(read[i], 1)
            pe.wait_ge(c.w3_loaded, c.W3_ALL)
            for i in range(2 * CI):
                nc.tensor.transpose(bank[1][:, i * P:(i + 1) * P], w.in_proj[:, i, :], c.ident[:, :])
            for i in range(CI):
                nc.tensor.transpose(bank[2][:, i * XD:(i + 1) * XD], w.x_proj[:, i * P:(i + 1) * P],
                                    c.ident[0:XD, 0:XD])
                nc.tensor.transpose(bank[3][0:RANK, i * P:(i + 1) * P], w.dt_proj[:, i, :], c.ident[:, :])
                done = nc.tensor.transpose(bank[4][:, i * D:(i + 1) * D], w.out_proj[:, i * P:(i + 1) * P],
                                           c.ident[:, :])
            done.then_inc(weights_turned, 1)
            norm_transpose(nc, c, s, 0, bank[0])
            pe.wait_ge(weights_ready, 1)
            with pe.Fori(0, NSEQ) as n:
                pe.wait_ge(read[0], PER0 * n + 1)
                wqkv = w.qkv[:, :, :].rearrange("p i d -> p (i d)")
                nc.tensor.matmul(bank[0][:, 0:3 * D], c.xnT[:, 0:P], wqkv, start=True, stop=True)\
                    .then_inc(qkv_in_psum, 1)
                pe.wait_ge(read[3], PER34 * n + 1)
                nc.tensor.matmul(bank[3][:, 0:3 * D], c.xnT[:, P:T], wqkv, start=True, stop=True)\
                    .then_inc(qkv_in_psum, 1)
                pe.wait_ge(read[4], PER34 * n + 1)
                for i in range(CI):
                    done = nc.tensor.matmul(bank[4][:, i * T:(i + 1) * T], in_projT[:, i, :], c.xnT[:, :],
                                            start=True, stop=True)
                done.then_inc(u_in_psum, 1)
                pe.wait_ge(read[0], PER0 * n + 2)
                for i in range(CI):
                    done = nc.tensor.matmul(bank[0][:, i * T:(i + 1) * T], in_projT[:, CI + i, :], c.xnT[:, :],
                                            start=True, stop=True)
                done.then_inc(z_in_psum, 1)

                def scores(h):
                    b, part = 1 + h % 2, slice(ROWS * (h // GR), ROWS * (h // GR) + ROWS)
                    pe.wait_ge(read[b], PER12 * n + h // 2 + 1)
                    for a in range(TILES):
                        done = nc.tensor.matmul(bank[b][:, a * T:(a + 1) * T], qT[part, h % GR, a * P:(a + 1) * P],
                                                kT[part, :], start=True, stop=True)
                    done.then_inc(scores_in_psum, 1)

                def turn_probs(h):
                    b = 3 + h % 2
                    pe.wait_ge(read[1 + h % 2], PER12 * n + h // 2 + 2)
                    pe.wait_ge(read[b], PER34 * n + h // 2 + 2)
                    for a in range(TILES):
                        for j in range(2):
                            done = nc.tensor.transpose(bank[b][:, (2 * a + j) * P:(2 * a + j + 1) * P],
                                                       probs[:, h % RP, a, j * P:(j + 1) * P], c.ident[:, :])
                    done.then_inc(pT_in_psum, 1)

                def head_out(h):
                    if h == 0:
                        pe.wait_ge(read[7], PER7 * n + 1)
                    pe.wait_ge(read[3 + h % 2], PER34 * n + h // 2 + 3)
                    for a in range(TILES):
                        for j in range(2):
                            done = nc.tensor.matmul(bank[7][:, a * D + h * HD3:a * D + (h + 1) * HD3],
                                                    pT[:, h % 2, (2 * a + j) * P:(2 * a + j + 1) * P],
                                                    qkv[:, j, 2 * D + h * HD3:2 * D + (h + 1) * HD3],
                                                    start=(j == 0), stop=(j == 1))
                    done.then_inc(head_done, 1)

                def spread(j):
                    b = 5 + j % 2
                    pe.wait_ge(read[b], PER56 * n + j // 2 + 1)
                    for i in range(2):
                        row = RANK + 2 * j + i
                        done = nc.tensor.matmul(bank[b][:, i * T:(i + 1) * T],
                                                c.ident[0:XD, row:row + 1].to_broadcast([XD, P]), xdbl[:, :],
                                                start=True, stop=True)
                    done.then_inc(bc_in_psum, 1)

                pe.wait_ge(rot_ready, n + 1)
                pe.wait_ge(read[0], PER0 * n + 3)
                for a in range(TILES):
                    for i in range(2):
                        done = nc.tensor.transpose(bank[0][:, i * T + a * P:i * T + (a + 1) * P],
                                                   rot[:, a, i, :, :, :].rearrange("p h o k -> p (h o k)"),
                                                   c.ident[:, :])
                done.then_inc(qkT_in_psum, 1)
                pe.wait_ge(read[0], PER0 * n + 4)
                for k in range(H3 + 2):
                    if k < H3:
                        scores(k)
                    if 1 <= k <= H3:
                        turn_probs(k - 1)
                    if k >= 2:
                        head_out(k - 2)
                    if k == 5:
                        pe.wait_ge(xs_ready, n + 1)
                        for i in range(CI):
                            done = nc.tensor.matmul(bank[0][0:XD, 0:T], x_projT[:, i, :], xs[:, i, :],
                                                    start=(i == 0), stop=(i == CI - 1))
                        done.then_inc(xdbl_in_psum, 1)
                    if k == 7:
                        pe.wait_ge(read[0], PER0 * n + 5)
                        for i in range(CI):
                            done = nc.tensor.matmul(bank[0][:, i * T:(i + 1) * T], dt_projT[:, i, :], xdbl[0:RANK, :],
                                                    start=True, stop=True)
                        done.then_inc(dt_in_psum, 1)
                    if 12 <= k < H3:
                        spread(2 * (k - 12))
                        spread(2 * (k - 12) + 1)
                pe.wait_ge(y_ready, n + 1)
                pe.wait_ge(read[0], PER0 * n + 6)
                for a in range(TILES):
                    done = nc.tensor.transpose(bank[0][:, a * P:(a + 1) * P], y[:, a, :], c.ident[:, :])
                done.then_inc(yT_in_psum, 1)
                pe.wait_ge(read[0], PER0 * n + 7)
                for a in range(TILES):
                    done = nc.tensor.matmul(bank[0][:, a * D:(a + 1) * D], yT[:, a * P:(a + 1) * P], w.o[:, :],
                                            start=True, stop=True)
                done.then_inc(o_in_psum, 1)
                spread(PAIRS)
                spread(PAIRS + 1)
                pe.wait_ge(x1_ready, n + 1)
                pe.wait_ge(read[0], PER0 * n + 8)
                for a in range(TILES):
                    done = nc.tensor.transpose(bank[0][:, a * P:(a + 1) * P], x1[:, a, :], c.ident[:, :])
                done.then_inc(x1T_in_psum, 1)
                pe.wait_ge(read[0], PER0 * n + 9)
                for a in range(TILES):
                    done = nc.tensor.matmul(bank[0][:, a * E3:(a + 1) * E3], x1T[:, a * P:(a + 1) * P], w.g[:, :],
                                            start=True, stop=True)
                done.then_inc(logits_in_psum, 1)

                def up(e):
                    for b in range(2):
                        pe.wait_ge(read[1 + b], PER12 * n + 8 + e + 1)
                        for i in range(2):
                            k = 2 * b + i
                            done = nc.tensor.matmul(bank[1 + b][:, i * T:(i + 1) * T],
                                                    w.w1[:, e, k * P:(k + 1) * P], x1T[:, :], start=True, stop=True)
                        done.then_inc(hidden_in_psum, 1)

                def down(e):
                    pe.wait_ge(read[1], PER12 * n + 8 + e + 2)
                    pe.wait_ge(read[2], PER12 * n + 8 + e + 2)
                    pe.wait_ge(read[7], PER7 * n + e + 2)
                    for a in range(TILES):
                        for k in range(KF):
                            done = nc.tensor.matmul(bank[7][:, a * D:(a + 1) * D],
                                                    hid[:, e % 2, k, a * P:(a + 1) * P], w.w2[:, e, k, :],
                                                    start=(k == 0), stop=(k == KF - 1))
                    done.then_inc(down_in_psum, 1)

                def add_states(p):
                    if p == 0:
                        for i in range(CI):
                            pe.wait_ge(read[3 + i], PER34 * n + 10)
                    pe.wait_ge(cstate_ready, PAIRS * n + p + 1)
                    for i in range(CI):
                        for j in range(2):
                            done = nc.tensor.matmul(bank[3 + i][:, 0:T], c.ident[:, :], st[i][:, 2 * p + j, :],
                                                    start=(p == 0 and j == 0), stop=(p == PAIRS - 1 and j == 1))
                    done.then_inc(sum_in_psum, 1)

                up(0)
                up(1)
                for e in range(E3):
                    down(e)
                    if e + 2 < E3:
                        up(e + 2)
                    if e >= 1:
                        add_states(e - 1)
                    if e + 2 < PAIRS:
                        spread(PAIRS + e + 2)
                    if e == 3:
                        pe.wait_ge(comb_ready, n + 1)
                        pe.wait_ge(read[0], PER0 * n + 10)
                        for a in range(TILES):
                            done = nc.tensor.transpose(bank[0][0:E3, a * P:(a + 1) * P], comb[:, a, :], c.ident[:, :])
                        done.then_inc(combT_in_psum, 1)
                add_states(PAIRS - 1)
                pe.wait_ge(read[0], PER0 * n + 11)
                pe.wait_ge(read[7], PER7 * n + 10)
                for a in range(TILES):
                    done = nc.tensor.matmul(bank[7][:, a * D:(a + 1) * D], combT[:, a * P:(a + 1) * P], w.b2[:, :],
                                            start=True, stop=True)
                done.then_inc(down_in_psum, 1)
                pe.wait_ge(ym_ready, n + 1)
                for a in range(TILES):
                    for i in range(CI):
                        done = nc.tensor.matmul(bank[0][:, a * D:(a + 1) * D], ym[:, i, a * P:(a + 1) * P],
                                                out_projT[:, i, :], start=(i == 0), stop=(i == CI - 1))
                done.then_inc(s_in_psum, 1)
                pe.wait_ge(read[0], PER0 * n + 12)
                norm_transpose(nc, c, s, n + 1, bank[0])

        @block.scalar
        def _(act):
            v = nc.scalar
            act.wait_ge(c.w3_loaded, c.W3_ALL)
            v.activation(negA[:, :, :], w.A_log[:, :, :], ACT.Exp).then_inc(a_exp, 1)
            norm_copy(nc, c, s, 0, bank[0], read[0])
            act.wait_ge(weights_ready, 1)
            with act.Fori(0, NSEQ) as n:
                def exp_scores(h):
                    act.wait_ge(max_ready, H3 * n + h + 1)
                    for a in range(TILES):
                        done = v.activation(probs[:, h % RP, a, :], bank[1 + h % 2][:, a * T:(a + 1) * T], ACT.Exp,
                                            bias=nmax[:, h % RP, a:a + 1], accum_out=total[:, a, h:h + 1])
                    done.then_inc(read[1 + h % 2], 1)

                def copy_pT(h):
                    if h >= 2:
                        act.wait_ge(head_done, H3 * n + h - 1)
                    act.wait_ge(pT_in_psum, H3 * n + h + 1)
                    v.activation(pT[:, h % 2, :], bank[3 + h % 2][:, :], ACT.Copy).then_inc(read[3 + h % 2], 1)

                def log_part(j):
                    act.wait_ge(dneg_ready, 2 * n + j + 1)
                    v.activation(dneg[:, :, :], dneg[:, :, :], ACT.Exp)
                    v.drain()
                    v.activation(dneg[:, :, :], dneg[:, :, :], ACT.Ln, bias=1.0).then_inc(dlog_ready, 1)

                def decay(g, i):
                    for m in range(SG * g, SG * g + SG):
                        done = v.activation(dA[i][:, m, 1:T], delta[:, i, 1:T], ACT.Exp, scale=negA[:, i, m:m + 1])
                    done.then_inc(dA_ready, 1)

                act.wait_ge(u_in_psum, n + 1)
                v.activation(upad[:, :, DCONV - 1:], bank[4][:, :].rearrange("p (i t) -> p i t", i=CI), ACT.Copy)\
                    .then_inc(read[4], 1)
                act.wait_ge(z_in_psum, n + 1)
                zp = bank[0][:, :].rearrange("p (i t) -> p i t", i=CI)
                v.activation(z[:, :, :], zp, ACT.Copy)
                v.activation(zg[:, :, :], zp, ACT.Exp, scale=-1.0).then_inc(read[0], 1)
                act.wait_ge(qkT_in_psum, n + 1)
                v.activation(kT[:, :], bank[0][:, T:2 * T], ACT.Copy)
                for i in range(GR):
                    done = v.activation(qT[:, i, :], bank[0][:, 0:T], ACT.Copy, scale=scale_mask[:, i:i + 1])
                done.then_inc(read[0], 1)
                for k in range(H3 + 1):
                    if k < H3:
                        exp_scores(k)
                    if k >= 1:
                        copy_pT(k - 1)
                    if k == 3:
                        act.wait_ge(conv_ready, n + 1)
                        for i in range(CI):
                            done = v.activation(tmp[:, i, :], xs[:, i, :], ACT.Exp, bias=nconv_b[:, i:i + 1],
                                                scale=-1.0)
                        done.then_inc(conv_exp, 1)
                    if k == 6:
                        act.wait_ge(xdbl_in_psum, n + 1)
                        v.activation(xdbl[:, :], bank[0][0:XD, 0:T], ACT.Copy).then_inc(read[0], 1)
                    if k == 9:
                        log_part(0)
                    if k == 11:
                        log_part(1)
                    if k == 12:
                        act.wait_ge(delta_ready, n + 1)
                    if 12 <= k < H3:
                        decay((k - 12) // 2, (k - 12) % 2)
                act.wait_ge(yT_in_psum, n + 1)
                v.activation(yT[:, :], bank[0][:, 0:T], ACT.Copy).then_inc(read[0], 1)
                for g in (2, 3):
                    for i in range(CI):
                        decay(g, i)
                act.wait_ge(x1T_in_psum, n + 1)
                v.activation(x1T[:, :], bank[0][:, 0:T], ACT.Copy).then_inc(read[0], 1)
                route_exp(nc, r, n)

                def gelu(e):
                    if e >= 2:
                        act.wait_ge(down_in_psum, 9 * n + e - 1)
                    for b in range(2):
                        act.wait_ge(hidden_in_psum, 2 * E3 * n + 2 * e + b + 1)
                        for i in range(2):
                            k = 2 * b + i
                            done = v.activation(hid[:, e % 2, k, :], bank[1 + b][:, i * T:(i + 1) * T], ACT.Gelu,
                                                bias=w.b1[:, e, k:k + 1])
                        done.then_inc(read[1 + b], 1)

                for e in range(E3):
                    gelu(e)
                    if e == 5:
                        act.wait_ge(combT_in_psum, n + 1)
                        v.activation(combT[:, :], bank[0][0:E3, 0:T], ACT.Copy).then_inc(read[0], 1)
                act.wait_ge(gate_ready, n + 1)
                v.activation(th_z[:, :, :], rows[:, :, :], ACT.Tanh, scale=0.5).then_inc(th_z_ready, 1)
                norm_copy(nc, c, s, n + 1, bank[0], read[0])

        @block.gpsimd
        def _(pool):
            def inner_power(count):
                pool.wait_ge(var_ready, count)
                nc.gpsimd.tensor_tensor(rstd[:, :], var_eps[:, :], c.minus_half[:, 0:TILES], ALU.pow)\
                    .then_inc(rstd_ready, 1)

            norm_power(nc, c, s, 0)
            with pool.Fori(0, NSEQ) as n:
                inner_power(2 * n + 1)
                norm_power(nc, c, s, n + 1)
                inner_power(2 * n + 2)

        @block.vector
        def _(dve):
            v = nc.vector
            for i in range(CI):
                v.memset(dA[i][:, :, 0:1], 0.0)
            v.memset(upad[:, :, 0:DCONV - 1], 0.0)
            dve.wait_ge(c.w3_loaded, c.W3_ALL)
            v.tensor_scalar(nconv_b[:, :], w.conv_b[:, :], -1.0, None, ALU.mult)
            v.tensor_scalar(scale_mask[:, :], c.row_mask[:, :], float(HD3) ** -0.5, None, ALU.mult)
            dve.wait_ge(a_exp, 1)
            v.tensor_scalar(negA[:, :, :], negA[:, :, :], -1.0, None, ALU.mult)
            dve.wait_ge(weights_turned, 1)
            v.tensor_copy(in_projT[:, :, :], bank[1][:, :].rearrange("p (i d) -> p i d", d=P))
            v.tensor_copy(x_projT[:, :, :], bank[2][:, 0:CI * XD].rearrange("p (i d) -> p i d", d=XD))
            v.tensor_copy(dt_projT[:, :, :], bank[3][0:RANK, 0:DI].rearrange("p (i d) -> p i d", d=P))
            v.tensor_copy(out_projT[:, :, :], bank[4][:, 0:CI * D].rearrange("p (i d) -> p i d", d=D))
            v.drain().then_inc(weights_ready, 2)
            norm_stats(nc, c, s, 0)
            norm_apply(nc, c, s, 0, True)
            with dve.Fori(0, NSEQ) as n:
                bq = w.bqkv[:, :, :].rearrange("p i d -> p (i d)")
                for a in range(TILES):
                    dve.wait_ge(qkv_in_psum, TILES * n + a + 1)
                    b = (0, 3)[a]
                    v.tensor_tensor(qkv[:, a, :], bank[b][:, 0:3 * D], bq, ALU.add).then_inc(read[b], 1)
                v.drain()
                for a in range(TILES):
                    for i in range(2):
                        part = qkv[:, a, i * D:(i + 1) * D].rearrange("p (h o k) -> p h o k", h=H3, o=2)
                        lo, hi = part[:, :, 0, :], part[:, :, 1, :]
                        cos = c.cos1[:, a, i * D // 2:(i + 1) * D // 2].rearrange("p (h k) -> p h k", h=H3)
                        sin = c.sin1[:, a, i * D // 2:(i + 1) * D // 2].rearrange("p (h k) -> p h k", h=H3)
                        v.tensor_tensor(t1[:, i], lo, cos, ALU.mult)
                        v.tensor_tensor(t2[:, i], hi, sin, ALU.mult)
                        v.tensor_tensor(t3[:, i], lo, sin, ALU.mult)
                        v.tensor_tensor(t4[:, i], hi, cos, ALU.mult)
                    v.drain()
                    v.tensor_tensor(rot[:, a, :, :, 0, :], t1[:, :, :, :], t2[:, :, :, :], ALU.subtract)
                    v.tensor_tensor(rot[:, a, :, :, 1, :], t3[:, :, :, :], t4[:, :, :, :], ALU.add)
                    done = v.drain()
                done.then_inc(rot_ready, 1)

                def head_max(h):
                    dve.wait_ge(scores_in_psum, H3 * n + h + 1)
                    v.tensor_reduce(nmax[:, h % RP, :], bank[1 + h % 2][:, :].rearrange("p (a t) -> p a t", a=TILES),
                                    AX, ALU.max, negate=True).then_inc(max_ready, 1)

                def conv():
                    for i in range(CI):
                        for k in range(DCONV):
                            src = upad[:, i, k:k + T]
                            if k == 0:
                                v.tensor_scalar(xs[:, i, :], src, w.conv[:, i, 0:1], None, ALU.mult)
                            else:
                                v.scalar_tensor_tensor(out=xs[:, i, :], in0=src, scalar=w.conv[:, i, k:k + 1],
                                                       in1=xs[:, i, :], op0=ALU.mult, op1=ALU.add)
                            v.drain()

                def softplus_arg(src, j):
                    for i in range(CI):
                        done = v.tensor_scalar(dv[:, i, :], src[:, i, :], w.dt_b[:, i:i + 1], None, ALU.add)
                    if j == 0:
                        done.then_inc(read[0], 1)
                    v.drain()
                    v.scalar_tensor_tensor(out=dneg[:, :, :], in0=dv[:, :, :], scalar=-1.0, in1=dv[:, :, :],
                                           op0=ALU.mult, op1=ALU.min).then_inc(dneg_ready, 1)

                def softplus_sum(j):
                    dve.wait_ge(dlog_ready, 2 * n + j + 1)
                    v.scalar_tensor_tensor(out=delta[:, :, :], in0=dv[:, :, :], scalar=0.0, in1=dneg[:, :, :],
                                           op0=ALU.max, op1=ALU.add)
                    v.drain()

                def silu_from_exp(out, x, e):
                    v.tensor_scalar(e, e, 1.0, None, ALU.add)
                    v.drain()
                    v.reciprocal(e, e)
                    v.drain()
                    v.tensor_tensor(out, x, e, ALU.mult)

                def state_input(p):
                    dve.wait_ge(bc_in_psum, 2 * PAIRS * n + p + 1)
                    b = bank[5 + p % 2][:, :].rearrange("p (m t) -> p m t", m=2)
                    for i in range(CI):
                        done = v.tensor_tensor(st[i][:, 2 * p:2 * p + 2, :], b,
                                               du[:, i, :].unsqueeze(1).to_broadcast([P, 2, T]), ALU.mult)
                    done.then_inc(read[5 + p % 2], 1)

                def scan(g, i):
                    dve.wait_ge(dA_ready, 2 * (NS // SG) * n + 2 * g + i + 1)
                    group = st[i][:, SG * g:SG * (g + 1), :].rearrange("p m t -> p (m t)")
                    v.tensor_tensor_scan(group, dA[i][:, SG * g:SG * (g + 1), :].rearrange("p m t -> p (m t)"),
                                         group, 0.0, ALU.mult, ALU.add)

                def times_c(p):
                    dve.wait_ge(bc_in_psum, 2 * PAIRS * n + PAIRS + p + 1)
                    b = bank[5 + p % 2][:, :].rearrange("p (m t) -> p m t", m=2)
                    for i in range(CI):
                        done = v.tensor_tensor(st[i][:, 2 * p:2 * p + 2, :], st[i][:, 2 * p:2 * p + 2, :], b, ALU.mult)
                    done.then_inc(read[5 + p % 2], 1)
                    v.drain().then_inc(cstate_ready, 1)

                def inner_stats():
                    for a in range(TILES):
                        v.bn_stats(stats[:, a, :], rows[:, a, :])
                    v.drain()
                    for a in range(TILES):
                        v.bn_aggr(meanvar[:, a, :], stats[:, a, :])
                    v.drain()
                    v.tensor_scalar(var_eps[:, :], meanvar[:, :, 1], LN_EPS, None, ALU.add).then_inc(var_ready, 1)

                def inner_apply(out, weight, bias, count):
                    dve.wait_ge(rstd_ready, count)
                    for a in range(TILES):
                        v.tensor_scalar(rows[:, a, :], rows[:, a, :], meanvar[:, a, 0:1], rstd[:, a:a + 1],
                                        ALU.subtract, ALU.mult)
                    v.drain()
                    wide = [x[:, :].unsqueeze(1).to_broadcast([P, TILES, D]) for x in (weight, bias)]
                    v.tensor_tensor(rows[:, :, :], rows[:, :, :], wide[0], ALU.mult)
                    v.drain()
                    v.tensor_tensor(out, rows[:, :, :], wide[1], ALU.add)

                for k in range(H3):
                    head_max(k)
                    if k == 2:
                        conv()
                        v.drain().then_inc(conv_ready, 1)
                    if k == 4:
                        dve.wait_ge(conv_exp, n + 1)
                        for i in range(CI):
                            v.tensor_scalar(xs[:, i, :], xs[:, i, :], w.conv_b[:, i:i + 1], None, ALU.add)
                        v.drain()
                        silu_from_exp(xs[:, :, :], xs[:, :, :], tmp[:, :, :])
                        v.drain().then_inc(xs_ready, 1)
                    if k == 6:
                        silu_from_exp(zg[:, :, :], z[:, :, :], zg[:, :, :])
                    if k == 8:
                        dve.wait_ge(dt_in_psum, n + 1)
                        softplus_arg(bank[0][:, :].rearrange("p (i t) -> p i t", i=CI), 0)
                    if k == 10:
                        softplus_sum(0)
                        softplus_arg(delta, 1)
                    if k == 11:
                        softplus_sum(1)
                        v.drain().then_inc(delta_ready, 1)
                        v.tensor_tensor(du[:, :, :], delta[:, :, :], xs[:, :, :], ALU.mult)
                        v.drain()
                    if k >= 12:
                        state_input(2 * (k - 12))
                        state_input(2 * (k - 12) + 1)
                dve.wait_ge(read[2], PER12 * n + 9)
                v.reciprocal(recip[:, :, :], total[:, :, :])
                v.drain()
                dve.wait_ge(head_done, H3 * n + H3)
                v.tensor_tensor(y[:, :, :].rearrange("p a (h v) -> p (a h) v", v=HD3),
                                bank[7][:, 0:TILES * D].rearrange("p (g v) -> p g v", v=HD3),
                                bcast(recip[:, :, :].rearrange("p a h -> p (a h)"), HD3), ALU.mult)\
                    .then_inc(read[7], 1)
                v.drain().then_inc(y_ready, 1)
                scan(0, 0)
                dve.wait_ge(o_in_psum, n + 1)
                v.tensor_tensor(rows[:, :, :], bank[0][:, 0:TILES * D].rearrange("p (a d) -> p a d", d=D),
                                w.bo[:, :].unsqueeze(1).to_broadcast([P, TILES, D]), ALU.add).then_inc(read[0], 1)
                v.drain()
                v.tensor_tensor(rows[:, :, :], rows[:, :, :], c.xn[:, :, :], ALU.add)
                v.drain()
                inner_stats()
                scan(0, 1)
                inner_apply(x1[:, :, :], w.g1, w.be1, 2 * n + 1)
                v.drain().then_inc(x1_ready, 1)
                times_c(0)
                times_c(1)
                norm_stats(nc, c, s, n + 1)
                dve.wait_ge(logits_in_psum, n + 1)
                route_shift(nc, r, bank[0][:, 0:TILES * E3].rearrange("p (a e) -> p a e", e=E3), read[0],
                            w.bg[:, :].unsqueeze(1).to_broadcast([P, TILES, E3]))
                route_best(nc, r, n)
                v.tensor_tensor(psum2[:, :], r.best[:, :, 0], r.best[:, :, 1], ALU.add)
                v.drain()
                v.reciprocal(psum2[:, :], psum2[:, :])
                v.drain()
                v.tensor_tensor(first[:, :], r.best[:, :, 0], psum2[:, :], ALU.mult)
                v.tensor_tensor(second[:, :], r.best[:, :, 1], psum2[:, :], ALU.mult)
                v.drain()
                for a in range(TILES):
                    v.tensor_scalar(comb[:, a, :], c.iota8[:, :], r.place[:, a, 0:1], first[:, a:a + 1],
                                    ALU.is_equal, ALU.mult)
                    v.tensor_scalar(comb2[:, a, :], c.iota8[:, :], r.place[:, a, 1:2], second[:, a:a + 1],
                                    ALU.is_equal, ALU.mult)
                v.drain()
                v.tensor_tensor(comb[:, :, :], comb[:, :, :], comb2[:, :, :], ALU.add)
                v.drain().then_inc(comb_ready, 1)
                for e in range(E3):
                    if e < 6:
                        scan(1 + e // 2, e % 2)
                    if e == 1:
                        norm_apply(nc, c, s, n + 1, False)
                    if e % 2 == 1 and e < 6:
                        v.drain()
                        times_c(e + 1)
                        times_c(e + 2)
                    dve.wait_ge(down_in_psum, 9 * n + e + 1)
                    for a in range(TILES):
                        part = bank[7][:, a * D:(a + 1) * D]
                        if e == 0:
                            done = v.tensor_scalar(acc[:, a, :], part, comb[:, a, 0:1], None, ALU.mult)
                        else:
                            done = v.scalar_tensor_tensor(out=acc[:, a, :], in0=part, scalar=comb[:, a, e:e + 1],
                                                          in1=acc[:, a, :], op0=ALU.mult, op1=ALU.add)
                    done.then_inc(read[7], 1)
                dve.wait_ge(sum_in_psum, PAIRS * n + PAIRS)
                for i in range(CI):
                    v.scalar_tensor_tensor(out=ym[:, i, :], in0=xs[:, i, :], scalar=w.skip[:, i:i + 1],
                                           in1=bank[3 + i][:, 0:T], op0=ALU.mult, op1=ALU.add)\
                        .then_inc(read[3 + i], 1)
                v.drain()
                v.tensor_tensor(ym[:, :, :], ym[:, :, :], zg[:, :, :], ALU.mult)
                v.drain().then_inc(ym_ready, 1)
                dve.wait_ge(down_in_psum, 9 * n + 9)
                v.tensor_tensor(rows[:, :, :], bank[7][:, 0:TILES * D].rearrange("p (a d) -> p a d", d=D),
                                acc[:, :, :], ALU.add).then_inc(read[7], 1)
                v.drain()
                v.tensor_tensor(rows[:, :, :], rows[:, :, :], x1[:, :, :], ALU.add)
                v.drain()
                inner_stats()
                dve.wait_ge(s_in_psum, n + 1)
                v.tensor_copy(s_out[:, :, :], bank[0][:, 0:TILES * D].rearrange("p (a d) -> p a d", d=D))\
                    .then_inc(read[0], 1)
                inner_apply(rows[:, :, :], w.g2, w.be2, 2 * n + 2)
                v.drain().then_inc(gate_ready, 1)
                dve.wait_ge(th_z_ready, n + 1)
                close_layer(nc, c, n, s_out[:, :, :], rows[:, :, :], th_z[:, :, :], u[:, :, :])


def store(nc, c, out):
    with ExitStack() as ctx:
        stored = ctx.enter_context(nc.semaphore("stored"))
        block = ctx.enter_context(nc.Block())

        @block.sync
        def _(sp):
            rows = out.rearrange("b (a p) d -> p (b a) d", p=P)
            sp.dma_start(rows, c.x[:, 0:TILES * NSEQ, :]).then_inc(stored, 16)
            sp.wait_ge(stored, 16)


def program(nc, A, out):
    with ExitStack() as ctx:
        c = Core()
        with ExitStack() as ctx01:
            setup(nc, ctx, ctx01, A, c)
            run_layer(nc, c, layer0)
            if LAYERS >= 2:
                run_layer(nc, c, layer1)
        layer3_weights(nc, ctx, A, c)
        if LAYERS >= 3:
            run_layer(nc, c, layer2)
        if LAYERS >= 4:
            run_layer(nc, c, layer3)
        store(nc, c, out)


def shape_constants():
    import numpy as np

    f = np.float32
    i = np.arange(P)
    tri = np.where(i[:, None] >= i[None, :], f(0), f(-1e30)).astype(f)
    k = {"const_iota8": np.tile(np.arange(8, dtype=f), (P, 1)),
         "const_causal": np.concatenate([tri, np.zeros((P, P), f), tri], 1),
         "const_row_mask": ((i[:, None] // HD1) % GR == np.arange(GR)[None, :]).astype(f)}
    pairs = np.arange(1, HD1 // 2 + 1, dtype=f)
    theta = f(1) / f(10000) ** (f(2) * (pairs - f(1)) / f(HD1))
    angle = (np.arange(T, dtype=f)[:, None] * theta[None, :]).astype(f)
    same = np.zeros((P, 3, P), f)
    for d in range(2):
        same[:, d, :] = (i[:, None] // 2 == i[None, :] // 2) & (i[None, :] % 2 == d)
    same[:, 2, :] = i[:, None] // 2 == i[None, :] // 2
    k["const_same_head"] = same
    k["const_until"] = (i[:, None] <= i[None, :]).astype(f)
    k["const_cos1"] = np.tile(np.cos(angle).astype(f), (1, 2 * H1))
    k["const_sin1"] = np.tile(np.sin(angle).astype(f), (1, 2 * H1))
    return k


def kernel(**inputs):
    import numpy as _np
    import concourse.bacc as _bacc
    from concourse.bass_utils import run_bass_kernel_spmd as _run

    nc = _bacc.Bacc("TRN2", target_bir_lowering=False, num_devices=1)
    arrays, aps = {}, {}
    for name, value in {**inputs, **shape_constants()}.items():
        a = _np.ascontiguousarray(value)
        arrays[f"in_{name}_dram"] = a
        aps[name] = nc.dram_tensor(f"in_{name}_dram", a.shape, F32, kind="ExternalInput").ap()
    out = nc.dram_tensor("out_dram", (NSEQ, T, D), F32, kind="ExternalOutput").ap()
    program(nc, aps, out)
    r = _run(nc, [arrays], core_ids=[0])
    return r.results[0]["out_dram"]
```

```python
from contextlib import ExitStack

import concourse.bass as bass
from concourse import mybir

ALU = mybir.AluOpType
ACT = mybir.ActivationFunctionType
AX = mybir.AxisListType.X
F32 = mybir.dt.float32

P = 128
NSEQ, T, D = 16, 256, 128
TILES = T // P
LN_EPS = 1e-5
LAYERS = 4

H0, DK0, SEG = 8, 64, 32
F0 = 512
NCH0 = H0 * DK0 // P
HALF0 = H0 // 2
W0 = 128

H1, HD1 = 16, 8
E1, F1 = 8, 256
ROWS = 32
GR = ROWS // HD1


def bcast(ap, n):
    return ap.unsqueeze(2).to_broadcast([ap.shape[0], ap.shape[1], n])


class Core:
    pass


def layer_norm_buffers(nc, ctx, c):
    c.stats = ctx.enter_context(nc.sbuf_tensor("ln_stats", [P, TILES, 6], F32))
    c.meanvar = ctx.enter_context(nc.sbuf_tensor("ln_meanvar", [P, TILES, 2], F32))
    c.var_eps = ctx.enter_context(nc.sbuf_tensor("ln_var_eps", [P, TILES], F32))
    c.rstd = ctx.enter_context(nc.sbuf_tensor("ln_rstd", [P, TILES], F32))
    c.minus_half = ctx.enter_context(nc.sbuf_tensor("minus_half", [P, 8], F32))
    c.xn = ctx.enter_context(nc.sbuf_tensor("xn", [P, TILES, D], F32))
    c.xnT = ctx.enter_context(nc.sbuf_tensor("xnT", [P, T], F32))


def layer_semaphore(nc, name):
    return nc.alloc_semaphore(name=name)


def run_layer(nc, c, layer):
    before = nc.snapshot_sems()
    layer(nc, c)
    nc.clear_and_free_semaphores(nc.allocated_since(before))
    nc.all_engine_barrier()


class NormSems:

    def __init__(self, sem, name):
        self.var_ready = sem(name + "_var_ready")
        self.rstd_ready = sem(name + "_rstd_ready")
        self.xn_ready = sem(name + "_xn_ready")
        self.xnT_in_psum = sem(name + "_xnT_in_psum")


def norm_stats(nc, c, s, m):
    for a in range(TILES):
        nc.vector.bn_stats(c.stats[:, a, :], c.x[:, 2 * m + a, :])
    nc.vector.drain()
    for a in range(TILES):
        nc.vector.bn_aggr(c.meanvar[:, a, :], c.stats[:, a, :])
    nc.vector.drain()
    nc.vector.tensor_scalar(c.var_eps[:, :], c.meanvar[:, :, 1], LN_EPS, None, ALU.add).then_inc(s.var_ready, 1)


def norm_power(nc, c, s, m):
    nc.gpsimd.wait_ge(s.var_ready, m + 1)
    nc.gpsimd.tensor_tensor(c.rstd[:, :], c.var_eps[:, :], c.minus_half[:, 0:TILES], ALU.pow).then_inc(s.rstd_ready, 1)


def norm_apply(nc, c, s, m, first):
    nc.vector.wait_ge(s.rstd_ready, m + 1)
    if not first:
        nc.vector.wait_ge(s.xnT_in_psum, m)
    for a in range(TILES):
        done = nc.vector.tensor_scalar(c.xn[:, a, :], c.x[:, 2 * m + a, :], c.meanvar[:, a, 0:1],
                                       c.rstd[:, a:a + 1], ALU.subtract, ALU.mult)
    done.then_inc(s.xn_ready, 1)


def norm_transpose(nc, c, s, m, bank):
    nc.tensor.wait_ge(s.xn_ready, m + 1)
    for a in range(TILES):
        done = nc.tensor.transpose(bank[:, a * P:(a + 1) * P], c.xn[:, a, :], c.ident[:, :])
    done.then_inc(s.xnT_in_psum, 1)


def norm_copy(nc, c, s, m, bank, bank_read):
    nc.scalar.wait_ge(s.xnT_in_psum, m + 1)
    nc.scalar.activation(c.xnT[:, :], bank[:, 0:T], ACT.Copy).then_inc(bank_read, 1)


H2 = 64
E2, F2 = 8, 512
CAP2 = NSEQ * T // E2


H3, HD3 = 16, 8
E3, F3 = 8, 512
DI, NS, DCONV, RANK = 256, 16, 4, 64
CI = DI // P
SG = 4


class RouteBuffers:

    def __init__(self, sb, sem):
        self.logits = sb("r_logits", [P, TILES, 8])
        self.most = sb("r_most", [P, TILES])
        self.total = sb("r_total", [P, TILES])
        self.recip = sb("r_recip", [P, TILES])
        self.probs = sb("r_probs", [P, TILES, 8])
        self.best = sb("r_best", [P, TILES, 8])
        self.index = sb("r_index", [P, TILES, 8], mybir.dt.uint32)
        self.place = sb("r_place", [P, TILES, 8])
        self.shifted = sem("r_shifted")
        self.exped = sem("r_exped")


def route_shift(nc, r, bank_cols, bank_read, bias=None):
    v = nc.vector
    if bias is None:
        v.tensor_copy(r.logits[:, :, :], bank_cols).then_inc(bank_read, 1)
    else:
        v.tensor_tensor(r.logits[:, :, :], bank_cols, bias, ALU.add).then_inc(bank_read, 1)
    v.drain()
    v.tensor_reduce(r.most[:, :], r.logits[:, :, :], AX, ALU.max)
    v.drain()
    v.tensor_tensor(r.logits[:, :, :], r.logits[:, :, :], bcast(r.most[:, :], 8), ALU.subtract)\
        .then_inc(r.shifted, 1)


def route_exp(nc, r, n):
    nc.scalar.wait_ge(r.shifted, n + 1)
    nc.scalar.activation(r.logits[:, :, :], r.logits[:, :, :], ACT.Exp).then_inc(r.exped, 1)


def route_best(nc, r, n):
    v = nc.vector
    v.wait_ge(r.exped, n + 1)
    v.tensor_reduce(r.total[:, :], r.logits[:, :, :], AX, ALU.add)
    v.drain()
    v.reciprocal(r.recip[:, :], r.total[:, :])
    v.drain()
    v.tensor_tensor(r.probs[:, :, :], r.logits[:, :, :], bcast(r.recip[:, :], 8), ALU.mult)
    v.drain()
    for a in range(TILES):
        v.max(r.best[:, a, :], r.probs[:, a, :])
    v.drain()
    for a in range(TILES):
        v.max_index(r.index[:, a, :], r.best[:, a, :], r.probs[:, a, :])
    v.drain()
    v.tensor_copy(r.place[:, :, :], r.index[:, :, :])


def close_layer(nc, c, n, s_rows, z_rows, half_tanh, u, done_sem=None):
    v = nc.vector
    v.scalar_tensor_tensor(out=u, in0=half_tanh, scalar=1.0, in1=z_rows, op0=ALU.add, op1=ALU.mult)
    v.drain()
    v.scalar_tensor_tensor(out=u, in0=u, scalar=0.5, in1=s_rows, op0=ALU.mult, op1=ALU.mult)
    v.drain()
    for a in range(TILES):
        v.tensor_tensor(c.x[:, 2 * n + a, :], c.x[:, 2 * n + a, :], u[:, a, :], ALU.add)


def setup(nc, ctx, ctx01, A, c):
    def sb_all(name, shape):
        return ctx.enter_context(nc.sbuf_tensor(name, shape, F32))

    def sb(name, shape):
        return ctx01.enter_context(nc.sbuf_tensor(name, shape, F32))

    layer_norm_buffers(nc, ctx, c)
    c.x = sb_all("x", [P, TILES * (NSEQ + 1), D])
    c.ident = sb_all("ident", [P, P])
    c.iota8 = sb_all("iota8", [P, 8])
    c.row_mask = sb_all("row_mask", [P, GR])
    c.cos1, c.sin1 = (sb_all(name, [P, TILES, 2 * H1 * HD1 // 2]) for name in ("cos1", "sin1"))
    c.w2 = {}
    for name in ("Wq", "Wk", "Wv", "Wo"):
        c.w2[name] = sb_all("l2_" + name, [P, D])
    for name in ("bq", "bk", "bv", "bo"):
        c.w2[name] = sb_all("l2_" + name, [P, D])
    c.beta = sb_all("beta", [P, 1])
    c.same_head = sb_all("same_head", [P, 3, P])
    c.until = sb_all("until", [P, P])
    c.wg2 = sb_all("wg2", [P, E2])
    c.w12, c.b12 = sb_all("w12", [P, E2, F2]), sb_all("b12", [P, E2, F2 // P])
    c.w22, c.b22 = sb_all("w22", [P, E2, F2 // P, D]), sb_all("b22", [E2, D])
    c.w2_loaded = ctx.enter_context(nc.semaphore("w2_loaded"))
    c.W2_ALL = 16 * 16
    c.wq0, c.wk0, c.wv0 = sb("wq0", [P, H0 * DK0]), sb("wk0", [P, H0 * DK0]), sb("wv0", [P, H0 * DK0])
    c.wo0 = sb("wo0", [P, NCH0, D])
    c.gate = sb("gate", [P, H0 * DK0])
    c.gate1m = sb("gate1m", [P, H0 * DK0])
    c.lnw0 = sb("lnw0", [P, F0 // P])
    c.lnb0 = sb("lnb0", [P, F0 // P])
    c.wfcT = sb("wfcT", [P, F0])
    c.wprojT = sb("wprojT", [P, F0 // P, D])
    c.zrow = sb("zrow", [P, 2, W0])
    c.mem_mask = sb("mem_mask", [P, 3 * P])

    c.causal = sb("causal", [P, 3 * P])
    c.wqkv1, c.bqkv1 = sb("wqkv1", [P, 3 * D]), sb("bqkv1", [P, 3 * D])
    c.wproj1, c.bproj1 = sb("wproj1", [P, D]), sb("bproj1", [P, D])
    c.router1 = sb("router1", [P, E1])
    c.gating1, c.up1 = sb("gating1", [P, E1, F1]), sb("up1", [P, E1, F1])
    c.down1 = sb("down1", [P, E1, F1 // P, D])

    c.w1_loaded = ctx.enter_context(nc.semaphore("w1_loaded"))
    c.W1_ALL = 13 * 16
    c.x_loaded = ctx.enter_context(nc.semaphore("x_loaded"))
    c.w0_loaded = ctx.enter_context(nc.semaphore("w0_loaded"))
    consts_made = ctx.enter_context(nc.semaphore("consts_made"))
    gate_ready = ctx.enter_context(nc.semaphore("gate_ready"))
    abs_sums = ctx.enter_context(nc.semaphore("abs_sums"))
    totals = ctx.enter_context(nc.semaphore("totals"))
    ternary = ctx.enter_context(nc.semaphore("ternary"))
    turned = ctx.enter_context(nc.semaphore("turned"))
    out_copied = ctx.enter_context(nc.semaphore("ternary_copied"))

    with ExitStack() as tmp:
        wfc = tmp.enter_context(nc.sbuf_tensor("wfc", [P, F0 // P, D], F32))
        wproj = tmp.enter_context(nc.sbuf_tensor("wproj", [P, F0], F32))
        ones = tmp.enter_context(nc.sbuf_tensor("ones", [P, P], F32))
        sums = tmp.enter_context(nc.sbuf_tensor("abs_sum", [P, 2], F32))
        limit = tmp.enter_context(nc.sbuf_tensor("limit", [P, 4], F32))
        neg = tmp.enter_context(nc.sbuf_tensor("neg", [P, 2, F0], F32))
        bank = [tmp.enter_context(nc.psum_tensor(f"setup_bank{i}", [P, 512], F32)) for i in range(3)]
        block = tmp.enter_context(nc.Block())

        @block.sync
        def _(sp):
            sp.dma_start(wfc[:, :, :], A["L0_ffn_W_fc"].rearrange("(c p) d -> p c d", p=P)).then_inc(c.w0_loaded, 16)
            sp.dma_start(wproj[:, :], A["L0_ffn_W_proj"]).then_inc(c.w0_loaded, 16)
            x_rows = A["L0_attn_x"].rearrange("b (a p) d -> p (b a) d", p=P)
            sp.dma_start(c.x[:, 0:TILES * NSEQ, :], x_rows).then_inc(c.x_loaded, 16)
            sp.dma_start(c.wq0[:, :], A["L0_attn_Wq"]).then_inc(c.w0_loaded, 16)
            sp.dma_start(c.wk0[:, :], A["L0_attn_Wk"]).then_inc(c.w0_loaded, 16)
            sp.dma_start(c.wv0[:, :], A["L0_attn_Wv"]).then_inc(c.w0_loaded, 16)
            sp.dma_start(c.wo0[:, :, :], A["L0_attn_Wo"].rearrange("(c p) d -> p c d", p=P)).then_inc(c.w0_loaded, 16)

            for dst, src in (
                    (c.iota8[:, :], A["const_iota8"]), (c.causal[:, :], A["const_causal"]),
                    (c.row_mask[:, :], A["const_row_mask"]),
                    (c.cos1[:, :, :], A["const_cos1"].rearrange("(a p) k -> p a k", p=P)),
                    (c.sin1[:, :, :], A["const_sin1"].rearrange("(a p) k -> p a k", p=P)),
                    (c.wqkv1[:, :], A["L1_attn_W_qkv"]), (c.bqkv1[:, :], A["L1_attn_b_qkv"].partition_broadcast(P)),
                    (c.wproj1[:, :], A["L1_attn_W_proj"]), (c.bproj1[:, :], A["L1_attn_b_proj"].partition_broadcast(P)),
                    (c.router1[:, :], A["L1_ffn_router_kernel_DE"]),
                    (c.gating1[:, :, :], A["L1_ffn_kernel_gating_EDF"].rearrange("e d f -> d e f")),
                    (c.up1[:, :, :], A["L1_ffn_kernel_up_EDF"].rearrange("e d f -> d e f")),
                    (c.down1[:, :, :, :], A["L1_ffn_kernel_down_EFD"].rearrange("e (k p) d -> p e k d", p=P))):
                sp.dma_start(dst, src).then_inc(c.w1_loaded, 16)
            for name in ("Wq", "Wk", "Wv", "Wo"):
                sp.dma_start(c.w2[name][:, :], A["L2_attn_" + name]).then_inc(c.w2_loaded, 16)
            for name in ("bq", "bk", "bv", "bo"):
                sp.dma_start(c.w2[name][:, :], A["L2_attn_" + name].partition_broadcast(P)).then_inc(c.w2_loaded, 16)
            for dst, src in (
                    (c.beta[:, :], A["L2_attn_beta"].partition_broadcast(P)),
                    (c.same_head[:, :, :], A["const_same_head"]), (c.until[:, :], A["const_until"]),
                    (c.wg2[:, :], A["L2_ffn_wg"]),
                    (c.w12[:, :, :], A["L2_ffn_w1"].rearrange("e d f -> d e f")),
                    (c.b12[:, :, :], A["L2_ffn_b1"].rearrange("e (k p) -> p e k", p=P)),
                    (c.w22[:, :, :, :], A["L2_ffn_w2"].rearrange("e (k p) d -> p e k d", p=P)),
                    (c.b22[:, :], A["L2_ffn_b2"])):
                with nc.allow_non_contiguous_dma("the columns of b1 are small"):
                    sp.dma_start(dst, src).then_inc(c.w2_loaded, 16)

        @block.scalar
        def _(act):
            betas = A["L0_attn_betas"].rearrange("a h b v -> (a b) (h v)")
            act.dma_start(c.gate[:, :], betas[0].partition_broadcast(P)).then_inc(gate_ready, 16)
            with nc.allow_non_contiguous_dma("two small columns"):
                act.dma_start(c.lnw0[:, :], A["L0_ffn_ln_w"].rearrange("(c p) -> p c", p=P)).then_inc(c.w0_loaded, 16)
                act.dma_start(c.lnb0[:, :], A["L0_ffn_ln_b"].rearrange("(c p) -> p c", p=P)).then_inc(c.w0_loaded, 16)
            act.wait_ge(gate_ready, 16)
            nc.scalar.activation(c.gate[:, :], c.gate[:, :], ACT.Sigmoid).then_inc(gate_ready, 1)

        @block.gpsimd
        def _(pool):
            nc.gpsimd.memset(c.minus_half[:, :], -0.5)
            nc.gpsimd.memset(c.x[:, TILES * NSEQ:, :], 0.0)
            nc.gpsimd.memset(c.ident[:, :], 0.0)
            nc.gpsimd.memset(c.zrow[:, :, :], 0.0)
            nc.gpsimd.memset(c.mem_mask[:, :], 1.0)
            nc.gpsimd.drain()
            nc.gpsimd.affine_select(out=c.ident[:, :], in_=c.ident[:, :], compare_op=ALU.not_equal, fill=1.0,
                                    base=0, pattern=[[-1, P]], channel_multiplier=1)
            for lo, hi in ((0, 2 * P), (2 * P, 3 * P)):
                seg = c.mem_mask[:, lo:hi].rearrange("p (a r) -> p a r", r=SEG)
                nc.gpsimd.affine_select(out=seg, in_=seg, compare_op=ALU.is_gt, fill=0.0, base=0,
                                        pattern=[[SEG, (hi - lo) // SEG], [0, SEG]], channel_multiplier=-1)
            nc.gpsimd.memset(c.zrow[0:DK0, 0, DK0:DK0 + 1], 1.0 / DK0)
            nc.gpsimd.drain()
            nc.gpsimd.memset(c.zrow[DK0:P, 1, DK0:DK0 + 1], 1.0 / DK0).then_inc(consts_made, 1)

        @block.vector
        def _(dve):
            nc.vector.memset(ones[:, :], 1.0)
            dve.wait_ge(c.w0_loaded, 16 * 8)
            nc.vector.tensor_reduce(sums[:, 0:1], wfc[:, :, :], mybir.AxisListType.XY, ALU.add,
                                    apply_absolute_value=True)
            nc.vector.tensor_reduce(sums[:, 1:2], wproj[:, :], AX, ALU.add,
                                    apply_absolute_value=True).then_inc(abs_sums, 1)
            dve.wait_ge(totals, 1)
            nc.vector.tensor_scalar(limit[:, 2:4], bank[2][:, 0:2], 1.0 / (F0 * D), 1e-6, ALU.mult, ALU.add)
            nc.vector.drain()
            nc.vector.tensor_scalar(limit[:, 0:2], limit[:, 2:4], 0.5, None, ALU.mult)
            nc.vector.tensor_scalar(limit[:, 2:4], limit[:, 2:4], -0.5, None, ALU.mult)
            nc.vector.drain()
            for i, w in enumerate((wfc[:, :, :].rearrange("p c d -> p (c d)"), wproj[:, :])):
                nc.vector.tensor_scalar(neg[:, i, :], w, limit[:, 2 + i:3 + i], None, ALU.is_lt)
            nc.vector.drain()
            for i, w in enumerate((wfc[:, :, :].rearrange("p c d -> p (c d)"), wproj[:, :])):
                done = nc.vector.scalar_tensor_tensor(out=w, in0=w, scalar=limit[:, i:i + 1], in1=neg[:, i, :],
                                                      op0=ALU.is_gt, op1=ALU.subtract)
            done.then_inc(ternary, 1)
            dve.wait_ge(gate_ready, 17)
            nc.vector.tensor_scalar(c.gate1m[:, :], c.gate[:, :], -1.0, 1.0, ALU.mult, ALU.add)
            dve.wait_ge(turned, 1)
            nc.vector.tensor_copy(c.wfcT[:, :], bank[0][:, :])
            nc.vector.tensor_copy(c.wprojT[:, :, :].rearrange("p c d -> p (c d)"), bank[1][:, :]).then_inc(out_copied, 1)

        @block.tensor
        def _(pe):
            pe.wait_ge(consts_made, 1)
            pe.wait_ge(abs_sums, 1)
            nc.tensor.matmul(bank[2][:, 0:2], ones[:, :], sums[:, :], start=True, stop=True).then_inc(totals, 1)
            pe.wait_ge(ternary, 1)
            for j in range(F0 // P):
                nc.tensor.transpose(bank[0][:, j * P:(j + 1) * P], wfc[:, j, :], c.ident[:, :])
                done = nc.tensor.transpose(bank[1][:, j * P:(j + 1) * P], wproj[:, j * P:(j + 1) * P], c.ident[:, :])
            done.then_inc(turned, 1)


def layer0(nc, c):
    with ExitStack() as ctx:
        def sb(name, shape):
            return ctx.enter_context(nc.sbuf_tensor("a0_" + name, shape, F32))

        def sem(name):
            return layer_semaphore(nc, "l0_" + name)

        bank = [ctx.enter_context(nc.psum_tensor(f"l0_bank{i}", [P, 512], F32)) for i in range(8)]
        qk = sb("qk", [P, NCH0, 2, T])
        pos = sb("pos", [P, NCH0, 2, T])
        low = sb("low", [P, 2, 2 * T])
        vdot = sb("vdot", [P, TILES, H0 * DK0])
        vmem = sb("vmem", [P, TILES, H0, W0])
        AG = TILES * H0 // 2
        top = sb("top", [P, 2, AG])
        shifted = sb("shifted", [P, 2, AG, SEG])
        recip = sb("recip", [P, TILES, H0])
        total = sb("total", [P, AG, 2])
        probsT = sb("probsT", [P, 2, AG, P])
        memT = sb("memT", [P, 2, 3 * P])
        rden = sb("rden", [P, TILES, HALF0])
        part = sb("part", [P, TILES, HALF0, DK0])
        part2 = sb("part2", [P, TILES, HALF0, DK0])
        att = sb("att", [P, TILES, H0 * DK0])
        attT = sb("attT", [P, TILES, NCH0, P])
        h = sb("h", [P, TILES, F0])
        hstats = sb("hstats", [P, TILES, 6])
        hmv = sb("hmv", [P, TILES, 2])
        hve = sb("hve", [P, TILES])
        hrstd = sb("hrstd", [P, TILES])
        hT = sb("hT", [P, TILES, F0 // P, P])
        th = sb("th", [P, TILES, D])
        u = sb("u", [P, TILES, D])

        s = NormSems(sem, "n")
        free = [sem(f"bank{i}_read") for i in range(8)]
        PER0, PER1, PER45, PER67 = 4, 3, 7, 3
        qk_in_psum = sem("qk_in_psum")
        v_in_psum = sem("v_in_psum")
        h_in_psum = sem("h_in_psum")
        low_ready = sem("low_ready")
        low_exp = sem("low_exp")
        pos_ready = sem("pos_ready")
        scores_in_psum = sem("scores_in_psum")
        shifted_ready = sem("shifted_ready")
        exp_ready = sem("exp_ready")
        probs_ready = sem("probs_ready")
        mem_scores = sem("mem_scores")
        mem_used = sem("mem_used")
        dot_done = sem("dot_done")
        att_ready = sem("att_ready")
        attT_in_psum = sem("attT_in_psum")
        hvar_ready = sem("hvar_ready")
        hrstd_ready = sem("hrstd_ready")
        hn_ready = sem("hn_ready")
        hT_in_psum = sem("hT_in_psum")
        sz_in_psum = sem("sz_in_psum")
        th_ready = sem("th_ready")

        block = ctx.enter_context(nc.Block())

        @block.tensor
        def _(pe):
            pe.sem_inc(free[1], 1)
            for i in (2, 3, 4, 5, 6, 7):
                pe.sem_inc(free[i], 1)
            norm_transpose(nc, c, s, 0, bank[0])
            with pe.Fori(0, NSEQ) as n:
                pe.wait_ge(free[0], PER0 * n + 1)
                for j in range(NCH0):
                    per = PER0 if j % 2 == 0 else PER1
                    pe.wait_ge(free[j % 2], per * n + j // 2 + 1)
                    cols = slice(j * P, (j + 1) * P)
                    nc.tensor.matmul(bank[j % 2][:, 0:T], c.wq0[:, cols], c.xnT[:, :], start=True, stop=True)
                    nc.tensor.matmul(bank[j % 2][:, T:2 * T], c.wk0[:, cols], c.xnT[:, :],
                                     start=True, stop=True).then_inc(qk_in_psum, 1)
                for a in range(TILES):
                    pe.wait_ge(free[a], (PER0, PER1)[a] * n + 3)
                    nc.tensor.matmul(bank[a][:, :], c.xnT[:, a * P:(a + 1) * P], c.wv0[:, :],
                                     start=True, stop=True).then_inc(v_in_psum, 1)
                for a in range(TILES):
                    if a == 1:
                        pe.wait_ge(free[0], PER0 * n + 3)
                        pe.wait_ge(free[2], 2 * n + 1)
                        pe.wait_ge(free[3], 2 * n + 1)
                        pe.wait_ge(shifted_ready, 2 * n + 1)
                        pe.wait_ge(free[1], PER1 * n + 3)
                    pe.wait_ge(free[6 + a], PER67 * n + 1)
                    nc.tensor.matmul(bank[6 + a][:, :], c.xnT[:, a * P:(a + 1) * P], c.wfcT[:, :],
                                     start=True, stop=True).then_inc(h_in_psum, 1)
                for odd in range(2):
                    rows = slice(DK0 * odd, DK0 * odd + DK0)
                    for ag in range(AG):
                        a, pair = divmod(ag, H0 // 2)
                        for g in range(P // SEG):
                            t0 = a * P + g * SEG
                            done = nc.tensor.matmul(
                                bank[2 + odd][g * SEG:(g + 1) * SEG, ag * SEG:(ag + 1) * SEG],
                                qk[rows, pair, 0, t0:t0 + SEG], qk[rows, pair, 1, t0:t0 + SEG],
                                start=True, stop=True)
                    done.then_inc(scores_in_psum, 1)

                def memory_scores(hd):
                    b = 4 + hd % 2
                    pe.wait_ge(free[b], PER45 * n + hd // 2 + 1)
                    rows = slice(DK0 * (hd % 2), DK0 * (hd % 2) + DK0)
                    nc.tensor.matmul(bank[b][:, 0:T], pos[rows, hd // 2, 1, 0:P], pos[rows, hd // 2, 0, :],
                                     start=True, stop=True)
                    nc.tensor.matmul(bank[b][:, T:3 * P], pos[rows, hd // 2, 1, P:T], pos[rows, hd // 2, 0, P:T],
                                     start=True, stop=True).then_inc(mem_scores, 1)

                def memory_out(hd):
                    if hd % HALF0 == 0:
                        pe.wait_ge(free[6], PER67 * n + hd // HALF0 + 2)
                        pe.wait_ge(free[7], PER67 * n + hd // HALF0 + 2)
                    pe.wait_ge(free[4 + hd % 2], PER45 * n + hd // 2 + 2)
                    w = W0
                    for a in range(TILES):
                        out = bank[6 + a][:, (hd % HALF0) * w:(hd % HALF0 + 1) * w]
                        for kt in range(a + 1):
                            lo = (a if kt == 0 else 2) * P
                            nc.tensor.matmul(out, memT[:, hd % 2, lo:lo + P], vmem[:, kt, hd, :],
                                             start=(kt == 0), stop=False)
                        done = nc.tensor.matmul(out, pos[:, hd // 2, 0, a * P:(a + 1) * P],
                                                c.zrow[:, hd % 2, :],
                                                start=False, stop=True)
                    done.then_inc(mem_used, 1)

                def softmax_out(half):
                    pe.wait_ge(probs_ready, n + 1)
                    if half == 1:
                        pe.wait_ge(free[2], 2 * n + 2)
                        pe.wait_ge(free[3], 2 * n + 2)
                    for a in range(TILES):
                        for i in range(HALF0):
                            hd = half * HALF0 + i
                            done = nc.tensor.matmul(bank[2 + a][:, 256 + i * DK0:256 + (i + 1) * DK0],
                                                    probsT[:, hd % 2, a * (H0 // 2) + hd // 2, :], vdot[:, a, hd * DK0:(hd + 1) * DK0],
                                                    start=True, stop=True)
                    done.then_inc(dot_done, 1)

                pe.wait_ge(pos_ready, NCH0 * n + NCH0)
                pe.wait_ge(free[0], PER0 * n + 4)
                pe.wait_ge(free[1], PER1 * n + 4)
                memory_scores(0)
                for hd in range(H0):
                    if hd + 1 < H0:
                        memory_scores(hd + 1)
                    memory_out(hd)
                    if hd % HALF0 == HALF0 - 1:
                        softmax_out(hd // HALF0)
                pe.wait_ge(hn_ready, n + 1)
                for a in range(TILES):
                    pe.wait_ge(free[4 + a], PER45 * n + 5)
                    for j in range(F0 // P):
                        done = nc.tensor.transpose(bank[4 + a][:, j * P:(j + 1) * P], h[:, a, j * P:(j + 1) * P],
                                                   c.ident[:, :])
                    done.then_inc(hT_in_psum, 1)
                pe.wait_ge(free[0], PER0 * n + 4)
                norm_transpose(nc, c, s, n + 1, bank[0])
                pe.wait_ge(att_ready, 2 * n + 2)
                for a in range(TILES):
                    pe.wait_ge(free[4 + a], PER45 * n + 6)
                    for j in range(NCH0):
                        done = nc.tensor.transpose(bank[4 + a][:, j * P:(j + 1) * P],
                                                   att[:, a, j * P:(j + 1) * P], c.ident[:, :])
                    done.then_inc(attT_in_psum, 1)
                for a in range(TILES):
                    pe.wait_ge(free[4 + a], PER45 * n + 7)
                    for j in range(F0 // P):
                        nc.tensor.matmul(bank[4 + a][:, 0:D], hT[:, a, j, :], c.wprojT[:, j, :],
                                         start=(j == 0), stop=(j == F0 // P - 1))
                    for j in range(NCH0):
                        done = nc.tensor.matmul(bank[4 + a][:, D:2 * D], attT[:, a, j, :], c.wo0[:, j, :],
                                                start=(j == 0), stop=(j == NCH0 - 1))
                    done.then_inc(sz_in_psum, 1)

        @block.scalar
        def _(act):
            norm_copy(nc, c, s, 0, bank[0], free[0])
            with act.Fori(0, NSEQ) as n:
                def copy_qk(j):
                    if j == 0:
                        act.wait_ge(scores_in_psum, 2 * n + 1)
                    act.wait_ge(qk_in_psum, NCH0 * n + j + 1)
                    nc.scalar.activation(qk[:, j, :, :].rearrange("p a t -> p (a t)"), bank[j % 2][:, :],
                                         ACT.Copy).then_inc(free[j % 2], 1)

                def exp_low(j):
                    act.wait_ge(low_ready, NCH0 * n + j + 1)
                    nc.scalar.activation(low[:, j % 2, :], low[:, j % 2, :], ACT.Exp).then_inc(low_exp, 1)

                copy_qk(0)
                for j in range(1, NCH0):
                    copy_qk(j)
                    exp_low(j - 1)
                exp_low(NCH0 - 1)
                for a in range(TILES):
                    act.wait_ge(shifted_ready, TILES * n + a + 2)
                    rows = shifted[:, a, :, :].rearrange("p h k -> p (h k)")
                    nc.scalar.activation(rows, rows, ACT.Exp, scale=DK0 ** -0.5).then_inc(exp_ready, 1)
                act.wait_ge(hT_in_psum, TILES * n + 1)
                for a in range(TILES):
                    act.wait_ge(h_in_psum, TILES * n + a + 1)
                    nc.scalar.activation(h[:, a, :], bank[6 + a][:, :], ACT.Gelu).then_inc(free[6 + a], 1)
                act.wait_ge(sz_in_psum, TILES * n + 1)
                for a in range(TILES):
                    act.wait_ge(hT_in_psum, TILES * n + a + 2)
                    for j in range(F0 // P):
                        done = nc.scalar.activation(hT[:, a, j, :], bank[4 + a][:, j * P:(j + 1) * P], ACT.Identity,
                                                    bias=c.lnb0[:, j:j + 1], scale=c.lnw0[:, j:j + 1])
                    done.then_inc(free[4 + a], 1)
                act.wait_ge(h_in_psum, TILES * n + 2)
                norm_copy(nc, c, s, n + 1, bank[0], free[0])
                for a in range(TILES):
                    act.wait_ge(attT_in_psum, TILES * n + a + 2)
                    nc.scalar.activation(attT[:, a, :, :].rearrange("p c t -> p (c t)"), bank[4 + a][:, :],
                                         ACT.Copy).then_inc(free[4 + a], 1)
                for a in range(TILES):
                    act.wait_ge(sz_in_psum, TILES * n + a + 2)
                    nc.scalar.activation(th[:, a, :], bank[4 + a][:, 0:D], ACT.Tanh, scale=0.5).then_inc(th_ready, 1)

        @block.gpsimd
        def _(pool):
            norm_power(nc, c, s, 0)
            with pool.Fori(0, NSEQ) as n:
                norm_power(nc, c, s, n + 1)
                pool.wait_ge(hvar_ready, n + 1)
                nc.gpsimd.tensor_tensor(hrstd[:, :], hve[:, :], c.minus_half[:, 0:TILES], ALU.pow)\
                    .then_inc(hrstd_ready, 1)

        @block.vector
        def _(dve):
            nc.vector.memset(probsT[:, :, :, :].rearrange("p o g k -> p (o g k)"), 0.0)
            nc.vector.memset(vmem[:, :, :, :], 0.0)
            nc.vector.drain()
            nc.vector.memset(vmem[:, :, :, DK0:DK0 + 1], 1.0)
            for g in (shifted_ready, scores_in_psum, hT_in_psum, sz_in_psum, mem_used, dot_done, attT_in_psum):
                dve.sem_inc(g, 1)
            dve.wait_ge(c.x_loaded, 16)
            norm_stats(nc, c, s, 0)
            norm_apply(nc, c, s, 0, True)
            with dve.Fori(0, NSEQ) as n:
                def take_low(j):
                    dve.wait_ge(free[j % 2], (PER0, PER1)[j % 2] * n + j // 2 + 2)
                    nc.vector.tensor_scalar(low[:, j % 2, :], qk[:, j, :, :].rearrange("p a t -> p (a t)"), 0.0, None,
                                            ALU.min).then_inc(low_ready, 1)

                def elu_plus_1(j):
                    if j == 0:
                        dve.wait_ge(mem_used, H0 * n + 1)
                    dve.wait_ge(low_exp, NCH0 * n + j + 1)
                    nc.vector.scalar_tensor_tensor(
                        out=pos[:, j, :, :].rearrange("p a t -> p (a t)"),
                        in0=qk[:, j, :, :].rearrange("p a t -> p (a t)"), scalar=0.0,
                        in1=low[:, j % 2, :], op0=ALU.max, op1=ALU.add).then_inc(pos_ready, 1)

                take_low(0)
                for j in range(1, NCH0):
                    take_low(j)
                    elu_plus_1(j - 1)
                    nc.vector.drain()
                elu_plus_1(NCH0 - 1)
                dve.wait_ge(dot_done, 2 * n + 1)
                for a in range(TILES):
                    dve.wait_ge(v_in_psum, TILES * n + a + 1)
                    nc.vector.tensor_tensor(vdot[:, a, :], bank[a][:, :], c.gate1m[:, :], ALU.mult)
                    nc.vector.tensor_tensor(vmem[:, a, :, 0:DK0], bank[a][:, :].rearrange("p (h v) -> p h v", h=H0),
                                            c.gate[:, :].rearrange("p (h v) -> p h v", h=H0), ALU.mult)\
                        .then_inc(free[a], 1)
                norm_stats(nc, c, s, n + 1)
                for a in range(TILES):
                    dve.wait_ge(scores_in_psum, TILES * n + a + 2)
                    nc.vector.tensor_reduce(top[:, a, :], bank[2 + a][:, 0:256].rearrange("p (h k) -> p h k", h=AG),
                                            AX, ALU.max)
                nc.vector.drain()
                for a in range(TILES):
                    nc.vector.tensor_tensor(shifted[:, a, :, :], bank[2 + a][:, 0:256].rearrange("p (h k) -> p h k", h=AG),
                                            bcast(top[:, a, :], SEG), ALU.subtract).then_inc(shifted_ready, 1)
                norm_apply(nc, c, s, n + 1, False)
                def mask_memory(hd):
                    b = 4 + hd % 2
                    if hd >= 2:
                        dve.wait_ge(mem_used, H0 * n + hd)
                    dve.wait_ge(mem_scores, H0 * n + hd + 1)
                    nc.vector.tensor_tensor(memT[:, hd % 2, :], bank[b][:, 0:3 * P], c.mem_mask[:, :], ALU.mult)\
                        .then_inc(free[b], 1)

                def combine(half):
                    dve.wait_ge(mem_used, H0 * n + (half + 1) * HALF0 + 1)
                    w = W0
                    mem = [bank[6 + a][:, 0:HALF0 * w].rearrange("p (h v) -> p h v", v=w) for a in range(TILES)]
                    for a in range(TILES):
                        nc.vector.reciprocal(rden[:, a, :], mem[a][:, :, DK0])
                    nc.vector.drain()
                    for a in range(TILES):
                        nc.vector.tensor_tensor(part[:, a, :, :], mem[a][:, :, 0:DK0], bcast(rden[:, a, :], DK0),
                                                ALU.mult).then_inc(free[6 + a], 1)
                    dve.wait_ge(dot_done, 2 * n + half + 2)
                    for a in range(TILES):
                        nc.vector.tensor_tensor(part2[:, a, :, :],
                                                bank[2 + a][:, 256:512].rearrange("p (h v) -> p h v", v=DK0),
                                                bcast(recip[:, a, half * HALF0:(half + 1) * HALF0], DK0), ALU.mult)\
                            .then_inc(free[2 + a], 1)
                    nc.vector.drain()
                    if half == 0:
                        dve.wait_ge(attT_in_psum, TILES * n + 1)
                    lo = half * HALF0 * DK0
                    for a in range(TILES):
                        done = nc.vector.tensor_tensor(
                            att[:, a, lo:lo + HALF0 * DK0].rearrange("p (h v) -> p h v", v=DK0),
                            part[:, a, :, :], part2[:, a, :, :], ALU.add)
                    done.then_inc(att_ready, 1)

                mask_memory(0)
                mask_memory(1)
                for a in range(TILES):
                    dve.wait_ge(exp_ready, TILES * n + a + 1)
                    nc.vector.tensor_reduce(total[:, :, a], shifted[:, a, :, :], AX, ALU.add)
                    for g in range(P // SEG):
                        rows = slice(g * SEG, (g + 1) * SEG)
                        nc.vector.transpose(probsT[rows, a, :, rows], shifted[rows, a, :, :])
                    mask_memory(2 + a)
                nc.vector.drain()
                nc.vector.reciprocal(recip[:, :, :].rearrange("p a h -> p (a h)"),
                                     total[:, :, :].rearrange("p g o -> p (g o)")).then_inc(probs_ready, 1)
                mask_memory(4)
                dve.wait_ge(free[6], PER67 * n + 2)
                dve.wait_ge(free[7], PER67 * n + 2)
                for a in range(TILES):
                    nc.vector.bn_stats(hstats[:, a, :], h[:, a, :])
                nc.vector.drain()
                for a in range(TILES):
                    nc.vector.bn_aggr(hmv[:, a, :], hstats[:, a, :])
                nc.vector.drain()
                nc.vector.tensor_scalar(hve[:, :], hmv[:, :, 1], LN_EPS, None, ALU.add).then_inc(hvar_ready, 1)
                combine(0)
                for hd in range(HALF0 + 1, H0):
                    mask_memory(hd)
                dve.wait_ge(hrstd_ready, n + 1)
                for a in range(TILES):
                    done = nc.vector.tensor_scalar(h[:, a, :], h[:, a, :], hmv[:, a, 0:1], hrstd[:, a:a + 1],
                                                   ALU.subtract, ALU.mult)
                done.then_inc(hn_ready, 1)
                combine(1)
                for a in range(TILES):
                    dve.wait_ge(th_ready, TILES * n + a + 1)
                    nc.vector.scalar_tensor_tensor(out=u[:, a, :], in0=th[:, a, :], scalar=1.0, in1=bank[4 + a][:, 0:D],
                                                   op0=ALU.add, op1=ALU.mult)
                nc.vector.drain()
                for a in range(TILES):
                    nc.vector.scalar_tensor_tensor(out=u[:, a, :], in0=u[:, a, :], scalar=0.5,
                                                   in1=bank[4 + a][:, D:2 * D], op0=ALU.mult, op1=ALU.mult)\
                        .then_inc(free[4 + a], 1)
                nc.vector.drain()
                for a in range(TILES):
                    nc.vector.tensor_tensor(c.x[:, 2 * n + a, :], c.x[:, 2 * n + a, :], u[:, a, :], ALU.add)


def layer1(nc, c):
    with ExitStack() as ctx:
        def sb(name, shape, dtype=F32):
            return ctx.enter_context(nc.sbuf_tensor("b1_" + name, shape, dtype))

        def sem(name):
            return layer_semaphore(nc, "l1_" + name)

        bank = [ctx.enter_context(nc.psum_tensor(f"l1_bank{i}", [P, 512], F32)) for i in range(8)]
        KF = F1 // P
        CH = E1 * KF
        assert CH == H1 and KF == 2
        RP = 4
        qkv = sb("qkv", [P, TILES, 3 * D])
        rot = sb("rot", [P, TILES, 2, H1, HD1 // 2, 2])
        t1 = sb("t1", [P, 2, H1, HD1 // 2])
        t2 = sb("t2", [P, 2, H1, HD1 // 2])
        t3 = sb("t3", [P, 2, H1, HD1 // 2])
        t4 = sb("t4", [P, 2, H1, HD1 // 2])
        qT = sb("qT", [P, GR, T])
        kT = sb("kT", [P, H1 // GR, T])
        neg = sb("neg", [P, RP, 3 * P])
        nmax = sb("nmax", [P, RP, TILES])
        total = sb("total", [P, TILES, H1])
        recip = sb("recip", [P, TILES, H1])
        pT = sb("pT", [P, 2, 3 * P])
        y = sb("y", [P, TILES, D])
        yT = sb("yT", [P, T])
        s_out = sb("s_out", [P, TILES, D])
        r = RouteBuffers(sb, sem)
        diff = sb("diff", [P, TILES])
        ediff = sb("ediff", [P, TILES])
        ediff1 = sb("ediff1", [P, TILES])
        first = sb("first", [P, TILES])
        second = sb("second", [P, TILES])
        comb = sb("comb", [P, TILES, E1])
        comb2 = sb("comb2", [P, TILES, E1])
        th = sb("th", [P, 2, T])
        gated = sb("gated", [P, 2, T])
        fused = sb("fused", [P, 4, T])
        acc = sb("acc", [P, TILES, D])
        th_z = sb("th_z", [P, TILES, D])
        u = sb("u", [P, TILES, D])
        SCALE = float(HD1) ** -0.5

        s = NormSems(sem, "n")
        read = [sem(f"bank{i}_read") for i in range(8)]
        PER0 = 3
        PERS = H1 // 2
        PERB = PERS + 1
        PER7 = E1
        TURNS = GR + H1 // GR
        qkv_in_psum = sem("qkv_in_psum")
        logits_in_psum = sem("logits_in_psum")
        diff_ready = sem("diff_ready")
        ediff_ready = sem("ediff_ready")
        rot_ready = sem("rot_ready")
        qkT_in_psum = sem("qkT_in_psum")
        turned = sem("turned")
        scores_in_psum = sem("scores_in_psum")
        exp_ready = sem("exp_ready")
        pT_in_psum = sem("pT_in_psum")
        head_done = sem("head_done")
        y_ready = sem("y_ready")
        yT_in_psum = sem("yT_in_psum")
        s_in_psum = sem("s_in_psum")
        hidden_in_psum = sem("hidden_in_psum")
        th_ready = sem("th_ready")
        down_in_psum = sem("down_in_psum")
        acc_ready = sem("acc_ready")
        zeroed = sem("zeroed")
        th_z_ready = sem("th_z_ready")

        block = ctx.enter_context(nc.Block())

        @block.tensor
        def _(pe):
            def turn_rows(m):
                pe.wait_ge(read[5], PERB * m + 1)
                norm_transpose(nc, c, s, m, bank[5])

            def qkv_rows(m, a):
                b = (6, 1)[a]
                if a == 0:
                    pe.wait_ge(read[5], PERB * m + 2)
                pe.wait_ge(read[b], PERB * m + 1)
                nc.tensor.matmul(bank[b][:, 0:3 * D], c.xnT[:, a * P:(a + 1) * P], c.wqkv1[:, :],
                                 start=True, stop=True).then_inc(qkv_in_psum, 1)

            def route(m):
                pe.wait_ge(read[2], PERB * m + 1)
                for a in range(TILES):
                    done = nc.tensor.matmul(bank[2][:, a * E1:(a + 1) * E1], c.xnT[:, a * P:(a + 1) * P],
                                            c.router1[:, :], start=True, stop=True)
                done.then_inc(logits_in_psum, 1)

            for i in range(8):
                pe.sem_inc(read[i], 1)
            pe.wait_ge(c.w1_loaded, c.W1_ALL)
            turn_rows(0)
            qkv_rows(0, 0)
            qkv_rows(0, 1)
            route(0)
            with pe.Fori(0, NSEQ) as n:
                def hidden(k):
                    b, e, f = 5 + k % 2, k // KF, k % KF
                    pe.wait_ge(read[b], PERB * n + k // 2 + 2)
                    nc.tensor.matmul(bank[b][:, 0:T], c.gating1[:, e, f * P:(f + 1) * P], c.xnT[:, :],
                                     start=True, stop=True)
                    nc.tensor.matmul(bank[b][:, T:2 * T], c.up1[:, e, f * P:(f + 1) * P], c.xnT[:, :],
                                     start=True, stop=True).then_inc(hidden_in_psum, 1)

                def scores(h):
                    b, g = 1 + h % 2, h // GR
                    pe.wait_ge(turned, TURNS * n + (2 + h if h < GR else GR + 1 + g))
                    pe.wait_ge(read[b], PERB * n + h // 2 + 2)
                    nc.tensor.matmul(bank[b][:, 0:P], qT[:, h % GR, 0:P], kT[:, g, 0:P], start=True, stop=True)
                    nc.tensor.matmul(bank[b][:, P:3 * P], qT[:, h % GR, P:T], kT[:, g, :],
                                     start=True, stop=True).then_inc(scores_in_psum, 1)

                def turn_probs(h):
                    b = 3 + h % 2
                    pe.wait_ge(read[b], PERS * n + h // 2 + 1)
                    pe.wait_ge(exp_ready, H1 * n + h + 1)
                    for j in range(3):
                        done = nc.tensor.transpose(bank[b][:, j * P:(j + 1) * P],
                                                   neg[:, h % RP, j * P:(j + 1) * P], c.ident[:, :])
                    done.then_inc(pT_in_psum, 1)

                def head_out(h):
                    pe.wait_ge(turned, TURNS * (n + 1))
                    pe.wait_ge(read[3 + h % 2], PERS * n + h // 2 + 2)
                    v = [qkv[:, a, 3 * HD1 * h + 2 * HD1:3 * HD1 * h + 3 * HD1] for a in range(TILES)]
                    out = [bank[0][:, a * D + h * HD1:a * D + (h + 1) * HD1] for a in range(TILES)]
                    p = pT[:, h % 2, :]
                    nc.tensor.matmul(out[0], p[:, 0:P], v[0], start=True, stop=True)
                    nc.tensor.matmul(out[1], p[:, P:2 * P], v[0], start=True, stop=False)
                    nc.tensor.matmul(out[1], p[:, 2 * P:3 * P], v[1], start=False, stop=True).then_inc(head_done, 1)

                def down(e):
                    pe.wait_ge(read[6], PERB * n + e + 3)
                    pe.wait_ge(read[7], PER7 * n + e + 1)
                    for a in range(TILES):
                        for f in range(KF):
                            done = nc.tensor.matmul(bank[7][:, a * D:(a + 1) * D],
                                                    fused[:, (KF * e + f) % 4, a * P:(a + 1) * P],
                                                    c.down1[:, e, f, :], start=(f == 0), stop=(f == KF - 1))
                    done.then_inc(down_in_psum, 1)

                hidden(0)
                hidden(1)
                pe.wait_ge(rot_ready, n + 1)
                pe.wait_ge(read[0], PER0 * n + 1)
                for a in range(TILES):
                    for i in range(2):
                        done = nc.tensor.transpose(bank[0][:, i * T + a * P:i * T + (a + 1) * P],
                                                   rot[:, a, i, :, :, :].rearrange("p h k o -> p (h k o)"),
                                                   c.ident[:, :])
                done.then_inc(qkT_in_psum, 1)
                for k in range(H1 + 3):
                    if k < H1:
                        scores(k)
                    if k + 2 < CH:
                        hidden(k + 2)
                    if 2 <= k <= H1 + 1:
                        turn_probs(k - 2)
                    if k == H1 - 1:
                        turn_rows(n + 1)
                    if k == H1 + 2:
                        qkv_rows(n + 1, 0)
                    if k >= 3:
                        head_out(k - 3)
                    if k % 2 and k < H1:
                        down(k // 2)
                qkv_rows(n + 1, 1)
                route(n + 1)
                pe.wait_ge(y_ready, n + 1)
                for a in range(TILES):
                    done = nc.tensor.transpose(bank[0][:, a * P:(a + 1) * P], y[:, a, :], c.ident[:, :])
                done.then_inc(yT_in_psum, 1)
                pe.wait_ge(read[0], PER0 * n + 3)
                for a in range(TILES):
                    done = nc.tensor.matmul(bank[0][:, a * D:(a + 1) * D], yT[:, a * P:(a + 1) * P], c.wproj1[:, :],
                                            start=True, stop=True)
                done.then_inc(s_in_psum, 1)

        @block.scalar
        def _(act):
            act.wait_ge(zeroed, 1)
            norm_copy(nc, c, s, 0, bank[5], read[5])
            with act.Fori(0, NSEQ) as n:
                def tanh_gate(k):
                    act.wait_ge(hidden_in_psum, CH * n + k + 1)
                    nc.scalar.activation(th[:, k % 2, :], bank[5 + k % 2][:, 0:T], ACT.Tanh, scale=0.5)\
                        .then_inc(th_ready, 1)

                def exp_scores(h):
                    act.wait_ge(read[1 + h % 2], PERB * n + h // 2 + 3)
                    for a, cols in enumerate((slice(0, P), slice(P, 3 * P))):
                        done = nc.scalar.activation(neg[:, h % RP, cols], neg[:, h % RP, cols], ACT.Exp,
                                                    bias=nmax[:, h % RP, a:a + 1], scale=-1.0,
                                                    accum_out=total[:, a, h:h + 1])
                    done.then_inc(exp_ready, 1)

                def copy_pT(h):
                    if h >= 2:
                        act.wait_ge(head_done, H1 * n + h - 1)
                    act.wait_ge(pT_in_psum, H1 * n + h + 1)
                    nc.scalar.activation(pT[:, h % 2, :], bank[3 + h % 2][:, 0:3 * P], ACT.Copy)\
                        .then_inc(read[3 + h % 2], 1)

                route_exp(nc, r, n)
                tanh_gate(0)
                tanh_gate(1)
                act.wait_ge(qkT_in_psum, n + 1)
                def copy_kT(g):
                    rows = slice(ROWS * g, ROWS * (g + 1))
                    return nc.scalar.activation(kT[rows, g, :], bank[0][rows, T:2 * T], ACT.Copy).then_inc(turned, 1)

                copy_kT(0)
                for i in range(GR):
                    nc.scalar.activation(qT[:, i, :], bank[0][:, 0:T], ACT.Copy, scale=c.row_mask[:, i:i + 1])\
                        .then_inc(turned, 1)
                for g in range(1, H1 // GR):
                    copy_kT(g)
                for k in range(H1 + 2):
                    if k + 2 < CH:
                        tanh_gate(k + 2)
                    if k >= 2:
                        copy_pT(k - 2)
                    if k == 0:
                        act.wait_ge(diff_ready, n + 1)
                        nc.scalar.activation(ediff[:, :], diff[:, :], ACT.Exp).then_inc(ediff_ready, 1)
                    if k < H1:
                        exp_scores(k)
                    if k == H1 - 1:
                        norm_copy(nc, c, s, n + 1, bank[5], read[5])
                act.wait_ge(acc_ready, n + 1)
                nc.scalar.activation(th_z[:, :, :], acc[:, :, :], ACT.Tanh, scale=0.5).then_inc(th_z_ready, 1)
                act.wait_ge(yT_in_psum, n + 1)
                nc.scalar.activation(yT[:, :], bank[0][:, 0:T], ACT.Copy).then_inc(read[0], 1)

        @block.gpsimd
        def _(pool):
            norm_power(nc, c, s, 0)
            with pool.Fori(0, NSEQ) as n:
                norm_power(nc, c, s, n + 1)

        @block.vector
        def _(dve):
            nc.vector.memset(kT[:, :, :], 0.0).then_inc(zeroed, 1)
            dve.wait_ge(c.w1_loaded, c.W1_ALL)
            norm_stats(nc, c, s, 0)
            norm_apply(nc, c, s, 0, True)

            def take_qkv(m):
                for a in range(TILES):
                    b = (6, 1)[a]
                    dve.wait_ge(qkv_in_psum, TILES * m + a + 1)
                    nc.vector.tensor_tensor(qkv[:, a, :], bank[b][:, 0:3 * D], c.bqkv1[:, :], ALU.add)\
                        .then_inc(read[b], 1)
                dve.wait_ge(logits_in_psum, m + 1)
                route_shift(nc, r, bank[2][:, 0:TILES * E1].rearrange("p (a e) -> p a e", e=E1), read[2])

            def rotate(a):
                part = qkv[:, a, :].rearrange("p (h i k o) -> p i h k o", h=H1, i=3, o=2)
                cos = c.cos1[:, a, :].rearrange("p (i h k) -> p i h k", i=2, h=H1)
                sin = c.sin1[:, a, :].rearrange("p (i h k) -> p i h k", i=2, h=H1)
                for i in range(2):
                    even, odd = part[:, i, :, :, 0], part[:, i, :, :, 1]
                    nc.vector.tensor_tensor(t1[:, i], even, cos[:, i], ALU.mult)
                    nc.vector.tensor_tensor(t2[:, i], odd, sin[:, i], ALU.mult)
                    nc.vector.tensor_tensor(t3[:, i], even, sin[:, i], ALU.mult)
                    nc.vector.tensor_tensor(t4[:, i], odd, cos[:, i], ALU.mult)
                nc.vector.drain()
                nc.vector.tensor_tensor(rot[:, a, :, :, :, 0], t1[:, :, :, :], t2[:, :, :, :], ALU.subtract)
                done = nc.vector.tensor_tensor(rot[:, a, :, :, :, 1], t3[:, :, :, :], t4[:, :, :, :], ALU.add)
                if a == TILES - 1:
                    done.then_inc(rot_ready, 1)
                nc.vector.drain()

            take_qkv(0)
            for a in range(TILES):
                rotate(a)
            with dve.Fori(0, NSEQ) as n:
                def scores_come(h):
                    if h >= RP:
                        dve.wait_ge(pT_in_psum, H1 * n + h - RP + 1)
                    dve.wait_ge(scores_in_psum, H1 * n + h + 1)

                def fuse(k, h=None):
                    b = 5 + k % 2
                    dve.wait_ge(th_ready, CH * n + k + 1)
                    nc.vector.scalar_tensor_tensor(out=gated[:, k % 2, :], in0=th[:, k % 2, :], scalar=1.0,
                                                   in1=bank[b][:, 0:T], op0=ALU.add, op1=ALU.mult)
                    nc.vector.drain()
                    if h is not None:
                        scores_come(h)
                    nc.vector.tensor_tensor(fused[:, k % 4, :], gated[:, k % 2, :], bank[b][:, T:2 * T], ALU.mult)\
                        .then_inc(read[b], 1)

                def negate_scores(h):
                    b = 1 + h % 2
                    for a, (lo, hi) in enumerate(((0, P), (P, 3 * P))):
                        done = nc.vector.tensor_tensor_reduce(
                            neg[:, h % RP, lo:hi], bank[b][:, lo:hi], c.causal[:, lo:hi], -SCALE, 3e38,
                            ALU.add, ALU.min, nmax[:, h % RP, a:a + 1])
                    done.then_inc(read[b], 1)

                def accumulate(e):
                    dve.wait_ge(down_in_psum, E1 * n + e + 1)
                    for a in range(TILES):
                        rows = bank[7][:, a * D:(a + 1) * D]
                        if e == 0:
                            done = nc.vector.tensor_scalar(acc[:, a, :], rows, comb[:, a, 0:1], None, ALU.mult)
                        else:
                            done = nc.vector.scalar_tensor_tensor(out=acc[:, a, :], in0=rows,
                                                                  scalar=comb[:, a, e:e + 1], in1=acc[:, a, :],
                                                                  op0=ALU.mult, op1=ALU.add)
                    done.then_inc(read[7], 1)

                fuse(0)
                fuse(1)
                route_best(nc, r, n)
                nc.vector.tensor_tensor(diff[:, :], r.best[:, :, 1], r.best[:, :, 0], ALU.subtract)\
                    .then_inc(diff_ready, 1)
                for k in range(H1):
                    if k + 2 < CH:
                        fuse(k + 2, k)
                    else:
                        scores_come(k)
                        nc.vector.memset(nmax[:, k % RP, :], 0.0)
                        nc.vector.drain()
                    negate_scores(k)
                    if k == 0:
                        dve.wait_ge(ediff_ready, n + 1)
                        nc.vector.tensor_scalar(ediff1[:, :], ediff[:, :], 1.0, None, ALU.add)
                        nc.vector.drain()
                        nc.vector.reciprocal(first[:, :], ediff1[:, :])
                        nc.vector.drain()
                        nc.vector.tensor_scalar(first[:, :], first[:, :], 0.5, None, ALU.mult)
                        nc.vector.drain()
                        nc.vector.tensor_tensor(second[:, :], first[:, :], ediff[:, :], ALU.mult)
                        nc.vector.drain()
                    if k == 1:
                        for a in range(TILES):
                            nc.vector.tensor_scalar(comb[:, a, :], c.iota8[:, :], r.place[:, a, 0:1], first[:, a:a + 1],
                                                    ALU.is_equal, ALU.mult)
                            nc.vector.tensor_scalar(comb2[:, a, :], c.iota8[:, :], r.place[:, a, 1:2], second[:, a:a + 1],
                                                    ALU.is_equal, ALU.mult)
                        nc.vector.drain()
                        nc.vector.tensor_tensor(comb[:, :, :], comb[:, :, :], comb2[:, :, :], ALU.add)
                        nc.vector.drain()
                    if k == 2:
                        norm_stats(nc, c, s, n + 1)
                    if k == 5:
                        norm_apply(nc, c, s, n + 1, False)
                    if k >= 2 and k % 2 == 0:
                        accumulate(k // 2 - 1)
                accumulate(E1 - 1)
                nc.vector.drain().then_inc(acc_ready, 1)
                nc.vector.wait_ge(exp_ready, H1 * n + H1)
                nc.vector.reciprocal(recip[:, :, :], total[:, :, :])
                nc.vector.drain()
                dve.wait_ge(head_done, H1 * n + H1)
                nc.vector.tensor_tensor(y[:, :, :].rearrange("p a (h v) -> p (a h) v", v=HD1),
                                        bank[0][:, 0:TILES * D].rearrange("p (g v) -> p g v", v=HD1),
                                        bcast(recip[:, :, :].rearrange("p a h -> p (a h)"), HD1), ALU.mult)\
                    .then_inc(read[0], 1)
                nc.vector.drain().then_inc(y_ready, 1)
                take_qkv(n + 1)
                rotate(0)
                dve.wait_ge(s_in_psum, n + 1)
                nc.vector.tensor_tensor(s_out[:, :, :], bank[0][:, 0:TILES * D].rearrange("p (a d) -> p a d", d=D),
                                        c.bproj1[:, :].unsqueeze(1).to_broadcast([P, TILES, D]), ALU.add)\
                    .then_inc(read[0], 1)
                rotate(1)
                dve.wait_ge(th_z_ready, n + 1)
                close_layer(nc, c, n, s_out[:, :, :], acc[:, :, :], th_z[:, :, :], u[:, :, :])


def layer2(nc, c):
    with ExitStack() as ctx:
        def sb(name, shape, dtype=F32):
            return ctx.enter_context(nc.sbuf_tensor("c2_" + name, shape, dtype))

        def sem(name):
            return layer_semaphore(nc, "l2_" + name)

        c.ones = sb("ones", [P, T])
        bank = [ctx.enter_context(nc.psum_tensor(f"l2_bank{i}", [P, 512], F32)) for i in range(7)]
        KF = F2 // P
        wT = sb("wT", [P, 4, P])
        proj = sb("proj", [P, 4, P])
        brow = sb("brow", [P, 4, P])
        bcol = sb("bcol", [P, 4])
        nbeta = sb("nbeta", [P, 1])
        qk = sb("qk", [P, 2, T])
        kvk = sb("kvk", [P, 3, T])
        cum = sb("cum", [P, 3, T])
        qcum = sb("qcum", [P, 3, T])
        rden = sb("rden", [P, T])
        attT = sb("attT", [P, T])
        s_out = sb("s_out", [P, TILES, D])
        r = RouteBuffers(sb, sem)
        mask = sb("mask", [P, TILES, E2])
        kept = sb("kept", [P, TILES, E2])
        seen = sb("seen", [P, E2])
        comb = sb("comb", [P, TILES, E2])
        combT = sb("combT", [E2, T])
        hid = sb("hid", [P, 2, KF, T])
        acc = sb("acc", [P, TILES, D])
        th_z = sb("th_z", [P, TILES, D])
        u = sb("u", [P, TILES, D])

        s = NormSems(sem, "n")
        read = [sem(f"bank{i}_read") for i in range(7)]
        PER0 = 5
        PERU = E2
        PER3 = E2 + 1
        weights_turned = sem("weights_turned")
        weights_copied = sem("weights_copied")
        biases_turned = sem("biases_turned")
        attention_ready = sem("attention_weights_ready")
        beta_exp = sem("beta_exp")
        logits_in_psum = sem("logits_in_psum")
        mask_ready = sem("mask_ready")
        count_in_psum = sem("count_in_psum")
        comb_ready = sem("comb_ready")
        combT_in_psum = sem("combT_in_psum")
        qk_in_psum = sem("qk_in_psum")
        v_in_psum = sem("v_in_psum")
        qcum_ready = sem("qcum_ready")
        att_in_psum = sem("att_in_psum")
        attT_ready = sem("attT_ready")
        s_in_psum = sem("s_in_psum")
        hidden_in_psum = sem("hidden_in_psum")
        down_in_psum = sem("down_in_psum")
        acc_ready = sem("acc_ready")
        th_z_ready = sem("th_z_ready")

        block = ctx.enter_context(nc.Block())

        @block.sync
        def _(sp):
            with nc.allow_non_contiguous_dma("columns of small parameters"):
                for dst, src in c.w3_loads:
                    sp.dma_start(dst, src).then_inc(c.w3_loaded, 16)

        @block.tensor
        def _(pe):
            for i in range(1, 7):
                pe.sem_inc(read[i], 1)
            pe.wait_ge(c.w2_loaded, c.W2_ALL)
            for i, name in enumerate(("Wq", "Wk", "Wv", "Wo")):
                done = nc.tensor.transpose(bank[1][:, i * P:(i + 1) * P], c.w2[name][:, :], c.ident[:, :])
            done.then_inc(weights_turned, 1)
            pe.wait_ge(weights_copied, 1)
            for i in range(4):
                done = nc.tensor.transpose(bank[2][:, i * P:(i + 1) * P], brow[:, i, :], c.ident[:, :])
            done.then_inc(biases_turned, 1)
            norm_transpose(nc, c, s, 0, bank[0])
            pe.wait_ge(attention_ready, 1)
            with pe.Fori(0, NSEQ) as n:
                pe.wait_ge(read[0], PER0 * n + 1)
                for a in range(TILES):
                    done = nc.tensor.matmul(bank[0][:, a * E2:(a + 1) * E2], c.xnT[:, a * P:(a + 1) * P],
                                            c.wg2[:, :], start=True, stop=True)
                done.then_inc(logits_in_psum, 1)
                for b, lo, ready in ((4, 0, qk_in_psum), (5, 2, v_in_psum)):
                    pe.wait_ge(read[b], n + 1)
                    for i in range(2):
                        done = nc.tensor.matmul(bank[b][:, i * T:(i + 1) * T], proj[:, lo + i, :], c.xnT[:, :],
                                                start=True, stop=True)
                    done.then_inc(ready, 1)

                def up(e):
                    for b in range(2):
                        pe.wait_ge(read[1 + b], PERU * n + e + 1)
                        for i in range(2):
                            k = 2 * b + i
                            done = nc.tensor.matmul(bank[1 + b][:, i * T:(i + 1) * T],
                                                    c.w12[:, e, k * P:(k + 1) * P], c.xnT[:, :],
                                                    start=True, stop=True)
                        done.then_inc(hidden_in_psum, 1)

                def down(e):
                    pe.wait_ge(read[1], PERU * n + e + 2)
                    pe.wait_ge(read[2], PERU * n + e + 2)
                    pe.wait_ge(read[3], PER3 * n + e + 1)
                    for a in range(TILES):
                        for k in range(KF):
                            done = nc.tensor.matmul(bank[3][:, a * D:(a + 1) * D],
                                                    hid[:, e % 2, k, a * P:(a + 1) * P], c.w22[:, e, k, :],
                                                    start=(k == 0), stop=(k == KF - 1))
                    done.then_inc(down_in_psum, 1)

                up(0)
                up(1)
                pe.wait_ge(mask_ready, n + 1)
                pe.wait_ge(read[0], PER0 * n + 2)
                nc.tensor.matmul(bank[0][:, 0:E2], c.until[:, :], mask[:, 0, :], start=True, stop=True)
                nc.tensor.matmul(bank[0][:, E2:2 * E2], c.ones[:, 0:P], mask[:, 0, :], start=True, stop=False)
                nc.tensor.matmul(bank[0][:, E2:2 * E2], c.until[:, :], mask[:, 1, :], start=False, stop=True)
                nc.tensor.matmul(bank[0][:, 2 * E2:3 * E2], c.ones[:, 0:P], mask[:, 0, :], start=True, stop=False)
                nc.tensor.matmul(bank[0][:, 2 * E2:3 * E2], c.ones[:, 0:P], mask[:, 1, :], start=False, stop=True)\
                    .then_inc(count_in_psum, 1)
                for e in range(E2):
                    down(e)
                    if e + 2 < E2:
                        up(e + 2)
                    if e == 2:
                        pe.wait_ge(qcum_ready, n + 1)
                        pe.wait_ge(read[6], n + 1)
                        nc.tensor.matmul(bank[6][:, 0:T], c.same_head[:, 0, :], qcum[:, 0, :], start=True, stop=False)
                        nc.tensor.matmul(bank[6][:, 0:T], c.same_head[:, 1, :], qcum[:, 1, :], start=False, stop=True)
                        nc.tensor.matmul(bank[6][:, T:2 * T], c.same_head[:, 2, :], qcum[:, 2, :],
                                         start=True, stop=True).then_inc(att_in_psum, 1)
                    if e == 3:
                        pe.wait_ge(comb_ready, n + 1)
                        pe.wait_ge(read[0], PER0 * n + 3)
                        for a in range(TILES):
                            done = nc.tensor.transpose(bank[0][0:E2, a * P:(a + 1) * P], comb[:, a, :], c.ident[:, :])
                        done.then_inc(combT_in_psum, 1)
                    if e == 5:
                        pe.wait_ge(attT_ready, n + 1)
                        pe.wait_ge(read[0], PER0 * n + 4)
                        for a in range(TILES):
                            done = nc.tensor.matmul(bank[0][:, a * D:(a + 1) * D], attT[:, a * P:(a + 1) * P],
                                                    wT[:, 3, :], start=True, stop=True)
                        done.then_inc(s_in_psum, 1)
                    if e == 6:
                        pe.wait_ge(read[0], PER0 * n + 5)
                        norm_transpose(nc, c, s, n + 1, bank[0])
                pe.wait_ge(read[3], PER3 * n + E2 + 1)
                for a in range(TILES):
                    done = nc.tensor.matmul(bank[3][:, a * D:(a + 1) * D], combT[:, a * P:(a + 1) * P], c.b22[:, :],
                                            start=True, stop=True)
                done.then_inc(down_in_psum, 1)

        @block.scalar
        def _(act):
            act.wait_ge(c.w2_loaded, c.W2_ALL)
            nc.scalar.activation(c.beta[:, :], c.beta[:, :], ACT.Exp).then_inc(beta_exp, 1)
            norm_copy(nc, c, s, 0, bank[0], read[0])
            act.wait_ge(attention_ready, 1)
            with act.Fori(0, NSEQ) as n:
                route_exp(nc, r, n)
                act.wait_ge(qk_in_psum, n + 1)
                for i in range(2):
                    done = nc.scalar.activation(qk[:, i, :], bank[4][:, i * T:(i + 1) * T], ACT.Exp,
                                                bias=bcol[:, i:i + 1], scale=nbeta[:, 0:1])
                done.then_inc(read[4], 1)

                def gelu(e):
                    if e >= 2:
                        act.wait_ge(down_in_psum, PER3 * n + e - 1)
                    for b in range(2):
                        act.wait_ge(hidden_in_psum, 2 * E2 * n + 2 * e + b + 1)
                        for i in range(2):
                            k = 2 * b + i
                            done = nc.scalar.activation(hid[:, e % 2, k, :], bank[1 + b][:, i * T:(i + 1) * T],
                                                        ACT.Gelu_apprx_tanh, bias=c.b12[:, e, k:k + 1])
                        done.then_inc(read[1 + b], 1)

                for e in range(E2):
                    gelu(e)
                    if e == 5:
                        act.wait_ge(combT_in_psum, n + 1)
                        nc.scalar.activation(combT[:, :], bank[0][0:E2, 0:T], ACT.Copy).then_inc(read[0], 1)
                norm_copy(nc, c, s, n + 1, bank[0], read[0])
                act.wait_ge(acc_ready, n + 1)
                nc.scalar.activation(th_z[:, :, :], acc[:, :, :], ACT.Tanh, scale=0.5).then_inc(th_z_ready, 1)

        @block.gpsimd
        def _(pool):
            norm_power(nc, c, s, 0)
            with pool.Fori(0, NSEQ) as n:
                norm_power(nc, c, s, n + 1)

        @block.vector
        def _(dve):
            v = nc.vector
            v.memset(seen[:, :], 0.0)
            v.memset(c.ones[:, :], 1.0)
            dve.wait_ge(weights_turned, 1)
            v.tensor_copy(wT[:, :, :], bank[1][:, :].rearrange("p (i d) -> p i d", i=4))
            v.drain()
            for dst, src in ((proj, [wT[:, i, :] for i in range(3)]),
                             (brow, [c.w2[name][:, :] for name in ("bq", "bk", "bv")])):
                for i in range(2):
                    pair = src[i].rearrange("p (h o) -> p h o", o=2)
                    out = dst[:, i, :].rearrange("p (h o) -> p h o", o=2)
                    v.tensor_tensor(out[:, :, 0], pair[:, :, 0], pair[:, :, 1], ALU.subtract)
                    v.tensor_tensor(out[:, :, 1], pair[:, :, 1], pair[:, :, 0], ALU.subtract)
                pair = src[2].rearrange("p (h o) -> p h o", o=2)
                for i in range(2):
                    v.tensor_copy(dst[:, 2 + i, :].rearrange("p (h o) -> p h o", o=2), bcast(pair[:, :, i], 2))
            v.drain().then_inc(weights_copied, 1)
            dve.wait_ge(beta_exp, 1)
            v.tensor_scalar(nbeta[:, :], c.beta[:, :], -1.0, None, ALU.mult)
            v.drain()
            dve.wait_ge(biases_turned, 1)
            for i in range(4):
                col = bank[2][:, i * P:i * P + 1]
                if i < 2:
                    v.tensor_scalar(bcol[:, i:i + 1], col, nbeta[:, 0:1], None, ALU.mult)
                else:
                    v.tensor_copy(bcol[:, i:i + 1], col)
            v.drain().then_inc(attention_ready, 2)
            norm_stats(nc, c, s, 0)
            norm_apply(nc, c, s, 0, True)
            with dve.Fori(0, NSEQ) as n:
                dve.wait_ge(logits_in_psum, n + 1)
                route_shift(nc, r, bank[0][:, 0:TILES * E2].rearrange("p (a e) -> p a e", e=E2), read[0])
                route_best(nc, r, n)
                v.drain()
                for a in range(TILES):
                    v.tensor_scalar(mask[:, a, :], c.iota8[:, :], r.place[:, a, 0:1], None, ALU.is_equal)
                v.drain().then_inc(mask_ready, 1)
                dve.wait_ge(read[4], n + 2)
                v.tensor_scalar(qk[:, :, :], qk[:, :, :], 1.0, None, ALU.add)
                v.drain()
                v.reciprocal(qk[:, :, :], qk[:, :, :])
                v.drain()
                dve.wait_ge(v_in_psum, n + 1)
                for i in range(2):
                    done = v.scalar_tensor_tensor(out=kvk[:, i, :], in0=bank[5][:, i * T:(i + 1) * T],
                                                  scalar=bcol[:, 2 + i:3 + i], in1=qk[:, 1, :],
                                                  op0=ALU.add, op1=ALU.mult)
                done.then_inc(read[5], 1)
                v.drain()
                for i in range(3):
                    v.tensor_tensor_scan(cum[:, i, :], c.ones[:, :], kvk[:, i, :] if i < 2 else qk[:, 1, :], 0.0,
                                         ALU.mult, ALU.add)
                v.drain()
                dve.wait_ge(count_in_psum, n + 1)
                count = bank[0][:, 0:TILES * E2].rearrange("p (a e) -> p a e", e=E2)
                v.tensor_tensor(kept[:, :, :], count, seen[:, :].unsqueeze(1).to_broadcast([P, TILES, E2]), ALU.add)
                v.drain()
                v.tensor_tensor(seen[:, :], seen[:, :], bank[0][:, 2 * E2:3 * E2], ALU.add).then_inc(read[0], 1)
                v.tensor_scalar(kept[:, :, :], kept[:, :, :], float(CAP2), None, ALU.is_le)
                v.drain()
                v.tensor_tensor(kept[:, :, :], kept[:, :, :], mask[:, :, :], ALU.mult)
                v.drain()
                v.tensor_tensor(comb[:, :, :], kept[:, :, :], r.probs[:, :, :], ALU.mult)
                v.drain().then_inc(comb_ready, 1)
                for i in range(3):
                    v.tensor_tensor(qcum[:, i, :], cum[:, i, :], qk[:, 0, :], ALU.mult)
                v.drain().then_inc(qcum_ready, 1)
                norm_stats(nc, c, s, n + 1)

                def add_expert(e):
                    dve.wait_ge(down_in_psum, PER3 * n + e + 1)
                    for a in range(TILES):
                        rows = bank[3][:, a * D:(a + 1) * D]
                        if e == 0:
                            done = v.tensor_scalar(acc[:, a, :], rows, comb[:, a, 0:1], None, ALU.mult)
                        else:
                            done = v.scalar_tensor_tensor(out=acc[:, a, :], in0=rows, scalar=comb[:, a, e:e + 1],
                                                          in1=acc[:, a, :], op0=ALU.mult, op1=ALU.add)
                    done.then_inc(read[3], 1)

                for e in range(E2):
                    add_expert(e)
                    if e == 2:
                        norm_apply(nc, c, s, n + 1, False)
                    if e == 3:
                        dve.wait_ge(att_in_psum, n + 1)
                        v.reciprocal(rden[:, :], bank[6][:, T:2 * T])
                        v.drain()
                        v.tensor_tensor(attT[:, :], bank[6][:, 0:T], rden[:, :], ALU.mult).then_inc(read[6], 1)
                        v.drain().then_inc(attT_ready, 1)
                    if e == 5:
                        dve.wait_ge(s_in_psum, n + 1)
                        v.tensor_tensor(s_out[:, :, :], bank[0][:, 0:TILES * D].rearrange("p (a d) -> p a d", d=D),
                                        c.w2["bo"][:, :].unsqueeze(1).to_broadcast([P, TILES, D]), ALU.add)\
                            .then_inc(read[0], 1)
                dve.wait_ge(down_in_psum, PER3 * n + PER3)
                v.tensor_tensor(acc[:, :, :], bank[3][:, 0:TILES * D].rearrange("p (a d) -> p a d", d=D),
                                acc[:, :, :], ALU.add).then_inc(read[3], 1)
                v.drain().then_inc(acc_ready, 1)
                dve.wait_ge(th_z_ready, n + 1)
                close_layer(nc, c, n, s_out[:, :, :], acc[:, :, :], th_z[:, :, :], u[:, :, :])


def layer3_weights(nc, ctx, A, c):
    def sb(name, shape):
        return ctx.enter_context(nc.sbuf_tensor("w3_" + name, shape, F32))

    w = c.w3 = Core()
    w.in_proj = sb("in_proj", [P, 2 * CI, D])
    w.x_proj = sb("x_proj", [RANK + 2 * NS, DI])
    w.dt_proj = sb("dt_proj", [P, CI, RANK])
    w.out_proj = sb("out_proj", [P, DI])
    w.conv, w.conv_b = sb("conv", [P, CI, DCONV]), sb("conv_b", [P, CI])
    w.dt_b, w.A_log, w.skip = sb("dt_b", [P, CI]), sb("A_log", [P, CI, NS]), sb("skip", [P, CI])
    w.qkv, w.bqkv = sb("qkv", [P, 3, D]), sb("bqkv", [P, 3, D])
    w.o, w.bo = sb("o", [P, D]), sb("bo", [P, D])
    w.g, w.bg = sb("g", [P, E3]), sb("bg", [P, E3])
    w.w1, w.b1 = sb("w1", [P, E3, F3]), sb("b1", [P, E3, F3 // P])
    w.w2, w.b2 = sb("w2", [P, E3, F3 // P, D]), sb("b2", [E3, D])
    w.g1, w.be1, w.g2, w.be2 = (sb(name, [P, D]) for name in ("g1", "be1", "g2", "be2"))
    c.w3_loaded = ctx.enter_context(nc.semaphore("w3_loaded"))
    a, f = "L3_attn_", "L3_ffn_"
    c.w3_loads = [
        (w.in_proj[:, :, :], A[a + "in_proj_w"].rearrange("(c p) d -> p c d", p=P)),
        (w.x_proj[:, :], A[a + "x_proj_w"]),
        (w.dt_proj[:, :, :], A[a + "dt_proj_w"].rearrange("(c p) r -> p c r", p=P)),
        (w.out_proj[:, :], A[a + "out_proj_w"]),
        (w.conv[:, :, :], A[a + "conv_w"].rearrange("(c p) k -> p c k", p=P)),
        (w.conv_b[:, :], A[a + "conv_b"].rearrange("(c p) -> p c", p=P)),
        (w.dt_b[:, :], A[a + "dt_proj_b"].rearrange("(c p) -> p c", p=P)),
        (w.A_log[:, :, :], A[a + "A_log"].rearrange("(c p) s -> p c s", p=P)),
        (w.skip[:, :], A[a + "D"].rearrange("(c p) -> p c", p=P)),
        (w.o[:, :], A[f + "Wo"]), (w.g[:, :], A[f + "Wg"]),
        (w.w1[:, :, :], A[f + "W1"].rearrange("e d f -> d e f")),
        (w.b1[:, :, :], A[f + "b1"].rearrange("e (k p) -> p e k", p=P)),
        (w.w2[:, :, :, :], A[f + "W2"].rearrange("e (k p) d -> p e k d", p=P)),
        (w.b2[:, :], A[f + "b2"])]
    for i, name in enumerate("qkv"):
        c.w3_loads += [(w.qkv[:, i, :], A[f + "W" + name]),
                       (w.bqkv[:, i, :], A[f + "b" + name].partition_broadcast(P))]
    for dst, name in ((w.bo, "bo"), (w.bg, "bg"), (w.g1, "g1"), (w.be1, "be1"), (w.g2, "g2"), (w.be2, "be2")):
        c.w3_loads.append((dst[:, :], A[f + name].partition_broadcast(P)))
    c.W3_ALL = 16 * len(c.w3_loads)


def layer3(nc, c):
    w = c.w3
    with ExitStack() as ctx:
        def sb(name, shape, dtype=F32):
            return ctx.enter_context(nc.sbuf_tensor("d3_" + name, shape, dtype))

        def sem(name):
            return layer_semaphore(nc, "l3_" + name)

        bank = [ctx.enter_context(nc.psum_tensor(f"l3_bank{i}", [P, 512], F32)) for i in range(8)]
        KF = F3 // P
        PAIRS = NS // 2
        XD = RANK + 2 * NS
        RP = 2
        NBLK = H3 // GR
        F32R = mybir.dt.float32r
        in_projT = sb("in_projT", [P, 2 * CI, P])
        x_projT = sb("x_projT", [P, CI, P])
        dt_projT = sb("dt_projT", [RANK, CI, P])
        out_projT = sb("out_projT", [P, CI, D])
        negA = sb("negA", [P, CI, NS])
        hconv_b = sb("hconv_b", [P, CI])
        upad = sb("upad", [P, CI, DCONV - 1 + T])
        z = sb("z", [P, CI, T])
        zg = sb("zg", [P, CI, T])
        xs = sb("xs", [P, CI, T])
        tmp = sb("tmp", [P, CI, T])
        xdbl = sb("xdbl", [RANK, T])
        bc = sb("bc", [P, T], F32R)
        pick = sb("pick", [P, 2 * NS], F32R)
        dv = sb("dv", [P, CI, T])
        dneg = sb("dneg", [P, CI, T])
        delta = sb("delta", [P, CI, T])
        du = sb("du", [P, CI, T])
        dA = [c.w12[:, :, :].rearrange("p e f -> p (e f)").rearrange("p (s t) -> p s t", t=T),
              c.w22[:, :, :, :].rearrange("p e k d -> p (e k d)").rearrange("p (s t) -> p s t", t=T)]
        st = [sb(f"state{i}", [P, NS, T]) for i in range(CI)]
        qkv = delta
        rot = du[:, :, :].rearrange("p a (i h o k) -> p a i h o k", i=2, h=H3, o=2)
        scratch = dv[:, :, :].rearrange("p a (b i h k) -> p (a b) i h k", b=2, i=2, h=H3)
        t1, t2, t3, t4 = (scratch[:, i] for i in range(4))
        parts = sb("parts", [P, TILES, 2, H3 * ROWS], F32R)
        kS = sb("kS", [P, NBLK, T], F32R)
        qS = sb("qS", [P, H3, T], F32R)
        identR = sb("identR", [P, P], F32R)
        nmax = sb("nmax", [P, TILES, H3])
        nmaxT = sb("nmaxT", [H3, T], F32R)
        late = parts[:, :, :, :].bitcast(F32).rearrange("p a i (k t) -> p (a i k) t", t=T)
        probs = late[:, 0:2 * RP, :].rearrange("p (r j) t -> p r (j t)", r=RP)
        vaug = sb("vaug", [P, TILES, H3, ROWS])
        oS = late[:, 2 * RP:, :]
        recip = sb("recip", [P, TILES, H3])
        y = sb("y", [P, TILES, D])
        x1 = sb("x1", [P, TILES, D])
        x1T = sb("x1T", [P, T])
        yT = x1T
        rows = sb("rows", [P, TILES, D])
        stats = sb("stats", [P, TILES, 6])
        meanvar = sb("meanvar", [P, TILES, 2])
        var_eps = sb("var_eps", [P, TILES])
        rstd = sb("rstd", [P, TILES])
        r = RouteBuffers(sb, sem)
        psum2 = sb("psum2", [P, TILES])
        first = sb("first", [P, TILES])
        second = sb("second", [P, TILES])
        comb = sb("comb", [P, TILES, E3])
        comb2 = sb("comb2", [P, TILES, E3])
        combT = y[0:E3, :, :].rearrange("p a d -> p (a d)")
        hid = sb("hid", [P, 2, KF, T])
        ym = tmp
        acc, s_out, th_z, u = (x[:, i, :].rearrange("p (a d) -> p a d", a=TILES) for x in (dneg, dv) for i in range(2))

        s = NormSems(sem, "n")
        read = [sem(f"bank{i}_read") for i in range(8)]
        PER0 = 12
        PER12 = 17
        PER34 = 3
        PER56 = 8
        PER7 = 11
        weights_turned = sem("weights_turned")
        weights_ready = sem("weights_ready")
        a_exp = sem("a_exp")
        qkv_in_psum = sem("qkv_in_psum")
        u_in_psum = sem("u_in_psum")
        z_in_psum = sem("z_in_psum")
        z_exp = sem("z_exp")
        rot_ready = sem("rot_ready")
        qkT_in_psum = sem("qkT_in_psum")
        scores_in_psum = sem("scores_in_psum")
        max_ready = sem("max_ready")
        maxT_in_psum = sem("maxT_in_psum")
        pT_in_psum = sem("pT_in_psum")
        probs_ready = sem("probs_ready")
        head_done = sem("head_done")
        o_turned = sem("o_turned")
        bc_rounded = sem("bc_rounded")
        conv_ready = sem("conv_ready")
        conv_tanh = sem("conv_tanh")
        xs_ready = sem("xs_ready")
        xdbl_in_psum = sem("xdbl_in_psum")
        dt_in_psum = sem("dt_in_psum")
        dneg_ready = sem("dneg_ready")
        dlog_ready = sem("dlog_ready")
        delta_ready = sem("delta_ready")
        dA_ready = sem("dA_ready")
        bc_in_psum = sem("bc_in_psum")
        cstate_ready = sem("cstate_ready")
        sum_ready = sem("sum_ready")
        y_ready = sem("y_ready")
        yT_in_psum = sem("yT_in_psum")
        o_in_psum = sem("o_in_psum")
        var_ready = sem("var_ready")
        rstd_ready = sem("rstd_ready")
        x1_ready = sem("x1_ready")
        x1T_in_psum = sem("x1T_in_psum")
        logits_in_psum = sem("logits_in_psum")
        comb_ready = sem("comb_ready")
        combT_in_psum = sem("combT_in_psum")
        hidden_in_psum = sem("hidden_in_psum")
        down_in_psum = sem("down_in_psum")
        ym_ready = sem("ym_ready")
        s_in_psum = sem("s_in_psum")
        gate_ready = sem("gate_ready")
        th_z_ready = sem("th_z_ready")

        block = ctx.enter_context(nc.Block())

        @block.tensor
        def _(pe):
            for i in range(1, 8):
                pe.sem_inc(read[i], 1)
            pe.wait_ge(c.w3_loaded, c.W3_ALL)
            for i in range(2 * CI):
                nc.tensor.transpose(bank[1][:, i * P:(i + 1) * P], w.in_proj[:, i, :], c.ident[:, :])
            for i in range(CI):
                nc.tensor.transpose(bank[2][:, i * XD:(i + 1) * XD], w.x_proj[:, i * P:(i + 1) * P],
                                    c.ident[0:XD, 0:XD])
                nc.tensor.transpose(bank[3][0:RANK, i * P:(i + 1) * P], w.dt_proj[:, i, :], c.ident[:, :])
                done = nc.tensor.transpose(bank[4][:, i * D:(i + 1) * D], w.out_proj[:, i * P:(i + 1) * P],
                                           c.ident[:, :])
            done.then_inc(weights_turned, 1)
            norm_transpose(nc, c, s, 0, bank[0])
            wqkv = w.qkv[:, :, :].rearrange("p i d -> p (i d)")

            def qkv_rows(a, begin):
                pe.wait_ge(read[0], begin)
                nc.tensor.matmul(bank[0][:, 0:3 * D], c.xnT[:, a * P:(a + 1) * P], wqkv, start=True, stop=True)\
                    .then_inc(qkv_in_psum, 1)

            for a in range(TILES):
                qkv_rows(a, a + 1)
            pe.wait_ge(weights_ready, 1)

            def project(m, part):
                pe.wait_ge(read[3 + part], PER34 * m + 1)
                for i in range(CI):
                    done = nc.tensor.matmul(bank[3 + part][:, i * T:(i + 1) * T],
                                            in_projT[:, CI * (1 - part) + i, :], c.xnT[:, :],
                                            start=True, stop=True)
                done.then_inc((z_in_psum, u_in_psum)[part], 1)

            project(0, 1)
            with pe.Fori(0, NSEQ) as n:
                project(n, 0)

                def scores(h):
                    b = 1 + h % 2
                    pe.wait_ge(read[b], PER12 * n + h // 2 + 2)
                    for a in range(TILES):
                        done = nc.tensor.matmul(bank[b][:, a * T:(a + 1) * T], qS[:, h, a * P:(a + 1) * P],
                                                kS[:, h // GR, :], start=True, stop=True)
                    done.then_inc(scores_in_psum, 1)

                def scoresT(h):
                    b = 3 + h % 2
                    if h < 2:
                        pe.wait_ge(read[b], PER34 * n + 3)
                    else:
                        pe.wait_ge(probs_ready, H3 * n + h - 1)
                    for j in range(2):
                        nc.tensor.matmul(bank[b][:, j * T:(j + 1) * T], kS[:, h // GR, j * P:(j + 1) * P],
                                         qS[:, h, :], start=True, stop=False)
                        done = nc.tensor.matmul(bank[b][:, j * T:(j + 1) * T],
                                                identR[0:H3, h:h + 1].to_broadcast([H3, P]), nmaxT[:, :],
                                                start=False, stop=True)
                    done.then_inc(pT_in_psum, 1)

                def head_out(h):
                    if h % (H3 // 2) == 0:
                        pe.wait_ge(read[7], PER7 * n + h // (H3 // 2) + 1)
                    pe.wait_ge(probs_ready, H3 * n + h + 1)
                    rows, cols = ROWS * (h % GR), T * (h // GR % 2)
                    for j in range(2):
                        done = nc.tensor.matmul(bank[7][rows:rows + ROWS, cols:cols + T], vaug[:, j, h, :],
                                                probs[:, h % RP, j * T:(j + 1) * T],
                                                start=(j == 0), stop=(j == 1), tile_position=(0, rows))
                    done.then_inc(head_done, 1)

                def spread(j):
                    b = 5 + j % 2
                    pe.wait_ge(read[b], PER56 * n + j // 2 + 1)
                    for i in range(2):
                        row = 2 * j + i
                        done = nc.tensor.matmul(bank[b][:, i * T:(i + 1) * T],
                                                pick[:, row:row + 1].to_broadcast([P, P]), bc[:, :],
                                                start=True, stop=True)
                    done.then_inc(bc_in_psum, 1)

                pe.wait_ge(rot_ready, n + 1)
                for i in range(2):
                    for k in range(2):
                        if i == 0:
                            pe.wait_ge(read[1 + k], PER12 * n + 1)
                        else:
                            pe.wait_ge(read[3 + k], PER34 * n + 2)
                    for j in range(NBLK):
                        for a in range(TILES):
                            cols = slice(j % 2 * T + a * P, j % 2 * T + (a + 1) * P)
                            done = nc.tensor.transpose(bank[(1, 3)[i] + j // 2][:, cols],
                                                       parts[:, a, i, j * P:(j + 1) * P].bitcast(F32),
                                                       c.ident[:, :])
                    done.then_inc(qkT_in_psum, 1)
                pe.wait_ge(read[2], PER12 * n + 2)
                pe.wait_ge(read[3], PER34 * n + 3)
                pe.wait_ge(read[4], PER34 * n + 3)
                for h in range(H3):
                    scores(h)
                    if h == 1:
                        pe.wait_ge(xs_ready, n + 1)
                        pe.wait_ge(read[0], PER0 * n + 3)
                        for i in range(CI):
                            done = nc.tensor.matmul(bank[0][:, 0:T], x_projT[:, i, :], xs[:, i, :],
                                                    start=(i == 0), stop=(i == CI - 1))
                        done.then_inc(xdbl_in_psum, 1)
                    if h == 4:
                        pe.wait_ge(read[0], PER0 * n + 4)
                        for i in range(CI):
                            done = nc.tensor.matmul(bank[0][:, i * T:(i + 1) * T], dt_projT[:, i, :], xdbl[:, :],
                                                    start=True, stop=True)
                        done.then_inc(dt_in_psum, 1)
                pe.wait_ge(max_ready, n + 1)
                pe.wait_ge(read[0], PER0 * n + 5)
                for a in range(TILES):
                    done = nc.tensor.transpose(bank[0][0:H3, a * P:(a + 1) * P], nmax[:, a, :], c.ident[:, :])
                done.then_inc(maxT_in_psum, 1)
                spread(0)
                spread(1)
                pe.wait_ge(read[0], PER0 * n + 6)
                for k in range(H3 + 1):
                    if k < H3:
                        scoresT(k)
                    if k + 2 < PAIRS:
                        spread(k + 2)
                    if k >= 1:
                        head_out(k - 1)
                    if k in (7, 8, 12, 13):
                        spread(PAIRS + (7, 8, 12, 13).index(k))
                pe.wait_ge(read[7], PER7 * n + 3)
                for a in range(TILES):
                    pe.wait_ge(read[3 + a], PER34 * n + 3)
                    for j in range(NBLK):
                        done = nc.tensor.transpose(bank[3 + a][:, j * P:(j + 1) * P], oS[:, j, a * P:(a + 1) * P],
                                                   c.ident[:, :])
                done.then_inc(o_turned, 1)
                pe.wait_ge(y_ready, n + 1)
                pe.wait_ge(read[0], PER0 * n + 6)
                for a in range(TILES):
                    done = nc.tensor.transpose(bank[0][:, a * P:(a + 1) * P], y[:, a, :], c.ident[:, :])
                done.then_inc(yT_in_psum, 1)
                pe.wait_ge(read[0], PER0 * n + 7)
                for a in range(TILES):
                    done = nc.tensor.matmul(bank[0][:, a * D:(a + 1) * D], yT[:, a * P:(a + 1) * P], w.o[:, :],
                                            start=True, stop=True)
                done.then_inc(o_in_psum, 1)
                spread(PAIRS + 4)
                spread(PAIRS + 5)

                pe.wait_ge(x1_ready, n + 1)
                pe.wait_ge(read[0], PER0 * n + 8)
                for a in range(TILES):
                    done = nc.tensor.transpose(bank[0][:, a * P:(a + 1) * P], x1[:, a, :], c.ident[:, :])
                done.then_inc(x1T_in_psum, 1)
                pe.wait_ge(read[0], PER0 * n + 9)
                for a in range(TILES):
                    done = nc.tensor.matmul(bank[0][:, a * E3:(a + 1) * E3], x1T[:, a * P:(a + 1) * P], w.g[:, :],
                                            start=True, stop=True)
                done.then_inc(logits_in_psum, 1)

                def up(e):
                    for b in range(2):
                        pe.wait_ge(read[1 + b], PER12 * n + 9 + e + 1)
                        for i in range(2):
                            k = 2 * b + i
                            done = nc.tensor.matmul(bank[1 + b][:, i * T:(i + 1) * T],
                                                    w.w1[:, e, k * P:(k + 1) * P], x1T[:, :], start=True, stop=True)
                        done.then_inc(hidden_in_psum, 1)

                def down(e):
                    pe.wait_ge(read[1], PER12 * n + 9 + e + 2)
                    pe.wait_ge(read[2], PER12 * n + 9 + e + 2)
                    pe.wait_ge(read[7], PER7 * n + e + 3)
                    for a in range(TILES):
                        for k in range(KF):
                            done = nc.tensor.matmul(bank[7][:, a * D:(a + 1) * D],
                                                    hid[:, e % 2, k, a * P:(a + 1) * P], w.w2[:, e, k, :],
                                                    start=(k == 0), stop=(k == KF - 1))
                    done.then_inc(down_in_psum, 1)

                up(0)
                up(1)
                for e in range(E3):
                    down(e)
                    if e + 2 < E3:
                        up(e + 2)
                    if e < 2:
                        spread(PAIRS + 6 + e)
                    if e == 2:
                        pe.wait_ge(read[0], PER0 * n + 10)
                        norm_transpose(nc, c, s, n + 1, bank[0])
                    if e in (4, 5):
                        qkv_rows(e - 4, PER0 * n + 11 + e - 4)
                    if e == 5:
                        project(n + 1, 1)
                    if e == 6:
                        pe.wait_ge(comb_ready, n + 1)
                        pe.wait_ge(read[0], PER0 * n + 13)
                        for a in range(TILES):
                            done = nc.tensor.transpose(bank[0][0:E3, a * P:(a + 1) * P], comb[:, a, :], c.ident[:, :])
                        done.then_inc(combT_in_psum, 1)
                pe.wait_ge(read[0], PER0 * n + 14)
                pe.wait_ge(read[7], PER7 * n + 11)
                for a in range(TILES):
                    done = nc.tensor.matmul(bank[7][:, a * D:(a + 1) * D], combT[:, a * P:(a + 1) * P], w.b2[:, :],
                                            start=True, stop=True)
                done.then_inc(down_in_psum, 1)
                pe.wait_ge(ym_ready, n + 1)
                for a in range(TILES):
                    for i in range(CI):
                        done = nc.tensor.matmul(bank[0][:, a * D:(a + 1) * D], ym[:, i, a * P:(a + 1) * P],
                                                out_projT[:, i, :], start=(i == 0), stop=(i == CI - 1))
                done.then_inc(s_in_psum, 1)

        @block.scalar
        def _(act):
            v = nc.scalar
            act.wait_ge(c.w3_loaded, c.W3_ALL)
            v.activation(negA[:, :, :], w.A_log[:, :, :], ACT.Exp).then_inc(a_exp, 1)
            norm_copy(nc, c, s, 0, bank[0], read[0])
            act.wait_ge(weights_ready, 1)

            def copy_u(m):
                act.wait_ge(u_in_psum, m + 1)
                v.activation(upad[:, :, DCONV - 1:], bank[4][:, :].rearrange("p (i t) -> p i t", i=CI), ACT.Copy)\
                    .then_inc(read[4], 1)

            copy_u(0)
            with act.Fori(0, NSEQ) as n:
                def exp_scores(h):
                    act.wait_ge(pT_in_psum, H3 * n + h + 1)
                    if h >= RP:
                        act.wait_ge(head_done, H3 * n + h - RP + 1)
                    v.activation(probs[:, h % RP, :], bank[3 + h % 2][:, :], ACT.Exp, scale=float(HD3) ** -0.5)\
                        .then_inc(probs_ready, 1)

                def log_part(j):
                    act.wait_ge(dneg_ready, 2 * n + j + 1)
                    v.activation(dneg[:, :, :], dneg[:, :, :], ACT.Exp)
                    v.drain()
                    v.activation(dneg[:, :, :], dneg[:, :, :], ACT.Ln, bias=1.0).then_inc(dlog_ready, 1)

                def decay(g, i):
                    for m in range(SG * g, SG * g + SG):
                        done = v.activation(dA[i][:, m, 1:T], delta[:, i, 1:T], ACT.Exp, scale=negA[:, i, m:m + 1])
                    done.then_inc(dA_ready, 1)

                act.wait_ge(z_in_psum, n + 1)
                zp = bank[3][:, :].rearrange("p (i t) -> p i t", i=CI)
                v.activation(z[:, :, :], zp, ACT.Copy)
                v.activation(zg[:, :, :], zp, ACT.Tanh, scale=0.5).then_inc(read[3], 1)
                act.wait_ge(conv_ready, n + 1)
                for i in range(CI):
                    done = v.activation(tmp[:, i, :], du[:, i, :], ACT.Tanh, bias=hconv_b[:, i:i + 1], scale=0.5)
                done.then_inc(conv_tanh, 1)
                act.wait_ge(qkT_in_psum, 2 * n + 1)
                for j in range(2):
                    for g in range(GR):
                        own = slice(ROWS * g, ROWS * (g + 1))
                        heads = qS[own, 2 * GR * j:2 * GR * (j + 1), :].rearrange("p (b g) t -> p b g t", g=GR)
                        done = v.activation(heads[:, :, g, :], bank[1 + j][own, :].rearrange("p (b t) -> p b t", b=2),
                                            ACT.Copy)
                    done.then_inc(read[1 + j], 1)
                act.wait_ge(xdbl_in_psum, n + 1)
                v.activation(xdbl[:, :], bank[0][0:RANK, 0:T], ACT.Copy)
                v.activation(bc[RANK:, :], bank[0][RANK:, 0:T], ACT.Copy).then_inc(bc_rounded, 1)
                log_part(0)
                log_part(1)
                act.wait_ge(maxT_in_psum, n + 1)
                v.activation(nmaxT[:, :], bank[0][0:H3, 0:T], ACT.Copy).then_inc(read[0], 1)
                act.wait_ge(delta_ready, n + 1)
                for k in range(H3):
                    exp_scores(k)
                    if k % 2:
                        decay(k // 4, k // 2 % 2)
                    if k == 9:
                        act.wait_ge(head_done, H3 * n + H3 // 2)
                        v.activation(oS[:, 0:2, :], bank[7][:, :].rearrange("p (b t) -> p b t", b=2), ACT.Copy)\
                            .then_inc(read[7], 1)
                act.wait_ge(head_done, H3 * n + H3)
                v.activation(oS[:, 2:4, :], bank[7][:, :].rearrange("p (b t) -> p b t", b=2), ACT.Copy)\
                    .then_inc(read[7], 1)
                act.wait_ge(yT_in_psum, n + 1)
                v.activation(yT[:, :], bank[0][:, 0:T], ACT.Copy).then_inc(read[0], 1)
                act.wait_ge(x1T_in_psum, n + 1)
                v.activation(x1T[:, :], bank[0][:, 0:T], ACT.Copy).then_inc(read[0], 1)
                route_exp(nc, r, n)

                def gelu(e):
                    if e >= 2:
                        act.wait_ge(down_in_psum, 9 * n + e - 1)
                    for b in range(2):
                        act.wait_ge(hidden_in_psum, 2 * E3 * n + 2 * e + b + 1)
                        for i in range(2):
                            k = 2 * b + i
                            done = v.activation(hid[:, e % 2, k, :], bank[1 + b][:, i * T:(i + 1) * T], ACT.Gelu,
                                                bias=w.b1[:, e, k:k + 1])
                        done.then_inc(read[1 + b], 1)

                for e in range(E3):
                    gelu(e)
                    if e == 3:
                        norm_copy(nc, c, s, n + 1, bank[0], read[0])
                    if e == 6:
                        copy_u(n + 1)
                        act.wait_ge(combT_in_psum, n + 1)
                        v.activation(combT[:, :], bank[0][0:E3, 0:T], ACT.Copy).then_inc(read[0], 1)
                act.wait_ge(gate_ready, n + 1)
                v.activation(th_z[:, :, :], rows[:, :, :], ACT.Tanh, scale=0.5).then_inc(th_z_ready, 1)

        @block.gpsimd
        def _(pool):
            def inner_power(count):
                pool.wait_ge(var_ready, count)
                nc.gpsimd.tensor_tensor(rstd[:, :], var_eps[:, :], c.minus_half[:, 0:TILES], ALU.pow)\
                    .then_inc(rstd_ready, 1)

            norm_power(nc, c, s, 0)
            with pool.Fori(0, NSEQ) as n:
                def add_pair(p):
                    pool.wait_ge(cstate_ready, PAIRS * n + p + 1)
                    for i in range(CI):
                        done = nc.gpsimd.tensor_tensor(st[i][:, 0:2, :], st[i][:, 0:2, :],
                                                       st[i][:, 2 * p:2 * p + 2, :], ALU.add)
                    if p == PAIRS - 1:
                        done.then_inc(sum_ready, 1)
                    else:
                        nc.gpsimd.drain()

                for p in range(1, 4):
                    add_pair(p)
                inner_power(2 * n + 1)
                add_pair(4)
                add_pair(5)
                norm_power(nc, c, s, n + 1)
                add_pair(6)
                add_pair(7)
                inner_power(2 * n + 2)

        @block.vector
        def _(dve):
            v = nc.vector
            for i in range(CI):
                v.memset(dA[i][:, :, 0:1], 0.0)
            v.memset(upad[:, :, 0:DCONV - 1], 0.0)
            v.memset(vaug[:, :, :, :], 0.0)
            v.drain()
            zeros = vaug[:, :, :, :].rearrange("p a h w -> p (a h w)")
            for j in range(NBLK):
                v.tensor_copy(qS[:, GR * j:GR * (j + 1), :].rearrange("p h t -> p (h t)"), zeros)
            v.tensor_copy(bc[:, :], zeros[:, 0:T])
            v.drain()
            v.memset(vaug[:, :, :, HD3:HD3 + 1], 1.0)
            dve.wait_ge(c.w3_loaded, c.W3_ALL)
            v.tensor_scalar(hconv_b[:, :], w.conv_b[:, :], 0.5, None, ALU.mult)
            v.tensor_copy(identR[:, :], c.ident[:, :])
            v.tensor_tensor(pick[:, :], c.ident[:, RANK:XD], c.ident[:, XD:], ALU.add)
            dve.wait_ge(a_exp, 1)
            v.tensor_scalar(negA[:, :, :], negA[:, :, :], -1.0, None, ALU.mult)
            dve.wait_ge(weights_turned, 1)
            v.tensor_copy(in_projT[:, :, :], bank[1][:, :].rearrange("p (i d) -> p i d", d=P))
            turned = bank[2][:, 0:CI * XD].rearrange("p (i d) -> p i d", d=XD)
            v.tensor_copy(x_projT[:, :, 0:XD], turned)
            v.tensor_copy(x_projT[:, :, XD:], turned[:, :, RANK:])
            v.tensor_copy(dt_projT[:, :, :], bank[3][0:RANK, 0:DI].rearrange("p (i d) -> p i d", d=P))
            v.tensor_copy(out_projT[:, :, :], bank[4][:, 0:CI * D].rearrange("p (i d) -> p i d", d=D))
            v.drain().then_inc(weights_ready, 2)
            norm_stats(nc, c, s, 0)
            norm_apply(nc, c, s, 0, True)
            bq = w.bqkv[:, 0:2, :].rearrange("p i d -> p (i d)")
            bv = w.bqkv[:, 2, :].rearrange("p (h v) -> p h v", v=HD3)

            def take_qkv(m, a):
                dve.wait_ge(qkv_in_psum, TILES * m + a + 1)
                v.tensor_tensor(qkv[:, a, :], bank[0][:, 0:2 * D], bq, ALU.add)
                v.tensor_tensor(vaug[:, a, :, 0:HD3], bank[0][:, 2 * D:3 * D].rearrange("p (h v) -> p h v", v=HD3),
                                bv, ALU.add).then_inc(read[0], 1)
                v.drain()

            def rotate(a):
                for i in range(2):
                    part = qkv[:, a, i * D:(i + 1) * D].rearrange("p (h o k) -> p h o k", h=H3, o=2)
                    lo, hi = part[:, :, 0, :], part[:, :, 1, :]
                    cos = c.cos1[:, a, i * D // 2:(i + 1) * D // 2].rearrange("p (h k) -> p h k", h=H3)
                    sin = c.sin1[:, a, i * D // 2:(i + 1) * D // 2].rearrange("p (h k) -> p h k", h=H3)
                    v.tensor_tensor(t1[:, i], lo, cos, ALU.mult)
                    v.tensor_tensor(t2[:, i], hi, sin, ALU.mult)
                    v.tensor_tensor(t3[:, i], lo, sin, ALU.mult)
                    v.tensor_tensor(t4[:, i], hi, cos, ALU.mult)
                v.drain()
                v.tensor_tensor(rot[:, a, :, :, 0, :], t1[:, :, :, :], t2[:, :, :, :], ALU.subtract)
                v.tensor_tensor(rot[:, a, :, :, 1, :], t3[:, :, :, :], t4[:, :, :, :], ALU.add)
                v.drain()
                whole, los, his = [], [], []
                for i in range(2):
                    whole.append(rot[:, a, i, :, :, :].rearrange("p h o k -> p h (o k)")
                                 .unsqueeze(2).to_broadcast([P, H3, 2, HD3]))
                    split = parts[:, a, i, :].rearrange("p (h u v k) -> p h u v k", h=H3, u=2, v=2)
                    his.append(split[:, :, 0, :, :] if i == 0 else split[:, :, :, 0, :])
                    los.append(split[:, :, 1, :, :] if i == 0 else split[:, :, :, 1, :])
                    v.tensor_copy(his[i], whole[i])
                v.drain()
                for i in range(2):
                    v.tensor_tensor(los[i], whole[i], his[i], ALU.subtract)
                if a == TILES - 1:
                    v.drain().then_inc(rot_ready, 1)
                else:
                    v.drain()

            def conv(m):
                dve.wait_ge(read[4], PER34 * m + 2)
                for k in range(DCONV):
                    for i in range(CI):
                        src = upad[:, i, k:k + T]
                        if k == 0:
                            v.tensor_scalar(du[:, i, :], src, w.conv[:, i, 0:1], None, ALU.mult)
                        else:
                            v.scalar_tensor_tensor(out=du[:, i, :], in0=src, scalar=w.conv[:, i, k:k + 1],
                                                   in1=du[:, i, :], op0=ALU.mult, op1=ALU.add)
                    if k < DCONV - 1:
                        v.drain()
                v.drain().then_inc(conv_ready, 1)

            for a in range(TILES):
                take_qkv(0, a)
                rotate(a)
            conv(0)
            with dve.Fori(0, NSEQ) as n:
                def head_max(h):
                    dve.wait_ge(scores_in_psum, H3 * n + h + 1)
                    v.tensor_reduce(nmax[:, :, h], bank[1 + h % 2][:, :].rearrange("p (a t) -> p a t", a=TILES),
                                    AX, ALU.max, negate=True).then_inc(read[1 + h % 2], 1)

                def softplus_arg(src, j):
                    for i in range(CI):
                        done = v.tensor_scalar(dv[:, i, :], src[:, i, :], w.dt_b[:, i:i + 1], None, ALU.add)
                    if j == 0:
                        done.then_inc(read[0], 1)
                    v.drain()
                    v.scalar_tensor_tensor(out=dneg[:, :, :], in0=dv[:, :, :], scalar=-1.0, in1=dv[:, :, :],
                                           op0=ALU.mult, op1=ALU.min).then_inc(dneg_ready, 1)

                def softplus_sum(j):
                    dve.wait_ge(dlog_ready, 2 * n + j + 1)
                    v.scalar_tensor_tensor(out=delta[:, :, :], in0=dv[:, :, :], scalar=0.0, in1=dneg[:, :, :],
                                           op0=ALU.max, op1=ALU.add)
                    v.drain()

                def silu_from_tanh(out, x, t):
                    v.scalar_tensor_tensor(out=t, in0=t, scalar=1.0, in1=x, op0=ALU.add, op1=ALU.mult)
                    v.drain()
                    v.tensor_scalar(out, t, 0.5, None, ALU.mult)

                def state_input(p):
                    dve.wait_ge(bc_in_psum, 2 * PAIRS * n + p + 1)
                    b = bank[5 + p % 2][:, :].rearrange("p (m t) -> p m t", m=2)
                    for i in range(CI):
                        done = v.tensor_tensor(st[i][:, 2 * p:2 * p + 2, :], b,
                                               du[:, i, :].unsqueeze(1).to_broadcast([P, 2, T]), ALU.mult)
                    done.then_inc(read[5 + p % 2], 1)

                def scan(g, i):
                    dve.wait_ge(dA_ready, 2 * (NS // SG) * n + 2 * g + i + 1)
                    group = st[i][:, SG * g:SG * (g + 1), :].rearrange("p m t -> p (m t)")
                    v.tensor_tensor_scan(group, dA[i][:, SG * g:SG * (g + 1), :].rearrange("p m t -> p (m t)"),
                                         group, 0.0, ALU.mult, ALU.add)

                def times_c(p):
                    dve.wait_ge(bc_in_psum, 2 * PAIRS * n + PAIRS + p + 1)
                    b = bank[5 + p % 2][:, :].rearrange("p (m t) -> p m t", m=2)
                    for i in range(CI):
                        done = v.tensor_tensor(st[i][:, 2 * p:2 * p + 2, :], st[i][:, 2 * p:2 * p + 2, :], b, ALU.mult)
                    done.then_inc(read[5 + p % 2], 1)
                    v.drain().then_inc(cstate_ready, 1)

                def inner_stats():
                    for a in range(TILES):
                        v.bn_stats(stats[:, a, :], rows[:, a, :])
                    v.drain()
                    for a in range(TILES):
                        v.bn_aggr(meanvar[:, a, :], stats[:, a, :])
                    v.drain()
                    v.tensor_scalar(var_eps[:, :], meanvar[:, :, 1], LN_EPS, None, ALU.add).then_inc(var_ready, 1)

                def inner_apply(out, weight, bias, count):
                    dve.wait_ge(rstd_ready, count)
                    for a in range(TILES):
                        v.tensor_scalar(rows[:, a, :], rows[:, a, :], meanvar[:, a, 0:1], rstd[:, a:a + 1],
                                        ALU.subtract, ALU.mult)
                    v.drain()
                    wide = [x[:, :].unsqueeze(1).to_broadcast([P, TILES, D]) for x in (weight, bias)]
                    v.tensor_tensor(rows[:, :, :], rows[:, :, :], wide[0], ALU.mult)
                    v.drain()
                    v.tensor_tensor(out, rows[:, :, :], wide[1], ALU.add)

                dve.wait_ge(conv_tanh, n + 1)
                for i in range(CI):
                    v.tensor_scalar(xs[:, i, :], du[:, i, :], w.conv_b[:, i:i + 1], None, ALU.add)
                v.drain()
                silu_from_tanh(xs[:, :, :], xs[:, :, :], tmp[:, :, :])
                v.drain().then_inc(xs_ready, 1)
                dve.wait_ge(qkT_in_psum, 2 * n + 2)
                for j in range(2):
                    v.tensor_copy(kS[:, 2 * j:2 * j + 2, :].rearrange("p b t -> p (b t)"), bank[3 + j][:, :])\
                        .then_inc(read[3 + j], 1)
                for k in range(H3):
                    head_max(k)
                    if k == 3:
                        dve.wait_ge(bc_rounded, n + 1)
                        v.tensor_tensor(bc[XD:, :], bank[0][XD:, 0:T], bc[XD:, :], ALU.subtract).then_inc(read[0], 1)
                    if k == 5:
                        dve.wait_ge(dt_in_psum, n + 1)
                        softplus_arg(bank[0][:, :].rearrange("p (i t) -> p i t", i=CI), 0)
                    if k == 9:
                        softplus_sum(0)
                        softplus_arg(delta, 1)
                    if k == 13:
                        softplus_sum(1)
                        v.drain().then_inc(delta_ready, 1)
                v.drain().then_inc(max_ready, 1)
                v.tensor_tensor(du[:, :, :], delta[:, :, :], xs[:, :, :], ALU.mult)
                v.drain()
                for p in range(PAIRS):
                    state_input(p)
                v.drain()
                silu_from_tanh(zg[:, :, :], z[:, :, :], zg[:, :, :])
                for g in range(2):
                    scan(g, 0)
                    scan(g, 1)
                    v.drain()
                    times_c(2 * g)
                    times_c(2 * g + 1)
                dve.wait_ge(o_turned, n + 1)
                for a in range(TILES):
                    heads = bank[3 + a][:, :].rearrange("p (h w) -> p h w", w=ROWS)
                    v.reciprocal(recip[:, a, :], heads[:, :, HD3])
                v.drain()
                for a in range(TILES):
                    heads = bank[3 + a][:, :].rearrange("p (h w) -> p h w", w=ROWS)
                    v.tensor_tensor(y[:, a, :].rearrange("p (h v) -> p h v", v=HD3), heads[:, :, 0:HD3],
                                    bcast(recip[:, a, :], HD3), ALU.mult).then_inc(read[3 + a], 1)
                v.drain().then_inc(y_ready, 1)
                scan(2, 0)
                dve.wait_ge(o_in_psum, n + 1)
                v.tensor_tensor(rows[:, :, :], bank[0][:, 0:TILES * D].rearrange("p (a d) -> p a d", d=D),
                                w.bo[:, :].unsqueeze(1).to_broadcast([P, TILES, D]), ALU.add).then_inc(read[0], 1)
                v.drain()
                v.tensor_tensor(rows[:, :, :], rows[:, :, :], c.xn[:, :, :], ALU.add)
                v.drain()
                inner_stats()
                scan(2, 1)
                inner_apply(x1[:, :, :], w.g1, w.be1, 2 * n + 1)
                v.drain().then_inc(x1_ready, 1)
                times_c(4)
                times_c(5)
                norm_stats(nc, c, s, n + 1)
                dve.wait_ge(logits_in_psum, n + 1)
                route_shift(nc, r, bank[0][:, 0:TILES * E3].rearrange("p (a e) -> p a e", e=E3), read[0],
                            w.bg[:, :].unsqueeze(1).to_broadcast([P, TILES, E3]))
                route_best(nc, r, n)
                v.tensor_tensor(psum2[:, :], r.best[:, :, 0], r.best[:, :, 1], ALU.add)
                v.drain()
                v.reciprocal(psum2[:, :], psum2[:, :])
                v.drain()
                v.tensor_tensor(first[:, :], r.best[:, :, 0], psum2[:, :], ALU.mult)
                v.tensor_tensor(second[:, :], r.best[:, :, 1], psum2[:, :], ALU.mult)
                v.drain()
                for a in range(TILES):
                    v.tensor_scalar(comb[:, a, :], c.iota8[:, :], r.place[:, a, 0:1], first[:, a:a + 1],
                                    ALU.is_equal, ALU.mult)
                    v.tensor_scalar(comb2[:, a, :], c.iota8[:, :], r.place[:, a, 1:2], second[:, a:a + 1],
                                    ALU.is_equal, ALU.mult)
                v.drain()
                v.tensor_tensor(comb[:, :, :], comb[:, :, :], comb2[:, :, :], ALU.add)
                v.drain().then_inc(comb_ready, 1)
                for e in range(E3):
                    if e < 2:
                        scan(3, e)
                    if e == 1:
                        norm_apply(nc, c, s, n + 1, False)
                        v.drain()
                    if e in (2, 3):
                        times_c(e + 4)
                    dve.wait_ge(down_in_psum, 9 * n + e + 1)
                    for a in range(TILES):
                        part = bank[7][:, a * D:(a + 1) * D]
                        if e == 0:
                            done = v.tensor_scalar(acc[:, a, :], part, comb[:, a, 0:1], None, ALU.mult)
                        else:
                            done = v.scalar_tensor_tensor(out=acc[:, a, :], in0=part, scalar=comb[:, a, e:e + 1],
                                                          in1=acc[:, a, :], op0=ALU.mult, op1=ALU.add)
                    done.then_inc(read[7], 1)
                    if e in (4, 5):
                        take_qkv(n + 1, e - 4)
                        rotate(e - 4)
                    if e == 6:
                        conv(n + 1)
                dve.wait_ge(sum_ready, n + 1)
                for i in range(CI):
                    v.scalar_tensor_tensor(out=ym[:, i, :], in0=xs[:, i, :], scalar=w.skip[:, i:i + 1],
                                           in1=st[i][:, 0, :], op0=ALU.mult, op1=ALU.add)
                v.drain()
                for i in range(CI):
                    v.tensor_tensor(ym[:, i, :], ym[:, i, :], st[i][:, 1, :], ALU.add)
                v.drain()
                v.tensor_tensor(ym[:, :, :], ym[:, :, :], zg[:, :, :], ALU.mult)
                v.drain().then_inc(ym_ready, 1)
                dve.wait_ge(down_in_psum, 9 * n + 9)
                v.tensor_tensor(rows[:, :, :], bank[7][:, 0:TILES * D].rearrange("p (a d) -> p a d", d=D),
                                acc[:, :, :], ALU.add).then_inc(read[7], 1)
                v.drain()
                v.tensor_tensor(rows[:, :, :], rows[:, :, :], x1[:, :, :], ALU.add)
                v.drain()
                inner_stats()
                dve.wait_ge(s_in_psum, n + 1)
                v.tensor_copy(s_out[:, :, :], bank[0][:, 0:TILES * D].rearrange("p (a d) -> p a d", d=D))\
                    .then_inc(read[0], 1)
                inner_apply(rows[:, :, :], w.g2, w.be2, 2 * n + 2)
                v.drain().then_inc(gate_ready, 1)
                dve.wait_ge(th_z_ready, n + 1)
                close_layer(nc, c, n, s_out[:, :, :], rows[:, :, :], th_z[:, :, :], u[:, :, :])


def store(nc, c, out):
    with ExitStack() as ctx:
        stored = ctx.enter_context(nc.semaphore("stored"))
        block = ctx.enter_context(nc.Block())

        @block.sync
        def _(sp):
            rows = out.rearrange("b (a p) d -> p (b a) d", p=P)
            sp.dma_start(rows, c.x[:, 0:TILES * NSEQ, :]).then_inc(stored, 16)
            sp.wait_ge(stored, 16)


def program(nc, A, out):
    with ExitStack() as ctx:
        c = Core()
        with ExitStack() as ctx01:
            setup(nc, ctx, ctx01, A, c)
            run_layer(nc, c, layer0)
            if LAYERS >= 2:
                run_layer(nc, c, layer1)
        layer3_weights(nc, ctx, A, c)
        if LAYERS >= 3:
            run_layer(nc, c, layer2)
        if LAYERS >= 4:
            run_layer(nc, c, layer3)
        store(nc, c, out)


def shape_constants():
    import numpy as np

    f = np.float32
    i = np.arange(P)
    tri = np.where(i[:, None] >= i[None, :], f(0), f(-1e30)).astype(f)
    k = {"const_iota8": np.tile(np.arange(8, dtype=f), (P, 1)),
         "const_causal": np.concatenate([tri, np.zeros((P, P), f), tri], 1),
         "const_row_mask": ((i[:, None] // HD1) % GR == np.arange(GR)[None, :]).astype(f)}
    pairs = np.arange(1, HD1 // 2 + 1, dtype=f)
    theta = f(1) / f(10000) ** (f(2) * (pairs - f(1)) / f(HD1))
    angle = (np.arange(T, dtype=f)[:, None] * theta[None, :]).astype(f)
    same = np.zeros((P, 3, P), f)
    for d in range(2):
        same[:, d, :] = (i[:, None] // 2 == i[None, :] // 2) & (i[None, :] % 2 == d)
    same[:, 2, :] = i[:, None] // 2 == i[None, :] // 2
    k["const_same_head"] = same
    k["const_until"] = (i[:, None] <= i[None, :]).astype(f)
    k["const_cos1"] = np.tile(np.cos(angle).astype(f), (1, 2 * H1))
    k["const_sin1"] = np.tile(np.sin(angle).astype(f), (1, 2 * H1))
    return k


def kernel(**inputs):
    import numpy as _np
    import concourse.bacc as _bacc
    from concourse.bass_utils import run_bass_kernel_spmd as _run

    nc = _bacc.Bacc("TRN2", target_bir_lowering=False, num_devices=1)
    arrays, aps = {}, {}
    for name, value in {**inputs, **shape_constants()}.items():
        a = _np.ascontiguousarray(value)
        arrays[f"in_{name}_dram"] = a
        aps[name] = nc.dram_tensor(f"in_{name}_dram", a.shape, F32, kind="ExternalInput").ap()
    out = nc.dram_tensor("out_dram", (NSEQ, T, D), F32, kind="ExternalOutput").ap()
    program(nc, aps, out)
    r = _run(nc, [arrays], core_ids=[0])
    return r.results[0]["out_dram"]
```
